# Optimizing a Trainium2 kernel written in Bass

```python
import numpy as np
import jax
import jax.numpy as jnp

def _softmax(x, axis=-1):
    return jax.nn.softmax(x, axis=axis)

def _gelu(x):
    return jax.nn.gelu(x, approximate=True)

def _silu(x):
    return jax.nn.silu(x)

def _sigmoid(x):
    return jax.nn.sigmoid(x)

def _layernorm(x, axis=-1, eps=1e-05):
    m = jnp.mean(x, axis=axis, keepdims=True)
    v = jnp.var(x, axis=axis, keepdims=True)
    return (x - m) / jnp.sqrt(v + eps)

def _scatter_add(tgt, idx, src, axis=0):
    return tgt.at[idx].add(src)

def _segment_sum(src, seg, n):
    return jax.ops.segment_sum(src, seg, n)
kernel_name = 'mk_adaln_ffn_d1_seqx_r4_737d5c'

def setup_inputs(seed: int=0):
    np.random.seed(seed)
    _w = jnp.asarray

    def _rec_inputs():
        import jax
        import jax.numpy as jnp
        _rk = jax.random.key(seed)
        x = -0.0003929 + 0.9999 * jax.random.normal(jax.random.fold_in(_rk, 1), (8, 256, 512), jnp.float32)
        _lenS = 256 - jax.random.randint(jax.random.fold_in(_rk, 7), (8,), 0, max(1, 256 // 4) + 1, jnp.int32)
        _lenS2 = 256 - jax.random.randint(jax.random.fold_in(_rk, 8), (8,), 0, max(1, 256 // 4) + 1, jnp.int32)
        cond_2048 = 0.00782532 + 1.00527 * jax.random.normal(jax.random.fold_in(_rk, 11), (8, 512), jnp.float32)
        return (x, cond_2048)
    x, cond_2048 = _rec_inputs()

    def _L0_cond_setup():
        import jax, jax.numpy as jnp
        import numpy as np
        HEADS = 16
        EPS = 1e-06

        def _rms_norm(x, g):
            xf = x.astype(jnp.float32)
            y = xf * jax.lax.rsqrt(jnp.mean(xf * xf, axis=-1, keepdims=True) + EPS)
            return y.astype(x.dtype) * g
        key = jax.random.key(seed)
        ks = jax.random.split(key, 6)
        b, n, dim, emb_dim = (4, 512, 512, 512)
        d_head = dim // HEADS
        return {'x': jax.random.normal(ks[0], (b, n, dim), jnp.float32), 'emb': jax.random.normal(ks[1], (b, 1, emb_dim), jnp.float32), 'W_emb': jax.random.normal(ks[2], (emb_dim, 2 * dim), jnp.float32) * emb_dim ** (-0.5), 'b_emb': jnp.zeros((2 * dim,), jnp.float32), 'g_norm': jnp.ones((dim,), jnp.float32), 'W_qkv': jax.random.normal(ks[3], (dim, 3 * dim), jnp.float32) * dim ** (-0.5), 'g_q': jnp.ones((d_head,), jnp.float32), 'g_k': jnp.ones((d_head,), jnp.float32), 'W_out': jax.random.normal(ks[4], (dim, dim), jnp.float32) * dim ** (-0.5)}
    _L0_cond_all = _L0_cond_setup()
    _L0_cond_in = {k: v for k, v in _L0_cond_all.items() if k in ('W_emb', 'b_emb', 'g_norm', 'W_qkv', 'g_q', 'g_k', 'W_out')}
    del _L0_cond_all

    def _L0_ffn_setup():
        import jax, jax.numpy as jnp
        import numpy as np
        COST_LAMBDA = 1e-07
        HID = [256, 512, 768, 1024, 256, 512, 768, 1024]
        TOP_K = 2

        def _gelu(v):
            return jax.nn.gelu(v, approximate=False)

        def _forward(x, down_w, down_b, up_w, up_b, router_w, router_b, shared_w1, shared_b1, shared_w2, shared_b2, core_w, core_b, expert_params):
            E = len(expert_params)
            h = x @ down_w + down_b
            cost = jnp.array([w1.shape[0] * w1.shape[1] + w2.shape[0] * w2.shape[1] for w1, _, w2, _ in expert_params], jnp.float32)
            logits = x @ router_w + router_b - COST_LAMBDA * cost
            probs = jax.nn.softmax(logits, axis=-1)
            topv, topi = jax.lax.top_k(probs, TOP_K)
            gate = jax.nn.softmax(topv, axis=-1)
            out = jnp.zeros_like(h)
            for k in range(TOP_K):
                mask = jax.nn.one_hot(topi[..., k], E, dtype=h.dtype)
                acc = jnp.zeros_like(h)
                for e, (w1, b1, w2, b2) in enumerate(expert_params):
                    hm = h * mask[..., e:e + 1]
                    acc = acc + (_gelu(_gelu(hm) @ w1 + b1) @ w2 + b2)
                out = out + acc * gate[..., k:k + 1]
            out = out + 0.1 * (_gelu(_gelu(h) @ shared_w1 + shared_b1) @ shared_w2 + shared_b2)
            out = out @ up_w + up_b
            out = out + (_gelu(x) @ core_w + core_b)
            return out
        key = jax.random.key(seed)
        ks = iter(jax.random.split(key, 80))

        def W(shape):
            return jax.random.normal(next(ks), shape, jnp.float32) * 0.02
        B, T, D, L = (4, 512, 512, 256)
        inp = {'x': jax.random.normal(next(ks), (B, T, D), jnp.float32)}
        inp['down_w'] = W((D, L))
        inp['down_b'] = jnp.zeros((L,), jnp.float32)
        inp['up_w'] = W((L, D))
        inp['up_b'] = jnp.zeros((D,), jnp.float32)
        inp['router_w'] = W((D, len(HID)))
        inp['router_b'] = jnp.zeros((len(HID),), jnp.float32)
        inp['shared_w1'] = W((L, L))
        inp['shared_b1'] = jnp.zeros((L,), jnp.float32)
        inp['shared_w2'] = W((L, L))
        inp['shared_b2'] = jnp.zeros((L,), jnp.float32)
        inp['core_w'] = W((D, D))
        inp['core_b'] = jnp.zeros((D,), jnp.float32)
        for e, h in enumerate(HID):
            inp[f'e{e}_w1'] = W((L, h))
            inp[f'e{e}_b1'] = jnp.zeros((h,), jnp.float32)
            inp[f'e{e}_w2'] = W((h, L))
            inp[f'e{e}_b2'] = jnp.zeros((L,), jnp.float32)
        return inp
    _L0_ffn_all = _L0_ffn_setup()
    _L0_ffn_in = {k: v for k, v in _L0_ffn_all.items() if k in ('down_w', 'down_b', 'up_w', 'up_b', 'router_w', 'router_b', 'shared_w1', 'shared_b1', 'shared_w2', 'shared_b2', 'core_w', 'core_b', 'e0_w1', 'e0_b1', 'e0_w2', 'e0_b2', 'e1_w1', 'e1_b1', 'e1_w2', 'e1_b2', 'e2_w1', 'e2_b1', 'e2_w2', 'e2_b2', 'e3_w1', 'e3_b1', 'e3_w2', 'e3_b2', 'e4_w1', 'e4_b1', 'e4_w2', 'e4_b2', 'e5_w1', 'e5_b1', 'e5_w2', 'e5_b2', 'e6_w1', 'e6_b1', 'e6_w2', 'e6_b2', 'e7_w1', 'e7_b1', 'e7_w2', 'e7_b2')}
    del _L0_ffn_all
    return {'x': x, 'cond_2048': cond_2048, 'L0_cond_W_emb': _L0_cond_in['W_emb'], 'L0_cond_b_emb': _L0_cond_in['b_emb'], 'L0_cond_g_norm': _L0_cond_in['g_norm'], 'L0_cond_W_qkv': _L0_cond_in['W_qkv'], 'L0_cond_g_q': _L0_cond_in['g_q'], 'L0_cond_g_k': _L0_cond_in['g_k'], 'L0_cond_W_out': _L0_cond_in['W_out'], 'L0_ffn_down_w': _L0_ffn_in['down_w'], 'L0_ffn_down_b': _L0_ffn_in['down_b'], 'L0_ffn_up_w': _L0_ffn_in['up_w'], 'L0_ffn_up_b': _L0_ffn_in['up_b'], 'L0_ffn_router_w': _L0_ffn_in['router_w'], 'L0_ffn_router_b': _L0_ffn_in['router_b'], 'L0_ffn_shared_w1': _L0_ffn_in['shared_w1'], 'L0_ffn_shared_b1': _L0_ffn_in['shared_b1'], 'L0_ffn_shared_w2': _L0_ffn_in['shared_w2'], 'L0_ffn_shared_b2': _L0_ffn_in['shared_b2'], 'L0_ffn_core_w': _L0_ffn_in['core_w'], 'L0_ffn_core_b': _L0_ffn_in['core_b'], 'L0_ffn_e0_w1': _L0_ffn_in['e0_w1'], 'L0_ffn_e0_b1': _L0_ffn_in['e0_b1'], 'L0_ffn_e0_w2': _L0_ffn_in['e0_w2'], 'L0_ffn_e0_b2': _L0_ffn_in['e0_b2'], 'L0_ffn_e1_w1': _L0_ffn_in['e1_w1'], 'L0_ffn_e1_b1': _L0_ffn_in['e1_b1'], 'L0_ffn_e1_w2': _L0_ffn_in['e1_w2'], 'L0_ffn_e1_b2': _L0_ffn_in['e1_b2'], 'L0_ffn_e2_w1': _L0_ffn_in['e2_w1'], 'L0_ffn_e2_b1': _L0_ffn_in['e2_b1'], 'L0_ffn_e2_w2': _L0_ffn_in['e2_w2'], 'L0_ffn_e2_b2': _L0_ffn_in['e2_b2'], 'L0_ffn_e3_w1': _L0_ffn_in['e3_w1'], 'L0_ffn_e3_b1': _L0_ffn_in['e3_b1'], 'L0_ffn_e3_w2': _L0_ffn_in['e3_w2'], 'L0_ffn_e3_b2': _L0_ffn_in['e3_b2'], 'L0_ffn_e4_w1': _L0_ffn_in['e4_w1'], 'L0_ffn_e4_b1': _L0_ffn_in['e4_b1'], 'L0_ffn_e4_w2': _L0_ffn_in['e4_w2'], 'L0_ffn_e4_b2': _L0_ffn_in['e4_b2'], 'L0_ffn_e5_w1': _L0_ffn_in['e5_w1'], 'L0_ffn_e5_b1': _L0_ffn_in['e5_b1'], 'L0_ffn_e5_w2': _L0_ffn_in['e5_w2'], 'L0_ffn_e5_b2': _L0_ffn_in['e5_b2'], 'L0_ffn_e6_w1': _L0_ffn_in['e6_w1'], 'L0_ffn_e6_b1': _L0_ffn_in['e6_b1'], 'L0_ffn_e6_w2': _L0_ffn_in['e6_w2'], 'L0_ffn_e6_b2': _L0_ffn_in['e6_b2'], 'L0_ffn_e7_w1': _L0_ffn_in['e7_w1'], 'L0_ffn_e7_b1': _L0_ffn_in['e7_b1'], 'L0_ffn_e7_w2': _L0_ffn_in['e7_w2'], 'L0_ffn_e7_b2': _L0_ffn_in['e7_b2']}

def reference(x, cond_2048, L0_cond_W_emb, L0_cond_b_emb, L0_cond_g_norm, L0_cond_W_qkv, L0_cond_g_q, L0_cond_g_k, L0_cond_W_out, L0_ffn_down_w, L0_ffn_down_b, L0_ffn_up_w, L0_ffn_up_b, L0_ffn_router_w, L0_ffn_router_b, L0_ffn_shared_w1, L0_ffn_shared_b1, L0_ffn_shared_w2, L0_ffn_shared_b2, L0_ffn_core_w, L0_ffn_core_b, L0_ffn_e0_w1, L0_ffn_e0_b1, L0_ffn_e0_w2, L0_ffn_e0_b2, L0_ffn_e1_w1, L0_ffn_e1_b1, L0_ffn_e1_w2, L0_ffn_e1_b2, L0_ffn_e2_w1, L0_ffn_e2_b1, L0_ffn_e2_w2, L0_ffn_e2_b2, L0_ffn_e3_w1, L0_ffn_e3_b1, L0_ffn_e3_w2, L0_ffn_e3_b2, L0_ffn_e4_w1, L0_ffn_e4_b1, L0_ffn_e4_w2, L0_ffn_e4_b2, L0_ffn_e5_w1, L0_ffn_e5_b1, L0_ffn_e5_w2, L0_ffn_e5_b2, L0_ffn_e6_w1, L0_ffn_e6_b1, L0_ffn_e6_w2, L0_ffn_e6_b2, L0_ffn_e7_w1, L0_ffn_e7_b1, L0_ffn_e7_w2, L0_ffn_e7_b2):
    import jax
    import jax.numpy as jnp

    def _L0_cond_ref(x, emb, W_emb, b_emb, g_norm, W_qkv, g_q, g_k, W_out):
        import jax, jax.numpy as jnp
        import numpy as np
        HEADS = 16
        EPS = 1e-06

        def _rms_norm(x, g):
            xf = x.astype(jnp.float32)
            y = xf * jax.lax.rsqrt(jnp.mean(xf * xf, axis=-1, keepdims=True) + EPS)
            return y.astype(x.dtype) * g
        b, n, dim = x.shape
        h = HEADS
        d = dim // h
        scale_shift = emb @ W_emb + b_emb
        scale, shift = jnp.split(scale_shift, 2, axis=-1)
        xn = _rms_norm(x, g_norm) * (1.0 + scale) + shift
        qkv = xn @ W_qkv
        qkv = qkv.reshape(b, n, 3, h, d)
        q, k, v = jnp.moveaxis(qkv, 2, 0)
        q = jnp.swapaxes(q, 1, 2)
        k = jnp.swapaxes(k, 1, 2)
        v = jnp.swapaxes(v, 1, 2)
        q = _rms_norm(q, g_q)
        k = _rms_norm(k, g_k)
        logits = jnp.einsum('bhqd,bhkd->bhqk', q, k) * d ** (-0.5)
        attn = jax.nn.softmax(logits, axis=-1)
        o = jnp.einsum('bhqk,bhkd->bhqd', attn, v)
        o = jnp.swapaxes(o, 1, 2).reshape(b, n, dim)
        return o + o @ W_out

    def _L0_ffn_ref(x, down_w, down_b, up_w, up_b, router_w, router_b, shared_w1, shared_b1, shared_w2, shared_b2, core_w, core_b, e0_w1, e0_b1, e0_w2, e0_b2, e1_w1, e1_b1, e1_w2, e1_b2, e2_w1, e2_b1, e2_w2, e2_b2, e3_w1, e3_b1, e3_w2, e3_b2, e4_w1, e4_b1, e4_w2, e4_b2, e5_w1, e5_b1, e5_w2, e5_b2, e6_w1, e6_b1, e6_w2, e6_b2, e7_w1, e7_b1, e7_w2, e7_b2):
        import jax, jax.numpy as jnp
        import numpy as np
        COST_LAMBDA = 1e-07
        HID = [256, 512, 768, 1024, 256, 512, 768, 1024]
        TOP_K = 2

        def _gelu(v):
            return jax.nn.gelu(v, approximate=False)

        def _forward(x, down_w, down_b, up_w, up_b, router_w, router_b, shared_w1, shared_b1, shared_w2, shared_b2, core_w, core_b, expert_params):
            E = len(expert_params)
            h = x @ down_w + down_b
            cost = jnp.array([w1.shape[0] * w1.shape[1] + w2.shape[0] * w2.shape[1] for w1, _, w2, _ in expert_params], jnp.float32)
            logits = x @ router_w + router_b - COST_LAMBDA * cost
            probs = jax.nn.softmax(logits, axis=-1)
            topv, topi = jax.lax.top_k(probs, TOP_K)
            gate = jax.nn.softmax(topv, axis=-1)
            out = jnp.zeros_like(h)
            for k in range(TOP_K):
                mask = jax.nn.one_hot(topi[..., k], E, dtype=h.dtype)
                acc = jnp.zeros_like(h)
                for e, (w1, b1, w2, b2) in enumerate(expert_params):
                    hm = h * mask[..., e:e + 1]
                    acc = acc + (_gelu(_gelu(hm) @ w1 + b1) @ w2 + b2)
                out = out + acc * gate[..., k:k + 1]
            out = out + 0.1 * (_gelu(_gelu(h) @ shared_w1 + shared_b1) @ shared_w2 + shared_b2)
            out = out @ up_w + up_b
            out = out + (_gelu(x) @ core_w + core_b)
            return out
        ep = [(e0_w1, e0_b1, e0_w2, e0_b2), (e1_w1, e1_b1, e1_w2, e1_b2), (e2_w1, e2_b1, e2_w2, e2_b2), (e3_w1, e3_b1, e3_w2, e3_b2), (e4_w1, e4_b1, e4_w2, e4_b2), (e5_w1, e5_b1, e5_w2, e5_b2), (e6_w1, e6_b1, e6_w2, e6_b2), (e7_w1, e7_b1, e7_w2, e7_b2)]
        return _forward(x, down_w, down_b, up_w, up_b, router_w, router_b, shared_w1, shared_b1, shared_w2, shared_b2, core_w, core_b, ep)
    x = x + _L0_ffn_ref(_L0_cond_ref(x, cond_2048[:, None, :], L0_cond_W_emb, L0_cond_b_emb, L0_cond_g_norm, L0_cond_W_qkv, L0_cond_g_q, L0_cond_g_k, L0_cond_W_out), L0_ffn_down_w, L0_ffn_down_b, L0_ffn_up_w, L0_ffn_up_b, L0_ffn_router_w, L0_ffn_router_b, L0_ffn_shared_w1, L0_ffn_shared_b1, L0_ffn_shared_w2, L0_ffn_shared_b2, L0_ffn_core_w, L0_ffn_core_b, L0_ffn_e0_w1, L0_ffn_e0_b1, L0_ffn_e0_w2, L0_ffn_e0_b2, L0_ffn_e1_w1, L0_ffn_e1_b1, L0_ffn_e1_w2, L0_ffn_e1_b2, L0_ffn_e2_w1, L0_ffn_e2_b1, L0_ffn_e2_w2, L0_ffn_e2_b2, L0_ffn_e3_w1, L0_ffn_e3_b1, L0_ffn_e3_w2, L0_ffn_e3_b2, L0_ffn_e4_w1, L0_ffn_e4_b1, L0_ffn_e4_w2, L0_ffn_e4_b2, L0_ffn_e5_w1, L0_ffn_e5_b1, L0_ffn_e5_w2, L0_ffn_e5_b2, L0_ffn_e6_w1, L0_ffn_e6_b1, L0_ffn_e6_w2, L0_ffn_e6_b2, L0_ffn_e7_w1, L0_ffn_e7_b1, L0_ffn_e7_w2, L0_ffn_e7_b2)
    return x

_drawn_inputs = setup_inputs


def setup_inputs(seed=0):
    import zlib

    import numpy as np

    out = dict(_drawn_inputs(seed))
    spreads = {'L0_cond_b_emb': (0.0, 0.1),
     'L0_cond_g_norm': (1.0, 0.6),
     'L0_cond_g_q': (1.0, 0.6),
     'L0_cond_g_k': (1.0, 0.6),
     'L0_ffn_down_b': (0.0, 0.8),
     'L0_ffn_up_b': (0.0, 0.536),
     'L0_ffn_router_b': (0.0, 0.8),
     'L0_ffn_shared_b1': (0.0, 2.0),
     'L0_ffn_shared_b2': (0.0, 2.0),
     'L0_ffn_core_b': (0.0, 0.509),
     'L0_ffn_e0_b1': (0.0, 0.8),
     'L0_ffn_e0_b2': (0.0, 1.666),
     'L0_ffn_e1_b1': (0.0, 0.8),
     'L0_ffn_e1_b2': (0.0, 1.709),
     'L0_ffn_e2_b1': (0.0, 0.8),
     'L0_ffn_e2_b2': (0.0, 0.8),
     'L0_ffn_e3_b1': (0.0, 0.8),
     'L0_ffn_e3_b2': (0.0, 1.64),
     'L0_ffn_e4_b1': (0.0, 0.8),
     'L0_ffn_e4_b2': (0.0, 0.8),
     'L0_ffn_e5_b1': (0.0, 0.8),
     'L0_ffn_e5_b2': (0.0, 1.619),
     'L0_ffn_e6_b1': (0.0, 0.8),
     'L0_ffn_e6_b2': (0.0, 0.8),
     'L0_ffn_e7_b1': (0.0, 0.8),
     'L0_ffn_e7_b2': (0.0, 1.568)}
    factors = {'L0_ffn_down_w': 8.0,
     'L0_ffn_router_w': 8.0,
     'L0_ffn_shared_w1': 8.0,
     'L0_ffn_shared_w2': 8.0,
     'L0_ffn_e0_w1': 8.0,
     'L0_ffn_e0_w2': 8.0,
     'L0_ffn_e1_w1': 8.0,
     'L0_ffn_e1_w2': 8.0,
     'L0_ffn_e2_w1': 8.0,
     'L0_ffn_e2_w2': 6.44,
     'L0_ffn_e3_w1': 8.0,
     'L0_ffn_e3_w2': 6.208,
     'L0_ffn_e4_w1': 8.0,
     'L0_ffn_e4_w2': 8.0,
     'L0_ffn_e5_w1': 8.0,
     'L0_ffn_e5_w2': 7.833,
     'L0_ffn_e6_w1': 8.0,
     'L0_ffn_e6_w2': 6.425,
     'L0_ffn_e7_w1': 8.0,
     'L0_ffn_e7_w2': 5.585}
    for name, (base, spread) in spreads.items():
        noise = np.random.default_rng([zlib.crc32(name.encode()), seed]).standard_normal(out[name].shape)
        drawn = base * np.exp(spread * noise) if base else spread * noise
        out[name] = jnp.asarray(drawn.astype(out[name].dtype))
    for name, factor in factors.items():
        out[name] = (out[name] * factor).astype(out[name].dtype)
    return out
```

```python
from contextlib import ExitStack

import concourse.bass as bass
from concourse import mybir

ALU = mybir.AluOpType
ACT = mybir.ActivationFunctionType
AX = mybir.AxisListType
F32 = mybir.dt.float32
F32R = mybir.dt.float32r
I32 = mybir.dt.int32
U32 = mybir.dt.uint32

P = 128
HID = [256, 512, 768, 1024, 256, 512, 768, 1024]
HEADS = 16
EPS = 1e-6
COST_LAMBDA = 1e-7
SHARED_SCALE = 0.1


class Sem:

    def __init__(self, sem):
        self.sem, self.count = sem, 0

    def inc(self, ins, by=1):
        ins.then_inc(self.sem, by)
        self.count += by
        return self.count


def adaln_moe_program(nc, a, out):
    x, cond = a["x"], a["cond"]
    NB, SEQ, D = x.shape
    L = a["down_w"].shape[1]
    E = len(HID)
    NT = NB * SEQ // P
    TB = SEQ // P
    KC = D // P
    LC = L // P
    DH = D // HEADS
    HG = 4
    NG = HEADS // HG
    BLK = 256
    HB = BLK // P
    EXPERT_OF = [e for e, h in enumerate(HID) for _ in range(h // BLK)]
    NEB = len(EXPERT_OF)
    NBLK = NEB + 1
    CH = 512
    NCH = NB * SEQ // CH
    VW = DH + 1
    QW = 4 * DH
    assert SEQ == 256 and D == 512 and L == 256 and DH == 32 and TB == 2

    xt_dram = x.rearrange("b (t p) d -> p (b t) d", p=P)
    out_dram = out.rearrange("b (t p) d -> p (b t) d", p=P)
    ght_dram = nc.dram_tensor("ght_scratch", [P, NB, LC * SEQ], F32).ap()

    with ExitStack() as top:
        def sbt(name, shape, dt=F32, ctx=top):
            return ctx.enter_context(nc.sbuf_tensor(name, shape, dt))

        def sem(name):
            return top.enter_context(nc.semaphore(name))

        bank = {n: top.enter_context(nc.psum_tensor("ps_" + n, [P, 512], F32))
                for n in ("mm", "t0", "t1", "s0", "s1", "a0", "a1", "pv")}
        b_t, b_s, b_a = (bank["t0"], bank["t1"]), (bank["s0"], bank["s1"]), (bank["a0"], bank["a1"])
        b_mm, b_pv = bank["mm"], bank["pv"]

        resid = sbt("resid", [P, NT, D])
        ident = sbt("ident", [P, P])
        logits = sbt("logits", [P, NT, E])

        with ExitStack() as ph:
            def sb(name, shape, dt=F32):
                return sbt(name, shape, dt, ph)

            def pair(name, shape):
                return sb(name + "_hi", shape, F32R), sb(name + "_lo", shape, F32R)

            w_qkv = pair("w_qkv", [P, KC, 3 * D])
            w_out = pair("w_out", [P, KC, D])
            w_core = pair("w_core", [P, KC, D])
            w_down = pair("w_down", [P, KC, L])
            w_router = sb("w_router", [P, KC, E])
            xs = sb("xs", [P, KC * SEQ])
            xt = pair("xt", [P, KC, SEQ])
            qkraw = sb("qkraw", [P, 4, D])
            sq = sb("sq", [P, 2, D])
            q_tok = sb("q_tok", [P, TB, HEADS, QW], F32R)
            k_tok = sb("k_tok", [P, TB, HEADS, QW], F32R)
            stacks = sb("stacks", [P, 8, 512], F32R)
            att = sb("att", [P, 4, 512])
            v_tok = sb("v_tok", [P, TB, HEADS, VW])
            o_tok = xs[:].rearrange("p (t d) -> p t d", d=D)
            gh_tok = sq[:, 0, :].rearrange("p (t d) -> p t d", d=L)
            ght = sq[:, 1, :]
            negmax_row = sb("negmax_row", [HG, 2, SEQ], F32R)
            rowmax = sb("rowmax", [P, 2, TB, HG])
            sel = sb("sel", [HG, HG, P], F32R)
            rden = sb("rden", [P, TB, HG])
            ss = sb("ss", [P, 4, HEADS])
            rs = sb("rs", [P, 4, HEADS])
            rs_b = sb("rs_b", [P, 4 * HEADS])
            ssx = sb("ssx", [P, NT])
            rx = sb("rx", [P, NT])
            cond_row = sb("cond_row", [NB, D])
            condT = sb("condT", [P, KC, NB])
            bemb_col = sb("bemb_col", [P, 2 * KC])
            gnorm_col = sb("gnorm_col", [P, KC])
            aff_scale = sb("aff_scale", [P, KC, NB])
            aff_shift = sb("aff_shift", [P, KC, NB])
            gqk = sb("gqk", [P, DH])
            gk_b = sb("gk_b", [P, DH])
            down_bias = sb("down_bias", [P, L])
            router_bias = sb("router_bias", [P, E])

            oT = stacks[:, 0:2, :], stacks[:, 2:4, :]
            yT = stacks[:, 4:6, :], stacks[:, 6:8, :]
            gyT = oT
            o_f, y_f = att[:, 0:2, :], att[:, 2:4, :]
            gy_f = o_f
            stage = att[:].rearrange("p a b -> p (a b)"), qkraw[:].rearrange("p a b -> p (a b)")

            def quarter(n, part):
                w = (q_tok, k_tok)[n % 2][:, n // 2, :, :]
                if n % 2 == 0:
                    return w.rearrange("p h (r l d) -> p h r l d", l=2, d=DH)[:, :, :, part, :]
                return w.rearrange("p h (l r d) -> p h l r d", l=2, d=DH)[:, :, part, :, :]

            def twice(n):
                return qkraw[:, n, :].rearrange("p (h d) -> p h d", d=DH).unsqueeze(2).to_broadcast([P, HEADS, 2, DH])

            d_x = [sem(f"d_x{b}") for b in range(NB)]
            d_small, d_wemb = sem("d_small"), [sem("d_wemb0"), sem("d_wemb1")]
            d_w = [sem("d_w0"), sem("d_w1")]
            d_ght = sem("d_ght")
            p_const = sem("p_const")
            pc = Sem(p_const)
            v_step, v_wsplit, a_wsplit = Sem(sem("v_step")), Sem(sem("v_wsplit")), Sem(sem("a_wsplit"))
            a_ssx = sem("a_ssx")
            e_condT, e_ada = sem("e_condT"), sem("e_ada")
            v_condT, v_ada = sem("v_condT"), sem("v_ada")
            v_xs, e_xT, a_xaff, v_xT = sem("v_xs"), sem("e_xT"), sem("a_xaff"), sem("v_xT")
            e_qkv, a_mm = sem("e_qkv"), sem("a_mm")
            p_sq, p_gq, v_ss = sem("p_sq"), sem("p_gq"), sem("v_ss")
            v_qn, a_qhi, v_qlo = sem("v_qn"), sem("a_qhi"), sem("v_qlo")
            e_T, a_evT, v_evT = sem("e_T"), sem("a_evT"), sem("v_evT")
            e_S, v_max, e_mT, v_mrow = sem("e_S"), sem("v_max"), sem("e_mT"), sem("v_mrow")
            e_ST, a_exp, e_PV, v_rden, v_norm = sem("e_ST"), sem("a_exp"), sem("e_PV"), sem("v_rden"), sem("v_norm")
            e_oT, a_of, v_oT = sem("e_oT"), sem("a_of"), sem("v_oT")
            e_yT, v_y, a_yhi, v_ylo, a_gy, a_gyhi, v_gylo = (
                sem("e_yT"), sem("v_y"), sem("a_yhi"), sem("v_ylo"), sem("a_gy"), sem("a_gyhi"), sem("v_gylo"))
            e_down, v_h, a_gh, e_router, v_logits = sem("e_down"), sem("v_h"), sem("a_gh"), sem("e_router"), sem("v_logits")
            e_core, v_core, e_ghT, a_ghT = sem("e_core"), sem("v_core"), sem("e_ghT"), sem("a_ghT")

            parts = []
            wq_dram = a["w_qkv"].rearrange("(c p) n -> p c n", p=P)
            for c in range(KC):
                parts.append((wq_dram[:, c, :], [w[:, c, :] for w in w_qkv], 3 * D))
            for w, name in ((w_out, "w_out"), (w_core, "core_w"), (w_down, "down_w")):
                n = a[name].shape[1]
                dram = a[name].rearrange("(c p) n -> p c n", p=P)
                parts.append((dram, [t[:].rearrange("p c n -> p (c n)") for t in w], KC * n))
            NPART = len(parts)
            W_QKV_PARTS, W_OUT_PARTS, W_CORE_PARTS, W_DOWN_PARTS = KC, KC + 1, KC + 2, KC + 3
            block = ph.enter_context(nc.Block())

            @block.sync
            def _(sp):
                sp.dma_start(cond_row[:], cond).then_inc(d_small, 16)
                sp.dma_start(resid[:, 0:TB, :], xt_dram[:, 0:TB, :]).then_inc(d_x[0], 16)
                with nc.allow_non_contiguous_dma(reason="columns of biases and gains"):
                    sp.dma_start(bemb_col[:], a["b_emb"].rearrange("(c p) -> p c", p=P)).then_inc(d_small, 16)
                    sp.dma_start(gnorm_col[:], a["g_norm"].rearrange("(c p) -> p c", p=P)).then_inc(d_small, 16)
                    sp.dma_start(w_router[:], a["router_w"].rearrange("(c p) n -> p c n", p=P)).then_inc(d_small, 16)
                    sp.dma_start(gqk[:], a["g_q"].partition_broadcast(P)).then_inc(d_small, 16)
                    sp.dma_start(gk_b[:], a["g_k"].partition_broadcast(P)).then_inc(d_small, 16)
                    sp.dma_start(down_bias[:], a["down_b"].partition_broadcast(P)).then_inc(d_small, 16)
                    sp.dma_start(router_bias[:], a["router_b"].partition_broadcast(P)).then_inc(d_small, 16)
                for c in range(KC):
                    if c >= 2:
                        sp.wait_ge(e_ada, c - 1)
                    sp.dma_start(stage[c % 2][:, 0:2 * D],
                                 a["w_emb"].rearrange("(c p) n -> p c n", p=P)[:, c, :]).then_inc(d_wemb[c % 2], 16)
                for b in range(1, NB):
                    sp.dma_start(resid[:, b * TB:(b + 1) * TB, :], xt_dram[:, b * TB:(b + 1) * TB, :]).then_inc(d_x[b], 16)
                for n, (src, _, size) in enumerate(parts):
                    sp.wait_ge(e_ada, 3 + n % 2 if n < 2 else 4)
                    if n >= 2:
                        sp.wait_ge(v_wsplit.sem, n - 1)
                    dst = stage[n % 2][:, 0:size]
                    if len(src.shape) == 3:
                        dst = dst.rearrange("p (c n) -> p c n", c=KC)
                    sp.dma_start(dst, src).then_inc(d_w[n % 2], 16)
                for b in range(NB):
                    sp.wait_ge(a_ghT, b + 1)
                    sp.dma_start(ght_dram[:, b, :], ght).then_inc(d_ght, 16)
                sp.wait_ge(d_ght, 16 * NB)

            SMALL = 8

            @block.gpsimd
            def _(pool):
                pc.inc(pool.memset(ident[:], 0.0))
                pool.wait_ge(p_const, 1)
                pc.inc(pool.affine_select(out=ident[:], in_=ident[:], compare_op=ALU.not_equal, fill=1.0,
                                          base=0, pattern=[[-1, P]], channel_multiplier=1))
                pc.inc(pool.memset(v_tok[:, :, :, DH:VW], 1.0))
                g_b = gqk[:].unsqueeze(1).to_broadcast([P, HEADS, DH])
                for b in range(NB):
                    for n in range(4):
                        pool.wait_ge(a_mm, 6 * b + n + 1)
                        if 4 * b + n >= 2:
                            pool.wait_ge(v_ss, 4 * b + n - 1)
                        if n == 1 and b >= 2:
                            pool.wait_ge(d_ght, 16 * (b - 1))
                        pool.tensor_tensor(sq[:, n % 2, :], qkraw[:, n, :], qkraw[:, n, :], ALU.mult).then_inc(p_sq, 1)
                        if n % 2 == 0:
                            if n == 0 and b == 0:
                                pool.wait_ge(v_ada, 2)
                            pool.wait_ge(p_sq, 4 * b + n + 1)
                            q = qkraw[:, n, :].rearrange("p (h d) -> p h d", d=DH)
                            pool.tensor_tensor(q, q, g_b, ALU.mult).then_inc(p_gq, 1)

            @block.scalar
            def _(act):
                def row_squares(b):
                    act.wait_ge(d_x[b], 16)
                    for t in range(TB):
                        i = b * TB + t
                        unused = (q_tok, k_tok)[i // 8][:].rearrange("p t h w -> p (t h w)")[:, (i % 8) * D:(i % 8 + 1) * D]
                        act.activation(unused, resid[:, i, :], ACT.Square,
                                       accum_out=ssx[:, i:i + 1]).then_inc(a_ssx, 1)

                def split_hi(n):
                    act.wait_ge(d_w[n % 2], 16 * (n // 2 + 1))
                    _, (hi, _), size = parts[n]
                    a_wsplit.inc(act.activation(hi, stage[n % 2][:, 0:size], ACT.Copy))

                def x_affine(b):
                    for c in range(KC):
                        src = (b_t[1], b_a[1])[c // 2][:, (c % 2) * SEQ:(c % 2 + 1) * SEQ]
                        if c % 2 == 0:
                            act.wait_ge(e_xT, 2 * b + c // 2 + 1)
                        if c == 0:
                            act.wait_ge(e_xT, 2 * b + 2)
                        act.activation(xs[:, c * SEQ:(c + 1) * SEQ], src, ACT.Identity,
                                       bias=aff_shift[:, c, b:b + 1], scale=aff_scale[:, c, b:b + 1]).then_inc(a_xaff, 1)

                def copy_chunk(b, n):
                    act.wait_ge(e_qkv, 6 * b + n + 1)
                    if n < 4:
                        act.activation(qkraw[:, n, :], b_mm[:], ACT.Copy).then_inc(a_mm, 1)
                    else:
                        act.activation(v_tok[:, n - 4, :, 0:DH], b_mm[:].rearrange("p (h d) -> p h d", d=DH),
                                       ACT.Copy).then_inc(a_mm, 1)

                def q_hi(b):
                    for n in range(4):
                        act.wait_ge(v_qn, 4 * b + n + 1)
                        act.activation(quarter(n, 0), twice(n), ACT.Copy).then_inc(a_qhi, 1)

                def ev_T(b, h):
                    act.wait_ge(e_T, HEADS * b + h + 1)
                    act.activation(stacks[:, h % 8, :], b_t[h % 2][:], ACT.Copy).then_inc(a_evT, 1)

                def exp(b, h):
                    act.wait_ge(e_ST, HEADS * b + h + 1)
                    act.activation(att[:, h % 4, :], b_a[h % 2][:], ACT.Exp).then_inc(a_exp, 1)

                row_squares(0)
                act.wait_ge(v_ada, 1)
                x_affine(0)
                for n in range(W_QKV_PARTS):
                    split_hi(n)
                for b in range(1, NB):
                    row_squares(b)
                for n in range(W_QKV_PARTS, NPART):
                    split_hi(n)
                for n in range(4):
                    if n == 0:
                        act.wait_ge(v_wsplit.sem, NPART)
                    copy_chunk(0, n)
                q_hi(0)
                for n in (4, 5):
                    if n == 4:
                        act.wait_ge(p_const, 3)
                    copy_chunk(0, n)
                x_affine(1)

                for b in range(NB):
                    for g in range(NG + 1):
                        for j in range(HG):
                            h = HG * g + j
                            if g < NG and h % 2 == 0:
                                ev_T(b, h)
                            if g >= 1:
                                exp(b, h - HG)
                        if g < NG and b + 1 < NB:
                            copy_chunk(b + 1, g)
                    for i in range(2):
                        act.wait_ge(e_oT, 2 * b + i + 1)
                        act.activation(o_f[:, i, :], b_t[i][:], ACT.Copy).then_inc(a_of, 1)
                    if b + 1 < NB:
                        copy_chunk(b + 1, 4)
                        q_hi(b + 1)
                    for i in range(2):
                        act.wait_ge(v_y, 2 * b + i + 1)
                        act.activation(yT[0][:, i, :], y_f[:, i, :], ACT.Copy).then_inc(a_yhi, 1)
                    for i in range(2):
                        act.activation(gy_f[:, i, :], y_f[:, i, :], ACT.Gelu).then_inc(a_gy, 1)
                    if b + 1 < NB:
                        copy_chunk(b + 1, 5)
                    for i in range(2):
                        act.wait_ge(a_gy, 2 * b + i + 1)
                        act.activation(gyT[0][:, i, :], gy_f[:, i, :], ACT.Copy).then_inc(a_gyhi, 1)
                    if b + 2 < NB:
                        x_affine(b + 2)
                    for t in range(TB):
                        act.wait_ge(v_h, 2 * b + t + 1)
                        act.activation(gh_tok[:, t, :], gh_tok[:, t, :], ACT.Gelu).then_inc(a_gh, 1)
                    act.wait_ge(e_ghT, b + 1)
                    if b >= 1:
                        act.wait_ge(d_ght, 16 * b)
                    act.activation(ght, b_t[0][:], ACT.Copy).then_inc(a_ghT, 1)

            @block.vector
            def _(dve):
                def step(ins):
                    dve.wait_ge(v_step.sem, v_step.inc(ins))

                def rsqrt(dst, tmp, src, mean_over):
                    step(dve.tensor_scalar(src, src, 1.0 / mean_over, EPS, ALU.mult, ALU.add))
                    step(dve.tensor_single_scalar(tmp.bitcast(I32), src.bitcast(I32), 1, ALU.logical_shift_right))
                    step(dve.tensor_scalar(dst.bitcast(I32), tmp.bitcast(I32), -1, 0x5F3759DF, ALU.mult, ALU.add))
                    for _ in range(3):
                        step(dve.tensor_tensor(tmp, dst, dst, ALU.mult))
                        step(dve.scalar_tensor_tensor(out=tmp, in0=tmp, scalar=-0.5, in1=src, op0=ALU.mult, op1=ALU.mult))
                        step(dve.scalar_tensor_tensor(out=dst, in0=tmp, scalar=1.5, in1=dst, op0=ALU.add, op1=ALU.mult))

                def split_lo(n):
                    dve.wait_ge(a_wsplit.sem, n + 1)
                    _, (hi, lo), size = parts[n]
                    v_wsplit.inc(dve.tensor_tensor(lo, stage[n % 2][:, 0:size], hi.bitcast(F32), ALU.subtract))

                def scale_x(b):
                    for t in range(TB):
                        i = b * TB + t
                        dve.tensor_scalar(xs[:, t * D:(t + 1) * D], resid[:, i, :], rx[:, i:i + 1], None,
                                          ALU.mult).then_inc(v_xs, 1)

                def split_x(b):
                    dve.wait_ge(a_xaff, KC * (b + 1))
                    hi, lo = (w[:].rearrange("p c s -> p (c s)") for w in xt)
                    dve.tensor_copy(hi, xs[:]).then_inc(v_xT, 1)
                    dve.wait_ge(v_xT, 2 * b + 1)
                    dve.tensor_tensor(lo, xs[:], hi.bitcast(F32), ALU.subtract).then_inc(v_xT, 1)

                def sum_squares(b, n):
                    dve.wait_ge(p_sq, 4 * b + n + 1)
                    dve.tensor_reduce(ss[:, n, :], sq[:, n % 2, :].rearrange("p (h d) -> p h d", d=DH),
                                      AX.X, ALU.add).then_inc(v_ss, 1)

                def normalise_qk(b):
                    dve.wait_ge(v_ss, 4 * (b + 1))
                    flat = lambda t: t[:].rearrange("p n h -> p (n h)")
                    rsqrt(flat(rs), rs_b[:], flat(ss), DH)
                    dve.wait_ge(p_gq, 2 * (b + 1))
                    for n in range(4):
                        q = qkraw[:, n, :].rearrange("p (h d) -> p h d", d=DH)
                        dve.tensor_tensor(q, q, rs[:, n, :].unsqueeze(2).to_broadcast([P, HEADS, DH]),
                                          ALU.mult).then_inc(v_qn, 1)
                    for n in range(4):
                        dve.wait_ge(a_qhi, 4 * b + n + 1)
                        dve.tensor_tensor(quarter(n, 1), twice(n), quarter(n, 0).bitcast(F32), ALU.subtract).then_inc(v_qlo, 1)

                def norm(b, g):
                    dve.wait_ge(e_PV, NG * b + g + 1)
                    pv = b_pv[:, 0:TB * HG * VW].rearrange("p (t j w) -> p t j w", t=TB, w=VW)
                    dve.reciprocal(rden[:], pv[:, :, :, DH]).then_inc(v_rden, 1)
                    dve.wait_ge(v_rden, NG * b + g + 1)
                    for t in range(TB):
                        o = o_tok[:, t, g * HG * DH:(g + 1) * HG * DH].rearrange("p (j d) -> p j d", d=DH)
                        dve.tensor_tensor(o, pv[:, t, :, 0:DH], rden[:, t, :].unsqueeze(2).to_broadcast([P, HG, DH]),
                                          ALU.mult).then_inc(v_norm, 1)

                def row_max(b, h):
                    dve.wait_ge(e_S, HEADS * b + h + 1)
                    dve.tensor_reduce(rowmax[:, (h // HG) % 2, :, h % HG], b_s[h % 2][:].rearrange("p (t k) -> p t k", t=TB),
                                      AX.X, ALU.max).then_inc(v_max, 1)

                dve.wait_ge(e_condT, 1)
                dve.tensor_copy(condT[:], b_s[0][:, 0:KC * NB].rearrange("p (c b) -> p c b", b=NB)).then_inc(v_condT, 1)
                dve.wait_ge(a_ssx, TB)
                rsqrt(rx[:, 0:TB], rs_b[:, 0:TB], ssx[:, 0:TB], D)
                scale_x(0)
                dve.wait_ge(d_small, 16 * SMALL)
                dve.wait_ge(e_ada, KC)
                step(dve.tensor_copy(rs_b[:], b_s[1][:, 0:64]))
                for c in range(1, KC):
                    step(dve.tensor_tensor(rs_b[:], rs_b[:], b_s[1][:, c * 64:(c + 1) * 64], ALU.add))
                ada = rs_b[:].rearrange("p (f b) -> p f b", b=NB)
                step(dve.tensor_tensor(aff_shift[:], ada[:, KC:, :], bemb_col[:, KC:].unsqueeze(2).to_broadcast([P, KC, NB]), ALU.add))
                step(dve.tensor_tensor(aff_scale[:], ada[:, 0:KC, :], bemb_col[:, 0:KC].unsqueeze(2).to_broadcast([P, KC, NB]), ALU.add))
                gn = gnorm_col[:].unsqueeze(2).to_broadcast([P, KC, NB])
                dve.scalar_tensor_tensor(out=aff_scale[:], in0=aff_scale[:], scalar=1.0, in1=gn,
                                         op0=ALU.add, op1=ALU.mult).then_inc(v_ada, 1)
                dve.scalar_tensor_tensor(out=gqk[:], in0=gqk[:], scalar=float(DH) ** -0.5, in1=gk_b[:],
                                         op0=ALU.mult, op1=ALU.mult).then_inc(v_ada, 1)
                for e, hid in enumerate(HID):
                    step(dve.tensor_scalar(router_bias[:, e:e + 1], router_bias[:, e:e + 1],
                                           -COST_LAMBDA * 2 * L * hid, None, ALU.add))
                dve.wait_ge(p_const, 2)
                step(dve.tensor_copy(sel[:], ident[0:HG, 0:HG].unsqueeze(2).to_broadcast([HG, HG, P])))
                split_x(0)
                for n in range(W_QKV_PARTS):
                    split_lo(n)
                dve.wait_ge(a_ssx, NT)
                rsqrt(rx[:, TB:NT], rs_b[:, 0:NT - TB], ssx[:, TB:NT], D)
                for n in range(W_QKV_PARTS, NPART):
                    split_lo(n)
                for n in range(4):
                    sum_squares(0, n)
                scale_x(1)
                normalise_qk(0)
                split_x(1)

                for b in range(NB):
                    for g in range(NG + 1):
                        for j in range(HG):
                            h = HG * g + j
                            if g < NG:
                                if h % 2 == 1:
                                    dve.wait_ge(e_T, HEADS * b + h + 1)
                                    dve.tensor_copy(stacks[:, h % 8, :], b_t[1][:]).then_inc(v_evT, 1)
                                if j >= 1:
                                    row_max(b, h - 1)
                        if g < NG:
                            row_max(b, HG * g + HG - 1)
                            dve.wait_ge(e_mT, NG * b + g + 1)
                            dve.tensor_scalar(negmax_row[:, g % 2, :], b_t[0][0:HG, 0:SEQ], -1.0, None,
                                              ALU.mult).then_inc(v_mrow, 1)
                        if g >= 1:
                            norm(b, g - 1)
                        if g < NG and b + 1 < NB:
                            sum_squares(b + 1, g)
                    for i in range(2):
                        dve.wait_ge(a_of, 2 * b + i + 1)
                        dve.tensor_copy(oT[0][:, i, :], o_f[:, i, :]).then_inc(v_oT, 1)
                        dve.wait_ge(v_oT, 4 * b + 2 * i + 1)
                        dve.tensor_tensor(oT[1][:, i, :], o_f[:, i, :], oT[0][:, i, :].bitcast(F32), ALU.subtract).then_inc(v_oT, 1)
                    if b + 2 < NB:
                        scale_x(b + 2)
                    if b + 1 < NB:
                        normalise_qk(b + 1)
                    for i in range(2):
                        dve.wait_ge(e_yT, 2 * b + i + 1)
                        dve.tensor_tensor(y_f[:, i, :], b_s[i][:], o_f[:, i, :], ALU.add).then_inc(v_y, 1)
                    for i in range(2):
                        dve.wait_ge(a_yhi, 2 * b + i + 1)
                        dve.tensor_tensor(yT[1][:, i, :], y_f[:, i, :], yT[0][:, i, :].bitcast(F32), ALU.subtract).then_inc(v_ylo, 1)
                    for i in range(2):
                        dve.wait_ge(a_gyhi, 2 * b + i + 1)
                        dve.tensor_tensor(gyT[1][:, i, :], gy_f[:, i, :], gyT[0][:, i, :].bitcast(F32), ALU.subtract).then_inc(v_gylo, 1)
                    for t in range(TB):
                        dve.wait_ge(e_down, TB * (b + 1))
                        dve.tensor_tensor(gh_tok[:, t, :], b_a[0][:, t * L:(t + 1) * L], down_bias[:], ALU.add).then_inc(v_h, 1)
                    dve.wait_ge(e_router, b + 1)
                    dve.tensor_tensor(logits[:, b * TB:(b + 1) * TB, :], b_pv[:, 0:TB * E].rearrange("p (t e) -> p t e", e=E),
                                      router_bias[:].unsqueeze(1).to_broadcast([P, TB, E]), ALU.add).then_inc(v_logits, 1)
                    if b + 2 < NB:
                        split_x(b + 2)
                    for t in range(TB):
                        dve.wait_ge(e_core, TB * b + t + 1)
                        dve.tensor_tensor(resid[:, b * TB + t, :], resid[:, b * TB + t, :], b_s[t][:], ALU.add).then_inc(v_core, 1)

            @block.tensor
            def _(pe):
                def three(out_ap, lhs, rhs, first, last):
                    pe.matmul(out_ap, lhs[0], rhs[0], start=first, stop=False)
                    pe.matmul(out_ap, lhs[0], rhs[1], start=False, stop=False)
                    return pe.matmul(out_ap, lhs[1], rhs[0], start=False, stop=last)

                def x_T(b):
                    pe.wait_ge(v_xs, TB * (b + 1))
                    if b >= 2:
                        pe.wait_ge(a_of, 2 * (b - 2) + 2)
                    for half in range(2):
                        if half == 1 and b >= 2:
                            pe.wait_ge(a_exp, HEADS * (b - 1))
                        for c in (2 * half, 2 * half + 1):
                            for t in range(TB):
                                mm = pe.transpose((b_t[1], b_a[1])[half][:, (c % 2) * SEQ + t * P:(c % 2) * SEQ + (t + 1) * P],
                                                  xs[:, t * D + c * P:t * D + (c + 1) * P], ident[:])
                        mm.then_inc(e_xT, 1)

                CHUNKS = [(0, 0), (0, 1), (1, 0), (1, 1), (0, 2), (1, 2)]

                def qkv(b, n, c):
                    t, part = CHUNKS[n]
                    if c == 0:
                        if n == 0:
                            pe.wait_ge(v_xT, 2 * (b + 1))
                        if 6 * b + n >= 1:
                            pe.wait_ge(a_mm, 6 * b + n)
                    if b == 0 and n == 0:
                        pe.wait_ge(v_wsplit.sem, c + 1)
                    mm = three(b_mm[:], [w[:, c, t * P:(t + 1) * P] for w in xt],
                               [w[:, c, part * D:(part + 1) * D] for w in w_qkv], c == 0, c == KC - 1)
                    if c == KC - 1:
                        mm.then_inc(e_qkv, 1)

                def stack_T(b, h):
                    if h == 0:
                        pe.wait_ge(v_qlo, 4 * (b + 1))
                        if b >= 1:
                            pe.wait_ge(a_ghT, b)
                    if h == 1:
                        pe.wait_ge(a_xaff, KC * min(b + 2, NB))
                    if h >= 2:
                        if h % 2 == 0:
                            pe.wait_ge(a_evT, 8 * b + h // 2)
                        else:
                            pe.wait_ge(v_evT, 8 * b + h // 2)
                    if h % HG == 0 and h > 0:
                        pe.wait_ge(v_mrow, NG * b + h // HG)
                    for half, src in ((0, q_tok), (1, k_tok)):
                        for t in range(TB):
                            w = src[:, t, h, :].bitcast(F32)
                            o = (half * TB + t) * P
                            mm = pe.transpose(b_t[h % 2][:, o:o + P], w, ident[:])
                    mm.then_inc(e_T, 1)

                def scores(b, h):
                    if h % 2 == 0:
                        pe.wait_ge(a_evT, 8 * b + h // 2 + 1)
                    else:
                        pe.wait_ge(v_evT, 8 * b + h // 2 + 1)
                    if h >= 2:
                        pe.wait_ge(v_max, HEADS * b + h - 1)
                    elif b >= 1:
                        pe.wait_ge(v_core, TB * b)
                    st = stacks[:, h % 8, :]
                    for t in range(TB):
                        mm = pe.matmul(b_s[h % 2][:, t * SEQ:(t + 1) * SEQ], st[:, t * P:(t + 1) * P], st[:, SEQ:2 * SEQ],
                                       start=True, stop=True)
                    mm.then_inc(e_S, 1)

                def max_T(b, g):
                    pe.wait_ge(v_max, HEADS * b + HG * (g + 1))
                    pe.wait_ge(a_evT, 8 * b + 2 * (g + 1))
                    for t in range(TB):
                        mm = pe.transpose(b_t[0][0:HG, t * P:(t + 1) * P], rowmax[:, g % 2, t, :], ident[:])
                    mm.then_inc(e_mT, 1)

                def scores_T(b, h):
                    g, j = h // HG, h % HG
                    if j == 0:
                        pe.wait_ge(v_mrow, NG * b + g + 1)
                    if h >= 2:
                        pe.wait_ge(a_exp, HEADS * b + h - 1)
                    else:
                        if b >= 1:
                            pe.wait_ge(v_h, TB * b)
                        pe.wait_ge(a_xaff, KC * min(b + 2, NB))
                    st = stacks[:, h % 8, :]
                    for k in range(TB):
                        o = b_a[h % 2][:, k * SEQ:(k + 1) * SEQ]
                        pe.matmul(o, st[:, SEQ + k * P:SEQ + (k + 1) * P], st[:, 0:SEQ], start=True, stop=False)
                        mm = pe.matmul(o, sel[:, j, :], negmax_row[:, g % 2, :], start=False, stop=True)
                    mm.then_inc(e_ST, 1)

                def values(b, h):
                    g, j = h // HG, h % HG
                    pe.wait_ge(a_exp, HEADS * b + h + 1)
                    if j == 0:
                        if g >= 1:
                            pe.wait_ge(v_norm, 2 * (NG * b + g))
                        else:
                            pe.wait_ge(a_mm, 6 * b + 6)
                            if b >= 1:
                                pe.wait_ge(v_logits, b)
                    for t in range(TB):
                        for k in range(TB):
                            o = (t * HG + j) * VW
                            mm = pe.matmul(b_pv[:, o:o + VW], att[:, h % 4, k * SEQ + t * P:k * SEQ + (t + 1) * P],
                                           v_tok[:, k, h, :], start=k == 0, stop=k == TB - 1)
                    if j == HG - 1:
                        mm.then_inc(e_PV, 1)

                def o_T(b):
                    pe.wait_ge(v_norm, 2 * NG * (b + 1))
                    pe.wait_ge(v_mrow, NG * (b + 1))
                    pe.wait_ge(v_evT, 8 * (b + 1))
                    for half in range(2):
                        for c in (2 * half, 2 * half + 1):
                            for t in range(TB):
                                mm = pe.transpose(b_t[half][:, (c % 2) * SEQ + t * P:(c % 2) * SEQ + (t + 1) * P],
                                                  o_tok[:, t, c * P:(c + 1) * P], ident[:])
                        mm.then_inc(e_oT, 1)

                def feat(w, c):
                    return w[:, c // 2, (c % 2) * SEQ:(c % 2 + 1) * SEQ]

                def y_T(b):
                    pe.wait_ge(v_oT, 4 * (b + 1))
                    if b == 0:
                        pe.wait_ge(v_wsplit.sem, W_OUT_PARTS)
                    for f in range(KC):
                        for c in range(KC):
                            mm = three(b_s[f // 2][:, (f % 2) * SEQ:(f % 2 + 1) * SEQ],
                                       [w[:, c, f * P:(f + 1) * P] for w in w_out], [feat(w, c) for w in oT],
                                       c == 0, c == KC - 1)
                        if f % 2 == 1:
                            mm.then_inc(e_yT, 1)

                def down_and_router(b):
                    pe.wait_ge(a_yhi, 2 * (b + 1))
                    pe.wait_ge(v_ylo, 2 * (b + 1))
                    if b == 0:
                        pe.wait_ge(v_wsplit.sem, W_DOWN_PARTS)
                    pe.wait_ge(a_exp, HEADS * (b + 1))
                    for t in range(TB):
                        for c in range(KC):
                            mm = three(b_a[0][:, t * L:(t + 1) * L], [feat(w, c)[:, t * P:(t + 1) * P] for w in yT],
                                       [w[:, c, :] for w in w_down], c == 0, c == KC - 1)
                        mm.then_inc(e_down, 1)
                    for t in range(TB):
                        for c in range(KC):
                            mm = pe.matmul(b_pv[:, t * E:(t + 1) * E], feat(y_f, c)[:, t * P:(t + 1) * P], w_router[:, c, :],
                                           start=c == 0, stop=c == KC - 1)
                    mm.then_inc(e_router, 1)

                def core(b):
                    pe.wait_ge(a_gyhi, 2 * (b + 1))
                    pe.wait_ge(v_gylo, 2 * (b + 1))
                    for t in range(TB):
                        for c in range(KC):
                            mm = three(b_s[t][:], [feat(w, c)[:, t * P:(t + 1) * P] for w in gyT],
                                       [w[:, c, :] for w in w_core], c == 0, c == KC - 1)
                        mm.then_inc(e_core, 1)

                def gh_T(b):
                    pe.wait_ge(a_gh, TB * (b + 1))
                    for c in range(LC):
                        for t in range(TB):
                            mm = pe.transpose(b_t[0][:, c * SEQ + t * P:c * SEQ + (t + 1) * P], gh_tok[:, t, c * P:(c + 1) * P], ident[:])
                    mm.then_inc(e_ghT, 1)

                pe.wait_ge(d_small, 16 * SMALL)
                pe.wait_ge(p_const, 2)
                for c in range(KC):
                    mm = pe.transpose(b_s[0][:, c * NB:(c + 1) * NB], cond_row[:, c * P:(c + 1) * P], ident[0:NB, 0:NB])
                mm.then_inc(e_condT, 1)
                pe.wait_ge(v_condT, 1)
                for c in range(KC):
                    pe.wait_ge(d_wemb[c % 2], 16 * (c // 2 + 1))
                    for f in range(2 * KC):
                        mm = pe.matmul(b_s[1][:, c * 64 + f * NB:c * 64 + (f + 1) * NB], stage[c % 2][:, f * P:(f + 1) * P],
                                       condT[:, c, :], start=True, stop=True)
                    mm.then_inc(e_ada, 1)
                x_T(0)
                for n in range(6):
                    for c in range(KC):
                        qkv(0, n, c)
                x_T(1)
                for b in range(NB):
                    for g in range(NG + 1):
                        for j in range(HG):
                            h = HG * g + j
                            if g < NG:
                                stack_T(b, h)
                            if g >= 1:
                                scores_T(b, h - HG)
                            if g < NG and b + 1 < NB:
                                qkv(b + 1, g, j)
                            if g < NG and j >= 1:
                                scores(b, h - 1)
                            if g >= 1 and j >= 1:
                                values(b, h - HG - 1)
                        if g < NG:
                            scores(b, HG * g + HG - 1)
                        if g >= 1:
                            values(b, HG * g - 1)
                        if g < NG:
                            max_T(b, g)
                    o_T(b)
                    if b + 1 < NB:
                        for c in range(KC):
                            qkv(b + 1, 4, c)
                    y_T(b)
                    if b + 1 < NB:
                        for c in range(KC):
                            qkv(b + 1, 5, c)
                    if b + 2 < NB:
                        x_T(b + 2)
                    down_and_router(b)
                    core(b)
                    gh_T(b)

        with ExitStack() as ph:
            def sb(name, shape, dt=F32):
                return sbt(name, shape, dt, ph)

            def pair(name, shape):
                return sb(name + "_hi", shape, F32R), sb(name + "_lo", shape, F32R)

            ghT_f = sb("ghT_f", [P, NB // 4, LC * SEQ])
            ghT = pair("ghT", [P, NB, LC * SEQ])
            acc = sb("acc", [P, NT, L])
            wst = sb("wst", [P, 2, 2, 2 * BLK])
            w1 = pair("w1", [P, 2, LC * BLK])
            w2 = pair("w2", [P, 2, HB * L])
            hid_f = sb("hid_f", [P, 2, HB, CH])
            hid = pair("hid", [P, 2, HB * CH])
            b1_col = sb("b1_col", [P, NBLK * HB])
            gb1_col = sb("gb1_col", [P, NBLK * HB])
            gate = sb("gate", [P, NBLK, NT])
            top8 = sb("top8", [P, NT, 8])
            idx8 = sb("idx8", [P, NT, 8], U32)
            idxf = sb("idxf", [P, NT, 8])
            iota8 = sb("iota8", [P, E])
            ex = sb("ex", [P, NT, E])
            g8 = sb("g8", [P, NT, E])
            m8 = sb("m8", [P, NT, E])
            zz = sb("zz", [P, 6, NT])
            mT = sb("mT", [P, LC, E])
            KX = 2 * E + 1
            corr_rhs = sb("corr_rhs", [KX, L])
            gx = sb("gx", [P, NT, KX])
            gxT = sb("gxT", [KX, NT, P])
            accT_f = sb("accT_f", [P, 2, LC * P])
            accT = pair("accT", [P, 2 * LC * P])
            w_up = pair("w_up", [P, LC * D])
            upst = sb("upst", [P, LC * D])
            bias_out = sb("bias_out", [P, 2, D])

            d_gh, d_misc, d_up, d_out = sem("d_gh"), sem("d_misc"), sem("d_up"), sem("d_out")
            d_w12 = [sem("d_w12_0"), sem("d_w12_1")]
            pk = Sem(sem("pk"))
            ak = Sem(sem("ak"))
            vk = Sem(sem("vk"))
            a_whi, v_wlo = sem("a_whi"), sem("v_wlo")
            v_ghi, v_glo = sem("v_ghi"), sem("v_glo")
            e_h, a_gelu, a_hhi, v_hlo = sem("e_h"), sem("a_gelu"), sem("a_hhi"), sem("v_hlo")
            e_o, v_acc, e_m = sem("e_o"), sem("v_acc"), sem("e_m")
            v_gate, a_gate, a_b1 = sem("v_gate"), sem("a_gate"), sem("a_b1")
            v_m, e_mTT, v_mrows, e_gxT, v_gxT = sem("v_m"), sem("e_mTT"), sem("v_mrows"), sem("e_gxT"), sem("v_gxT")
            e_corr, v_corr = sem("e_corr"), sem("v_corr")
            e_aT, a_af, v_ahi, v_alo, e_up, v_up = sem("e_aT"), sem("a_af"), sem("v_ahi"), sem("v_alo"), sem("e_up"), sem("v_up")
            a_uhi, v_ulo = sem("a_uhi"), sem("v_ulo")
            h_banks = (bank["mm"], bank["t0"], bank["t1"])
            o_banks = (bank["s0"], bank["s1"], bank["a0"], bank["a1"])
            m_bank = bank["pv"]

            w1_dram = a["e_w1"].rearrange("(c p) (j n) -> p j c n", p=P, n=BLK)
            w2_dram = a["e_w2"].rearrange("(j c p) n -> p j c n", p=P, c=HB)
            block = ph.enter_context(nc.Block())
            NU = NBLK * NCH
            MISC = 4

            @block.sync
            def _(sp):
                with nc.allow_non_contiguous_dma(reason="columns of biases"):
                    sp.dma_start(b1_col[:], a["e_b1"].rearrange("(c p) -> p c", p=P)).then_inc(d_misc, 16)
                sp.dma_start(bias_out[:, 0, :], a["up_b"].partition_broadcast(P)).then_inc(d_misc, 16)
                sp.dma_start(bias_out[:, 1, :], a["core_b"].partition_broadcast(P)).then_inc(d_misc, 16)
                sp.dma_start(corr_rhs[E:KX, :], a["e_b2"]).then_inc(d_misc, 16)
                for q in range(4):
                    if q >= 1:
                        sp.wait_ge(v_glo, q)
                    n = NB // 4
                    sp.dma_start(ghT_f[:], ght_dram[:, q * n:(q + 1) * n, :]).then_inc(d_gh, 16)
                    if q < 2:
                        for w, dram in ((0, w1_dram), (1, w2_dram)):
                            sp.dma_start(wst[:, q, w, :].rearrange("p (c n) -> p c n", c=2), dram[:, q, :, :]).then_inc(d_w12[q], 16)
                for j in range(2, NBLK):
                    sp.wait_ge(v_wlo, 2 * (j - 1))
                    sp.wait_ge(e_m, j - 1)
                    for w, dram in ((0, w1_dram), (1, w2_dram)):
                        sp.dma_start(wst[:, j % 2, w, :].rearrange("p (c n) -> p c n", c=2), dram[:, j, :, :]).then_inc(d_w12[j % 2], 16)
                    if j == 4:
                        sp.dma_start(upst[:].rearrange("p (c n) -> p c n", c=LC), a["up_w"].rearrange("(c p) n -> p c n", p=P)).then_inc(d_up, 16)
                for i in range(NT):
                    sp.wait_ge(v_up, i + 1)
                    sp.dma_start(out_dram[:, i, :], resid[:, i, :]).then_inc(d_out, 16)
                sp.wait_ge(d_out, 16 * NT)

            @block.gpsimd
            def _(pool):
                pk.inc(pool.iota(iota8[:], pattern=[[1, E]], base=0, channel_multiplier=0,
                                 allow_small_or_imprecise_dtypes=True))
                pk.inc(pool.memset(gx[:, :, E:2 * E], 1.0))
                pk.inc(pool.memset(gx[:, :, 2 * E:KX], SHARED_SCALE))
                pk.inc(pool.memset(gate[:, NEB:NBLK, :], SHARED_SCALE))
                pool.wait_ge(d_misc, 16 * MISC)
                pk.inc(pool.tensor_tensor(bias_out[:, 0, :], bias_out[:, 0, :], bias_out[:, 1, :], ALU.add))
                pool.wait_ge(pk.sem, pk.count)
                for i in range(NT):
                    pk.inc(pool.tensor_tensor(resid[:, i, :], resid[:, i, :], bias_out[:, 0, :], ALU.add))

            P_CONST, P_RESID = 4, 5

            @block.scalar
            def _(act):
                act.wait_ge(v_gate, 1)
                act.activation(ex[:], ex[:], ACT.Exp).then_inc(a_gate, 1)

                def split_hi(j):
                    act.wait_ge(d_w12[j % 2], 32 * (j // 2 + 1))
                    if j >= 2:
                        act.wait_ge(e_o, 4 * NCH * (j - 1))
                    for w, dst in ((0, w1), (1, w2)):
                        act.activation(dst[0][:, j % 2, :], wst[:, j % 2, w, :], ACT.Copy).then_inc(a_whi, 1)

                split_hi(0)
                split_hi(1)
                act.wait_ge(v_gate, 2)
                act.activation(zz[:, 2, :], zz[:, 2, :], ACT.Exp).then_inc(a_gate, 1)
                act.wait_ge(d_misc, 16 * MISC)
                act.activation(gb1_col[:], b1_col[:], ACT.Gelu).then_inc(a_b1, 1)
                for u in range(NU):
                    j, c = u // NCH, u % NCH
                    for hb in range(HB):
                        v = u * HB + hb
                        act.wait_ge(e_h, v + 1)
                        act.activation(hid_f[:, u % 2, hb, :], h_banks[v % 3][:], ACT.Gelu,
                                       bias=b1_col[:, j * HB + hb:j * HB + hb + 1]).then_inc(a_gelu, 1)
                        act.wait_ge(a_gelu, v + 1)
                        act.activation(hid[0][:, u % 2, hb * CH:(hb + 1) * CH], hid_f[:, u % 2, hb, :], ACT.Copy).then_inc(a_hhi, 1)
                    if c == 0 and 1 <= j and j + 1 < NBLK:
                        split_hi(j + 1)
                    if u == 5 * NCH:
                        act.wait_ge(d_up, 16)
                        act.activation(w_up[0][:], upst[:], ACT.Copy).then_inc(a_uhi, 1)
                for i in range(NT):
                    act.wait_ge(e_aT, i + 1)
                    if i >= 2:
                        act.wait_ge(v_alo, i - 1)
                    act.activation(accT_f[:, i % 2, :], h_banks[i % 3][:, 0:LC * P], ACT.Copy).then_inc(a_af, 1)

            @block.vector
            def _(dve):
                def step(ins):
                    dve.wait_ge(vk.sem, vk.inc(ins))

                def split_gh(q):
                    n = NB // 4
                    dve.wait_ge(d_gh, 16 * (q + 1))
                    s = slice(q * n, (q + 1) * n)
                    dve.tensor_copy(ghT[0][:, s, :], ghT_f[:]).then_inc(v_ghi, 1)
                    dve.wait_ge(v_ghi, q + 1)
                    dve.tensor_tensor(ghT[1][:, s, :], ghT_f[:], ghT[0][:, s, :].bitcast(F32), ALU.subtract).then_inc(v_glo, 1)

                def split_lo(j):
                    for w, dst in ((0, w1), (1, w2)):
                        dve.wait_ge(a_whi, 2 * j + w + 1)
                        dve.tensor_tensor(dst[1][:, j % 2, :], wst[:, j % 2, w, :], dst[0][:, j % 2, :].bitcast(F32),
                                          ALU.subtract).then_inc(v_wlo, 1)

                split_gh(0)
                for i in range(NT):
                    dve.max(top8[:, i, :], logits[:, i, :]).then_inc(vk.sem, 1)
                    vk.count += 1
                dve.wait_ge(vk.sem, vk.count)
                dve.tensor_tensor(ex[:], logits[:], top8[:, :, 0:1].to_broadcast([P, NT, E]), ALU.subtract).then_inc(v_gate, 1)
                for i in range(NT):
                    dve.max_index(idx8[:, i, :], top8[:, i, :], logits[:, i, :]).then_inc(vk.sem, 1)
                    vk.count += 1
                dve.wait_ge(vk.sem, vk.count)
                step(dve.tensor_copy(idxf[:], idx8[:]))
                split_lo(0)
                split_lo(1)
                dve.wait_ge(a_gate, 1)
                step(dve.tensor_reduce(zz[:, 0, :], ex[:], AX.X, ALU.add))
                step(dve.reciprocal(zz[:, 1, :], zz[:, 0, :]))
                for i in range(NT):
                    dve.max(m8[:, i, :], ex[:, i, :]).then_inc(vk.sem, 1)
                    vk.count += 1
                dve.wait_ge(vk.sem, vk.count)
                step(dve.tensor_tensor(zz[:, 2, :], m8[:, :, 1], zz[:, 1, :], ALU.mult))
                dve.tensor_tensor(zz[:, 2, :], zz[:, 2, :], zz[:, 1, :], ALU.subtract).then_inc(v_gate, 1)
                dve.wait_ge(a_gate, 2)
                step(dve.tensor_scalar(zz[:, 3, :], zz[:, 2, :], 1.0, None, ALU.add))
                step(dve.reciprocal(zz[:, 4, :], zz[:, 3, :]))
                step(dve.tensor_tensor(zz[:, 5, :], zz[:, 4, :], zz[:, 2, :], ALU.mult))
                dve.wait_ge(pk.sem, P_CONST)
                for k, (dst, g) in enumerate(((g8, 4), (m8, 5))):
                    step(dve.tensor_tensor(dst[:], iota8[:].unsqueeze(1).to_broadcast([P, NT, E]),
                                           idxf[:, :, k:k + 1].to_broadcast([P, NT, E]), ALU.is_equal))
                    step(dve.tensor_tensor(dst[:], dst[:], zz[:, g, :].unsqueeze(2).to_broadcast([P, NT, E]), ALU.mult))
                step(dve.tensor_tensor(g8[:], g8[:], m8[:], ALU.add))
                for j, e in enumerate(EXPERT_OF):
                    dve.tensor_copy(gate[:, j, :], g8[:, :, e]).then_inc(vk.sem, 1)
                    vk.count += 1
                dve.tensor_scalar(gx[:, :, 0:E], g8[:], -1.0, 1.0, ALU.mult, ALU.add).then_inc(v_gate, 1)
                dve.wait_ge(vk.sem, vk.count)
                for q in range(1, 4):
                    split_gh(q)

                for u in range(NU + 1):
                    j, c = u // NCH, u % NCH
                    if u < NU:
                        for hb in range(HB):
                            v = u * HB + hb
                            dve.wait_ge(a_hhi, v + 1)
                            dve.tensor_tensor(hid[1][:, u % 2, hb * CH:(hb + 1) * CH], hid_f[:, u % 2, hb, :],
                                              hid[0][:, u % 2, hb * CH:(hb + 1) * CH].bitcast(F32), ALU.subtract).then_inc(v_hlo, 1)
                        if c == 1 and 1 <= j and j + 1 < NBLK:
                            split_lo(j + 1)
                    if u >= 1:
                        for tt in range(4):
                            w = u - 1
                            i = (w % NCH) * 4 + tt
                            dve.wait_ge(e_o, 4 * w + tt + 1)
                            src = o_banks[tt][:, 0:L]
                            g = gate[:, w // NCH, i:i + 1]
                            if w < NCH:
                                dve.tensor_scalar(acc[:, i, :], src, g, None, ALU.mult).then_inc(v_acc, 1)
                            else:
                                dve.scalar_tensor_tensor(out=acc[:, i, :], in0=src, scalar=g, in1=acc[:, i, :],
                                                         op0=ALU.mult, op1=ALU.add).then_inc(v_acc, 1)
                    if u == 5 * NCH + 1:
                        dve.wait_ge(a_uhi, 1)
                        dve.tensor_tensor(w_up[1][:], upst[:], w_up[0][:].bitcast(F32), ALU.subtract).then_inc(v_ulo, 1)
                dve.wait_ge(e_m, NEB)
                mb = m_bank[:, 0:LC * NEB].rearrange("p (c j) -> p c j", j=NEB)
                for e in range(E):
                    js = [j for j in range(NEB) if EXPERT_OF[j] == e]
                    dve.tensor_reduce(mT[:, :, e:e + 1], mb[:, :, js[0]:js[-1] + 1], AX.X, ALU.add).then_inc(v_m, 1)
                dve.wait_ge(e_mTT, 1)
                dve.tensor_copy(corr_rhs[0:E, :], h_banks[0][0:E, 0:L]).then_inc(v_mrows, 1)
                for q in range(4):
                    dve.wait_ge(e_gxT, q + 1)
                    dve.tensor_copy(gxT[:, 4 * q:4 * q + 4, :], o_banks[q][0:KX, :].rearrange("p (t n) -> p t n", n=P)).then_inc(v_gxT, 1)
                for i in range(NT):
                    dve.wait_ge(e_corr, i + 1)
                    if i == 0:
                        dve.wait_ge(v_acc, 4 * NU)
                    dve.tensor_tensor(acc[:, i, :], acc[:, i, :], o_banks[i % 4][:, 0:L], ALU.add).then_inc(v_corr, 1)
                for i in range(NT + 1):
                    if i < NT:
                        dve.wait_ge(a_af, i + 1)
                        s = slice((i % 2) * LC * P, (i % 2 + 1) * LC * P)
                        dve.tensor_copy(accT[0][:, s], accT_f[:, i % 2, :]).then_inc(v_ahi, 1)
                        dve.wait_ge(v_ahi, i + 1)
                        dve.tensor_tensor(accT[1][:, s], accT_f[:, i % 2, :], accT[0][:, s].bitcast(F32), ALU.subtract).then_inc(v_alo, 1)
                    if i >= 1:
                        dve.wait_ge(e_up, i)
                        if i == 1:
                            dve.wait_ge(pk.sem, P_RESID + NT)
                        dve.tensor_tensor(resid[:, i - 1, :], resid[:, i - 1, :], o_banks[(i - 1) % 4][:], ALU.add).then_inc(v_up, 1)

            @block.tensor
            def _(pe):
                def terms(lhs, rhs):
                    return ((lhs[0], rhs[0]), (lhs[0], rhs[1]), (lhs[1], rhs[0]))

                def hidden(u):
                    j, c = u // NCH, u % NCH
                    pe.wait_ge(v_wlo, 2 * (j + 1))
                    if j == 0:
                        pe.wait_ge(v_glo, c + 1)
                    n = NB // NCH
                    for hb in range(HB):
                        v = u * HB + hb
                        if v >= 3:
                            pe.wait_ge(a_gelu, v - 2)
                        o = h_banks[v % 3][:]
                        k_terms = []
                        for k in range(LC):
                            ws = [w[:, j % 2, k * BLK + hb * P:k * BLK + (hb + 1) * P] for w in w1]
                            gs = [w[:, c * n:(c + 1) * n, k * SEQ:(k + 1) * SEQ] for w in ghT]
                            k_terms += terms(ws, gs)
                        for i, (l, r) in enumerate(k_terms):
                            mm = pe.matmul(o, l, r, start=i == 0, stop=i == len(k_terms) - 1)
                        mm.then_inc(e_h, 1)

                def project(u):
                    j = u // NCH
                    pe.wait_ge(v_hlo, HB * (u + 1))
                    for tt in range(4):
                        if u >= 1:
                            pe.wait_ge(v_acc, 4 * (u - 1) + tt + 1)
                        k_terms = []
                        for hb in range(HB):
                            hs = [w[:, u % 2, hb * CH + tt * P:hb * CH + (tt + 1) * P] for w in hid]
                            ws = [w[:, j % 2, hb * L:(hb + 1) * L] for w in w2]
                            k_terms += terms(hs, ws)
                        for i, (l, r) in enumerate(k_terms):
                            mm = pe.matmul(o_banks[tt][:, 0:L], l, r, start=i == 0, stop=i == len(k_terms) - 1)
                        mm.then_inc(e_o, 1)

                def zero_image(j):
                    if j == 0:
                        pe.wait_ge(a_b1, 1)
                    for c in range(LC):
                        for hb in range(HB):
                            mm = pe.matmul(m_bank[:, c * NEB + j:c * NEB + j + 1], wst[:, j % 2, 1, hb * L + c * P:hb * L + (c + 1) * P],
                                           gb1_col[:, j * HB + hb:j * HB + hb + 1], start=hb == 0, stop=hb == HB - 1)
                    mm.then_inc(e_m, 1)

                for u in range(NU + 1):
                    if u < NU:
                        hidden(u)
                    if u >= 1:
                        project(u - 1)
                    if u < NU and u % NCH == 1 and u // NCH < NEB:
                        zero_image(u // NCH)
                pe.wait_ge(v_m, E)
                pe.wait_ge(a_gelu, HB * NU)
                for c in range(LC):
                    mm = pe.transpose(h_banks[0][0:E, c * P:(c + 1) * P], mT[:, c, :], ident[:])
                mm.then_inc(e_mTT, 1)
                pe.wait_ge(v_gate, 3)
                pe.wait_ge(v_acc, 4 * NU)
                for q in range(4):
                    for t in range(4):
                        mm = pe.transpose(o_banks[q][0:KX, t * P:(t + 1) * P], gx[:, 4 * q + t, :], ident[:])
                    mm.then_inc(e_gxT, 1)
                pe.wait_ge(v_mrows, 1)
                pe.wait_ge(v_gxT, 4)
                for i in range(NT):
                    if i >= 4:
                        pe.wait_ge(v_corr, i - 3)
                    pe.matmul(o_banks[i % 4][:, 0:L], gxT[:, i, :], corr_rhs[:], start=True, stop=True).then_inc(e_corr, 1)
                for i in range(NT + 1):
                    if i < NT:
                        pe.wait_ge(v_corr, i + 1)
                        if i >= 3:
                            pe.wait_ge(a_af, i - 2)
                        for c in range(LC):
                            mm = pe.transpose(h_banks[i % 3][:, c * P:(c + 1) * P], acc[:, i, c * P:(c + 1) * P], ident[:])
                        mm.then_inc(e_aT, 1)
                    if i >= 1:
                        w = i - 1
                        pe.wait_ge(v_alo, w + 1)
                        if w == 0:
                            pe.wait_ge(v_ulo, 1)
                            pe.wait_ge(v_corr, NT)
                        if w >= 4:
                            pe.wait_ge(v_up, w - 3)
                        k_terms = []
                        for c in range(LC):
                            s = (w % 2) * LC * P + c * P
                            k_terms += terms([t[:, s:s + P] for t in accT], [t[:, c * D:(c + 1) * D] for t in w_up])
                        for k, (l, r) in enumerate(k_terms):
                            mm = pe.matmul(o_banks[w % 4][:], l, r, start=k == 0, stop=k == len(k_terms) - 1)
                        mm.then_inc(e_up, 1)


def kernel(**inputs):
    import numpy as np
    import concourse.bacc as bacc
    from concourse.bass_utils import run_bass_kernel_spmd

    c = {k.removeprefix("L0_"): np.ascontiguousarray(v) for k, v in inputs.items()}
    E = len(HID)
    arrays = {
        "x": c["x"], "cond": c["cond_2048"], "w_emb": c["cond_W_emb"], "b_emb": c["cond_b_emb"],
        "g_norm": c["cond_g_norm"], "w_qkv": c["cond_W_qkv"], "g_q": c["cond_g_q"], "g_k": c["cond_g_k"],
        "w_out": c["cond_W_out"], "down_w": c["ffn_down_w"], "down_b": c["ffn_down_b"], "up_w": c["ffn_up_w"],
        "up_b": c["ffn_up_b"], "router_w": c["ffn_router_w"], "router_b": c["ffn_router_b"],
        "core_w": c["ffn_core_w"], "core_b": c["ffn_core_b"],
        "e_w1": np.concatenate([c[f"ffn_e{e}_w1"] for e in range(E)] + [c["ffn_shared_w1"]], axis=1),
        "e_b1": np.concatenate([c[f"ffn_e{e}_b1"] for e in range(E)] + [c["ffn_shared_b1"]]),
        "e_w2": np.concatenate([c[f"ffn_e{e}_w2"] for e in range(E)] + [c["ffn_shared_w2"]], axis=0),
        "e_b2": np.stack([c[f"ffn_e{e}_b2"] for e in range(E)] + [c["ffn_shared_b2"]]),
    }
    nc = bacc.Bacc("TRN2", target_bir_lowering=False, num_devices=1, dynamic_dma_scratch_size=1024)
    aps = {n: nc.dram_tensor(f"in_{n}", v.shape, mybir.dt.from_np(v.dtype), kind="ExternalInput").ap()
           for n, v in arrays.items()}
    out = nc.dram_tensor("out_0", c["x"].shape, F32, kind="ExternalOutput").ap()
    adaln_moe_program(nc, aps, out)
    r = run_bass_kernel_spmd(nc, [{f"in_{n}": v for n, v in arrays.items()}], core_ids=[0])
    return r.results[0]["out_0"]
```

```python
from contextlib import ExitStack

import concourse.bass as bass
from concourse import mybir

ALU = mybir.AluOpType
ACT = mybir.ActivationFunctionType
AX = mybir.AxisListType
F32 = mybir.dt.float32
F32R = mybir.dt.float32r
BF16 = mybir.dt.bfloat16
I32 = mybir.dt.int32
U32 = mybir.dt.uint32

P = 128
HID = [256, 512, 768, 1024, 256, 512, 768, 1024]
HEADS = 16
EPS = 1e-6
COST_LAMBDA = 1e-7
SHARED_SCALE = 0.1


class Sem:

    def __init__(self, sem):
        self.sem, self.count = sem, 0

    def inc(self, ins, by=1):
        ins.then_inc(self.sem, by)
        self.count += by
        return self.count


def adaln_moe_program(nc, a, out):
    x, cond = a["x"], a["cond"]
    NB, SEQ, D = x.shape
    L = a["down_w"].shape[1]
    E = len(HID)
    NT = NB * SEQ // P
    TB = SEQ // P
    KC = D // P
    LC = L // P
    DH = D // HEADS
    HG = 4
    NG = HEADS // HG
    BLK = 256
    HB = BLK // P
    NBK = [h // BLK for h in HID]
    B0 = [sum(NBK[:e]) for e in range(E + 1)]
    NEB = B0[E]
    MAXB = max(NBK)
    ST = 2 * P
    REGION = NB * SEQ + ST
    MAXT = 2 * NB * SEQ // ST + E
    RING = 9
    CH = 512
    NCH = NB * SEQ // CH
    VW = DH + 1
    QW = 4 * DH
    assert SEQ == 256 and D == 512 and L == 256 and DH == 32 and TB == 2

    xt_dram = x.rearrange("b (t p) d -> p (b t) d", p=P)
    out_dram = out.rearrange("b (t p) d -> p (b t) d", p=P)
    slots_dram = nc.dram_tensor("slots_scratch", [E * REGION, L], F32).ap()
    y_dram = nc.dram_tensor("y_scratch", [(MAXT + 1) * ST, L], F32).ap()
    ght_dram = nc.dram_tensor("ght_scratch", [P, NB, LC * SEQ], F32).ap()

    with ExitStack() as top:
        def sbt(name, shape, dt=F32, ctx=top):
            return ctx.enter_context(nc.sbuf_tensor(name, shape, dt))

        def sem(name):
            return top.enter_context(nc.semaphore(name))

        bank = {n: top.enter_context(nc.psum_tensor("ps_" + n, [P, 512], F32))
                for n in ("mm", "t0", "t1", "s0", "s1", "a0", "a1", "pv")}
        b_t, b_s, b_a = (bank["t0"], bank["t1"]), (bank["s0"], bank["s1"]), (bank["a0"], bank["a1"])
        b_mm, b_pv = bank["mm"], bank["pv"]

        resid = sbt("resid", [P, NT, D])
        ident = sbt("ident", [P, P])
        logits = sbt("logits", [P, NT, E])
        onehot = sbt("onehot", [P, 2, NT, E])
        slotf = sbt("slotf", [P, 2, NT])
        counts = sbt("counts", [P, E])
        region0 = sbt("region0", [P, E])
        iota_e = sbt("iota_e", [P, E + 1])
        slot_idx = sbt("slot_idx", [P, 2, NT], U32)

        with ExitStack() as ph:
            def sb(name, shape, dt=F32):
                return sbt(name, shape, dt, ph)

            def pair(name, shape):
                return sb(name + "_hi", shape, F32R), sb(name + "_lo", shape, F32R)

            w_qkv = pair("w_qkv", [P, KC, 3 * D])
            w_out = pair("w_out", [P, KC, D])
            w_core = pair("w_core", [P, KC, D])
            w_down = pair("w_down", [P, KC, L])
            w_router = sb("w_router", [P, KC, E])
            xs = sb("xs", [P, KC * SEQ])
            xt = pair("xt", [P, KC, SEQ])
            qkraw = sb("qkraw", [P, 4, D])
            sq = sb("sq", [P, 2, D])
            q_tok = sb("q_tok", [P, TB, HEADS, QW], F32R)
            k_tok = sb("k_tok", [P, TB, HEADS, QW], F32R)
            stacks = sb("stacks", [P, 8, 512], F32R)
            att = sb("att", [P, 4, 512])
            v_tok = sb("v_tok", [P, TB, HEADS, VW])
            o_tok = xs[:].rearrange("p (t d) -> p t d", d=D)
            gh_tok = sb("gh_tok", [P, TB, L])
            before = sb("before", [P, P], BF16)
            ones = sb("ones", [P, P], BF16)
            chosen = sb("chosen", [P, TB, E], BF16)
            chosen_sum = sb("chosen_sum", [P, TB + 1, E], BF16)
            top8 = sb("top8", [P, TB, 8])
            idx8 = sb("idx8", [P, TB, 8], U32)
            idxf = sb("idxf", [P, TB, 8])
            rank = sb("rank", [P, TB, E])
            picked = sb("picked", [P, 2, TB, E])
            ght = sq[:, 1, :]
            negmax_row = sb("negmax_row", [P, 2, SEQ], F32R)
            rowmax = sb("rowmax", [P, 2, TB, HG])
            sel = sb("sel", [P, HG, P], F32R)
            rden = sb("rden", [P, TB, HG])
            ss = sb("ss", [P, 4, HEADS])
            rs = sb("rs", [P, 4, HEADS])
            rs_b = sb("rs_b", [P, 4 * HEADS])
            ssx = sb("ssx", [P, NT])
            rx = sb("rx", [P, NT])
            cond_row = sb("cond_row", [NB, D])
            condT = sb("condT", [P, KC, NB])
            bemb_col = sb("bemb_col", [P, 2 * KC])
            gnorm_col = sb("gnorm_col", [P, KC])
            aff_scale = sb("aff_scale", [P, KC, NB])
            aff_shift = sb("aff_shift", [P, KC, NB])
            gqk = sb("gqk", [P, DH])
            gk_b = sb("gk_b", [P, DH])
            down_bias = sb("down_bias", [P, L])
            router_bias = sb("router_bias", [P, E])

            oT = stacks[:, 0:2, :], stacks[:, 2:4, :]
            yT = stacks[:, 4:6, :], stacks[:, 6:8, :]
            gyT = oT
            o_f, y_f = att[:, 0:2, :], att[:, 2:4, :]
            gy_f = o_f
            stage = att[:].rearrange("p a b -> p (a b)"), qkraw[:].rearrange("p a b -> p (a b)")

            def quarter(n, part):
                w = (q_tok, k_tok)[n % 2][:, n // 2, :, :]
                if n % 2 == 0:
                    return w.rearrange("p h (r l d) -> p h r l d", l=2, d=DH)[:, :, :, part, :]
                return w.rearrange("p h (l r d) -> p h l r d", l=2, d=DH)[:, :, part, :, :]

            def twice(n):
                return qkraw[:, n, :].rearrange("p (h d) -> p h d", d=DH).unsqueeze(2).to_broadcast([P, HEADS, 2, DH])

            d_x = [sem(f"d_x{b}") for b in range(NB)]
            d_small, d_wemb = sem("d_small"), [sem("d_wemb0"), sem("d_wemb1")]
            d_w = [sem("d_w0"), sem("d_w1")]
            d_ght = sem("d_ght")
            p_const = sem("p_const")
            pc = Sem(p_const)
            v_step, v_wsplit, a_wsplit = Sem(sem("v_step")), Sem(sem("v_wsplit")), Sem(sem("a_wsplit"))
            a_ssx = sem("a_ssx")
            e_condT, e_ada = sem("e_condT"), sem("e_ada")
            v_condT, v_ada = sem("v_condT"), sem("v_ada")
            v_xs, e_xT, a_xaff, v_xT = sem("v_xs"), sem("e_xT"), sem("a_xaff"), sem("v_xT")
            e_qkv, a_mm = sem("e_qkv"), sem("a_mm")
            p_sq, p_gq, v_ss = sem("p_sq"), sem("p_gq"), sem("v_ss")
            v_qn, a_qhi, v_qlo = sem("v_qn"), sem("a_qhi"), sem("v_qlo")
            e_T, a_evT, v_evT = sem("e_T"), sem("a_evT"), sem("v_evT")
            e_S, v_max, e_mT, v_mrow = sem("e_S"), sem("v_max"), sem("e_mT"), sem("v_mrow")
            e_ST, a_exp, e_PV, v_rden, v_norm = sem("e_ST"), sem("a_exp"), sem("e_PV"), sem("v_rden"), sem("v_norm")
            e_oT, a_of, v_oT = sem("e_oT"), sem("a_of"), sem("v_oT")
            e_yT, v_y, a_yhi, v_ylo, a_gy, a_gyhi, v_gylo = (
                sem("e_yT"), sem("v_y"), sem("a_yhi"), sem("v_ylo"), sem("a_gy"), sem("a_gyhi"), sem("v_gylo"))
            e_down, v_h, a_gh, e_router, v_logits = sem("e_down"), sem("v_h"), sem("a_gh"), sem("e_router"), sem("v_logits")
            v_chosen, e_rank, v_slot, d_slots, d_yzero = sem("v_chosen"), sem("e_rank"), sem("v_slot"), sem("d_slots"), sem("d_yzero")
            e_count = sem("e_count")
            e_core, v_core, e_ghT, a_ghT = sem("e_core"), sem("v_core"), sem("e_ghT"), sem("a_ghT")

            parts = []
            wq_dram = a["w_qkv"].rearrange("(c p) n -> p c n", p=P)
            for c in range(KC):
                parts.append((wq_dram[:, c, :], [w[:, c, :] for w in w_qkv], 3 * D))
            for w, name in ((w_out, "w_out"), (w_core, "core_w"), (w_down, "down_w")):
                n = a[name].shape[1]
                dram = a[name].rearrange("(c p) n -> p c n", p=P)
                parts.append((dram, [t[:].rearrange("p c n -> p (c n)") for t in w], KC * n))
            NPART = len(parts)
            W_QKV_PARTS, W_OUT_PARTS, W_CORE_PARTS, W_DOWN_PARTS = KC, KC + 1, KC + 2, KC + 3
            block = ph.enter_context(nc.Block())

            @block.sync
            def _(sp):
                sp.dma_start(cond_row[:], cond).then_inc(d_small, 16)
                sp.dma_start(resid[:, 0:TB, :], xt_dram[:, 0:TB, :]).then_inc(d_x[0], 16)
                with nc.allow_non_contiguous_dma(reason="columns of biases and gains"):
                    sp.dma_start(bemb_col[:], a["b_emb"].rearrange("(c p) -> p c", p=P)).then_inc(d_small, 16)
                    sp.dma_start(gnorm_col[:], a["g_norm"].rearrange("(c p) -> p c", p=P)).then_inc(d_small, 16)
                    sp.dma_start(w_router[:], a["router_w"].rearrange("(c p) n -> p c n", p=P)).then_inc(d_small, 16)
                    sp.dma_start(gqk[:], a["g_q"].partition_broadcast(P)).then_inc(d_small, 16)
                    sp.dma_start(gk_b[:], a["g_k"].partition_broadcast(P)).then_inc(d_small, 16)
                    sp.dma_start(down_bias[:], a["down_b"].partition_broadcast(P)).then_inc(d_small, 16)
                    sp.dma_start(router_bias[:], a["router_b"].partition_broadcast(P)).then_inc(d_small, 16)
                for c in range(KC):
                    if c >= 2:
                        sp.wait_ge(e_ada, c - 1)
                    sp.dma_start(stage[c % 2][:, 0:2 * D],
                                 a["w_emb"].rearrange("(c p) n -> p c n", p=P)[:, c, :]).then_inc(d_wemb[c % 2], 16)
                for b in range(1, NB):
                    sp.dma_start(resid[:, b * TB:(b + 1) * TB, :], xt_dram[:, b * TB:(b + 1) * TB, :]).then_inc(d_x[b], 16)
                for n, (src, _, size) in enumerate(parts):
                    sp.wait_ge(e_ada, 3 + n % 2 if n < 2 else 4)
                    if n >= 2:
                        sp.wait_ge(v_wsplit.sem, n - 1)
                    dst = stage[n % 2][:, 0:size]
                    if len(src.shape) == 3:
                        dst = dst.rearrange("p (c n) -> p c n", c=KC)
                    sp.dma_start(dst, src).then_inc(d_w[n % 2], 16)
                sp.wait_ge(p_const, 5)
                sp.dma_start(y_dram.rearrange("(n p) d -> p n d", p=P),
                             gh_tok[:, 0, :].unsqueeze(1).to_broadcast([P, (MAXT + 1) * ST // P, L])).then_inc(d_yzero, 16)
                for b in range(NB):
                    sp.wait_ge(a_ghT, b + 1)
                    sp.dma_start(ght_dram[:, b, :], ght).then_inc(d_ght, 16)
                sp.wait_ge(d_ght, 16 * NB)
                sp.wait_ge(d_yzero, 16)

            SMALL = 8
            P_CONSTS = 9

            @block.gpsimd
            def _(pool):
                pc.inc(pool.memset(ident[:], 0.0))
                pool.wait_ge(p_const, 1)
                pc.inc(pool.affine_select(out=ident[:], in_=ident[:], compare_op=ALU.not_equal, fill=1.0,
                                          base=0, pattern=[[-1, P]], channel_multiplier=1))
                pc.inc(pool.memset(v_tok[:, :, :, DH:VW], 1.0))
                pc.inc(pool.memset(negmax_row[:].bitcast(F32), 0.0))
                pc.inc(pool.memset(gh_tok[:], 0.0))
                pc.inc(pool.memset(ones[:], 1.0))
                pool.wait_ge(p_const, 6)
                pc.inc(pool.affine_select(out=before[:], in_=ones[:], compare_op=ALU.is_gt, fill=0.0,
                                          base=0, pattern=[[1, P]], channel_multiplier=-1))
                pc.inc(pool.iota(iota_e[:], pattern=[[1, E + 1]], base=0, channel_multiplier=0,
                                 allow_small_or_imprecise_dtypes=True))
                pc.inc(pool.memset(chosen_sum[:, 0, :], 0.0))
                assert pc.count == P_CONSTS

                def scatter(b):
                    pool.wait_ge(v_slot, b + 1)
                    for t in range(TB):
                        for k in range(2):
                            i = b * TB + t
                            pool.indirect_dma_start(
                                out=slots_dram, out_offset=bass.IndirectOffsetOnAxis(ap=slot_idx[:, k, i:i + 1], axis=0),
                                in_=gh_tok[:, t, :], in_offset=None, bounds_check=E * REGION - 1,
                                oob_is_err=True).then_inc(d_slots, 16)

                g_b = gqk[:].unsqueeze(1).to_broadcast([P, HEADS, DH])
                for b in range(NB):
                    for n in range(4):
                        pool.wait_ge(a_mm, 6 * b + n + 1)
                        if 4 * b + n >= 2:
                            pool.wait_ge(v_ss, 4 * b + n - 1)
                        if n == 1 and b >= 2:
                            pool.wait_ge(d_ght, 16 * (b - 1))
                        pool.tensor_tensor(sq[:, n % 2, :], qkraw[:, n, :], qkraw[:, n, :], ALU.mult).then_inc(p_sq, 1)
                        if n % 2 == 0:
                            if n == 0 and b == 0:
                                pool.wait_ge(v_ada, 2)
                            pool.wait_ge(p_sq, 4 * b + n + 1)
                            q = qkraw[:, n, :].rearrange("p (h d) -> p h d", d=DH)
                            pool.tensor_tensor(q, q, g_b, ALU.mult).then_inc(p_gq, 1)
                        if n == 1 and b >= 2:
                            scatter(b - 2)
                for b in range(NB - 2, NB):
                    scatter(b)
                pool.wait_ge(d_slots, 16 * 2 * NT)

            @block.scalar
            def _(act):
                def row_squares(b):
                    act.wait_ge(d_x[b], 16)
                    for t in range(TB):
                        i = b * TB + t
                        unused = (q_tok, k_tok)[i // 8][:].rearrange("p t h w -> p (t h w)")[:, (i % 8) * D:(i % 8 + 1) * D]
                        act.activation(unused, resid[:, i, :], ACT.Square,
                                       accum_out=ssx[:, i:i + 1]).then_inc(a_ssx, 1)

                def split_hi(n):
                    act.wait_ge(d_w[n % 2], 16 * (n // 2 + 1))
                    _, (hi, _), size = parts[n]
                    a_wsplit.inc(act.activation(hi, stage[n % 2][:, 0:size], ACT.Copy))

                def x_affine(b):
                    for c in range(KC):
                        src = (b_t[1], b_a[1])[c // 2][:, (c % 2) * SEQ:(c % 2 + 1) * SEQ]
                        if c % 2 == 0:
                            act.wait_ge(e_xT, 2 * b + c // 2 + 1)
                        if c == 0:
                            act.wait_ge(e_xT, 2 * b + 2)
                        act.activation(xs[:, c * SEQ:(c + 1) * SEQ], src, ACT.Identity,
                                       bias=aff_shift[:, c, b:b + 1], scale=aff_scale[:, c, b:b + 1]).then_inc(a_xaff, 1)

                def copy_chunk(b, n):
                    act.wait_ge(e_qkv, 6 * b + n + 1)
                    if n < 4:
                        act.activation(qkraw[:, n, :], b_mm[:], ACT.Copy).then_inc(a_mm, 1)
                    else:
                        act.activation(v_tok[:, n - 4, :, 0:DH], b_mm[:].rearrange("p (h d) -> p h d", d=DH),
                                       ACT.Copy).then_inc(a_mm, 1)

                def q_hi(b):
                    for n in range(4):
                        act.wait_ge(v_qn, 4 * b + n + 1)
                        act.activation(quarter(n, 0), twice(n), ACT.Copy).then_inc(a_qhi, 1)

                def ev_T(b, h):
                    act.wait_ge(e_T, HEADS * b + h + 1)
                    act.activation(stacks[:, h % 8, :], b_t[h % 2][:], ACT.Copy).then_inc(a_evT, 1)

                def exp(b, h):
                    act.wait_ge(e_ST, HEADS * b + h + 1)
                    act.activation(att[:, h % 4, :], b_a[h % 2][:], ACT.Exp).then_inc(a_exp, 1)

                row_squares(0)
                act.wait_ge(v_ada, 1)
                x_affine(0)
                for n in range(W_QKV_PARTS):
                    split_hi(n)
                for b in range(1, NB):
                    row_squares(b)
                for n in range(W_QKV_PARTS, NPART):
                    split_hi(n)
                for n in range(4):
                    if n == 0:
                        act.wait_ge(v_wsplit.sem, NPART)
                    copy_chunk(0, n)
                q_hi(0)
                for n in (4, 5):
                    if n == 4:
                        act.wait_ge(p_const, 3)
                    copy_chunk(0, n)
                x_affine(1)

                for b in range(NB):
                    for g in range(NG + 1):
                        for j in range(HG):
                            h = HG * g + j
                            if g < NG and h % 2 == 0:
                                ev_T(b, h)
                            if g >= 1:
                                exp(b, h - HG)
                        if g < NG and b + 1 < NB:
                            copy_chunk(b + 1, g)
                    for i in range(2):
                        act.wait_ge(e_oT, 2 * b + i + 1)
                        act.activation(o_f[:, i, :], b_t[i][:], ACT.Copy).then_inc(a_of, 1)
                    if b + 1 < NB:
                        copy_chunk(b + 1, 4)
                        q_hi(b + 1)
                    for i in range(2):
                        act.wait_ge(v_y, 2 * b + i + 1)
                        act.activation(yT[0][:, i, :], y_f[:, i, :], ACT.Copy).then_inc(a_yhi, 1)
                    for i in range(2):
                        act.activation(gy_f[:, i, :], y_f[:, i, :], ACT.Gelu).then_inc(a_gy, 1)
                    if b + 1 < NB:
                        copy_chunk(b + 1, 5)
                    for i in range(2):
                        act.wait_ge(a_gy, 2 * b + i + 1)
                        act.activation(gyT[0][:, i, :], gy_f[:, i, :], ACT.Copy).then_inc(a_gyhi, 1)
                    if b + 2 < NB:
                        x_affine(b + 2)
                    for t in range(TB):
                        act.wait_ge(v_h, 2 * b + t + 1)
                        act.activation(gh_tok[:, t, :], gh_tok[:, t, :], ACT.Gelu).then_inc(a_gh, 1)
                    act.wait_ge(e_ghT, b + 1)
                    if b >= 1:
                        act.wait_ge(d_ght, 16 * b)
                    act.activation(ght, b_t[0][:], ACT.Copy).then_inc(a_ghT, 1)

            @block.vector
            def _(dve):
                def step(ins):
                    dve.wait_ge(v_step.sem, v_step.inc(ins))

                def rsqrt(dst, tmp, src, mean_over):
                    step(dve.tensor_scalar(src, src, 1.0 / mean_over, EPS, ALU.mult, ALU.add))
                    step(dve.tensor_single_scalar(tmp.bitcast(I32), src.bitcast(I32), 1, ALU.logical_shift_right))
                    step(dve.tensor_scalar(dst.bitcast(I32), tmp.bitcast(I32), -1, 0x5F3759DF, ALU.mult, ALU.add))
                    for _ in range(3):
                        step(dve.tensor_tensor(tmp, dst, dst, ALU.mult))
                        step(dve.scalar_tensor_tensor(out=tmp, in0=tmp, scalar=-0.5, in1=src, op0=ALU.mult, op1=ALU.mult))
                        step(dve.scalar_tensor_tensor(out=dst, in0=tmp, scalar=1.5, in1=dst, op0=ALU.add, op1=ALU.mult))

                def split_lo(n):
                    dve.wait_ge(a_wsplit.sem, n + 1)
                    _, (hi, lo), size = parts[n]
                    v_wsplit.inc(dve.tensor_tensor(lo, stage[n % 2][:, 0:size], hi.bitcast(F32), ALU.subtract))

                def scale_x(b):
                    for t in range(TB):
                        i = b * TB + t
                        dve.tensor_scalar(xs[:, t * D:(t + 1) * D], resid[:, i, :], rx[:, i:i + 1], None,
                                          ALU.mult).then_inc(v_xs, 1)

                def split_x(b):
                    dve.wait_ge(a_xaff, KC * (b + 1))
                    hi, lo = (w[:].rearrange("p c s -> p (c s)") for w in xt)
                    dve.tensor_copy(hi, xs[:]).then_inc(v_xT, 1)
                    dve.wait_ge(v_xT, 2 * b + 1)
                    dve.tensor_tensor(lo, xs[:], hi.bitcast(F32), ALU.subtract).then_inc(v_xT, 1)

                def sum_squares(b, n):
                    dve.wait_ge(p_sq, 4 * b + n + 1)
                    dve.tensor_reduce(ss[:, n, :], sq[:, n % 2, :].rearrange("p (h d) -> p h d", d=DH),
                                      AX.X, ALU.add).then_inc(v_ss, 1)

                def normalise_qk(b):
                    dve.wait_ge(v_ss, 4 * (b + 1))
                    flat = lambda t: t[:].rearrange("p n h -> p (n h)")
                    rsqrt(flat(rs), rs_b[:], flat(ss), DH)
                    dve.wait_ge(p_gq, 2 * (b + 1))
                    for n in range(4):
                        q = qkraw[:, n, :].rearrange("p (h d) -> p h d", d=DH)
                        dve.tensor_tensor(q, q, rs[:, n, :].unsqueeze(2).to_broadcast([P, HEADS, DH]),
                                          ALU.mult).then_inc(v_qn, 1)
                    for n in range(4):
                        dve.wait_ge(a_qhi, 4 * b + n + 1)
                        dve.tensor_tensor(quarter(n, 1), twice(n), quarter(n, 0).bitcast(F32), ALU.subtract).then_inc(v_qlo, 1)

                def choose(b):
                    tiles = slice(b * TB, (b + 1) * TB)
                    dve.wait_ge(v_logits, b + 1)
                    for t in range(TB):
                        ins = dve.max(top8[:, t, :], logits[:, b * TB + t, :])
                        v_step.inc(ins)
                    dve.wait_ge(v_step.sem, v_step.count)
                    for t in range(TB):
                        v_step.inc(dve.max_index(idx8[:, t, :], top8[:, t, :], logits[:, b * TB + t, :]))
                    dve.wait_ge(v_step.sem, v_step.count)
                    step(dve.tensor_copy(idxf[:], idx8[:]))
                    if b >= 1:
                        step(dve.tensor_copy(chosen_sum[:, 0, :], chosen_sum[:, TB, :]))
                    for k in range(2):
                        v_step.inc(dve.tensor_tensor(onehot[:, k, tiles, :], iota_e[:, 0:E].unsqueeze(1).to_broadcast([P, TB, E]),
                                                     idxf[:, :, k:k + 1].to_broadcast([P, TB, E]), ALU.is_equal))
                    dve.wait_ge(v_step.sem, v_step.count)
                    step(dve.tensor_tensor(chosen[:], onehot[:, 0, tiles, :], onehot[:, 1, tiles, :], ALU.add))
                    for t in range(TB):
                        ins = dve.tensor_tensor(chosen_sum[:, t + 1, :], chosen_sum[:, t, :], chosen[:, t, :], ALU.add)
                        if t < TB - 1:
                            step(ins)
                    ins.then_inc(v_chosen, 1)

                def place(b):
                    dve.wait_ge(e_rank, b + 1)
                    step(dve.tensor_tensor(rank[:], b_pv[:, 0:TB * E].rearrange("p (t e) -> p t e", e=E),
                                           region0[:].unsqueeze(1).to_broadcast([P, TB, E]), ALU.add))
                    tiles = slice(b * TB, (b + 1) * TB)
                    for k in range(2):
                        v_step.inc(dve.tensor_tensor(picked[:, k, :, :], onehot[:, k, tiles, :], rank[:], ALU.mult))
                    dve.wait_ge(v_step.sem, v_step.count)
                    step(dve.tensor_reduce(slotf[:, :, tiles], picked[:], AX.X, ALU.add))
                    dve.tensor_copy(slot_idx[:, :, tiles], slotf[:, :, tiles]).then_inc(v_slot, 1)

                def norm(b, g):
                    dve.wait_ge(e_PV, NG * b + g + 1)
                    pv = b_pv[:, 0:TB * HG * VW].rearrange("p (t j w) -> p t j w", t=TB, w=VW)
                    dve.reciprocal(rden[:], pv[:, :, :, DH]).then_inc(v_rden, 1)
                    dve.wait_ge(v_rden, NG * b + g + 1)
                    for t in range(TB):
                        o = o_tok[:, t, g * HG * DH:(g + 1) * HG * DH].rearrange("p (j d) -> p j d", d=DH)
                        dve.tensor_tensor(o, pv[:, t, :, 0:DH], rden[:, t, :].unsqueeze(2).to_broadcast([P, HG, DH]),
                                          ALU.mult).then_inc(v_norm, 1)

                def row_max(b, h):
                    dve.wait_ge(e_S, HEADS * b + h + 1)
                    dve.tensor_reduce(rowmax[:, (h // HG) % 2, :, h % HG], b_s[h % 2][:].rearrange("p (t k) -> p t k", t=TB),
                                      AX.X, ALU.max).then_inc(v_max, 1)

                dve.wait_ge(e_condT, 1)
                dve.tensor_copy(condT[:], b_s[0][:, 0:KC * NB].rearrange("p (c b) -> p c b", b=NB)).then_inc(v_condT, 1)
                dve.wait_ge(a_ssx, TB)
                rsqrt(rx[:, 0:TB], rs_b[:, 0:TB], ssx[:, 0:TB], D)
                scale_x(0)
                dve.wait_ge(d_small, 16 * SMALL)
                dve.wait_ge(e_ada, KC)
                step(dve.tensor_copy(rs_b[:], b_s[1][:, 0:64]))
                for c in range(1, KC):
                    step(dve.tensor_tensor(rs_b[:], rs_b[:], b_s[1][:, c * 64:(c + 1) * 64], ALU.add))
                ada = rs_b[:].rearrange("p (f b) -> p f b", b=NB)
                step(dve.tensor_tensor(aff_shift[:], ada[:, KC:, :], bemb_col[:, KC:].unsqueeze(2).to_broadcast([P, KC, NB]), ALU.add))
                step(dve.tensor_tensor(aff_scale[:], ada[:, 0:KC, :], bemb_col[:, 0:KC].unsqueeze(2).to_broadcast([P, KC, NB]), ALU.add))
                gn = gnorm_col[:].unsqueeze(2).to_broadcast([P, KC, NB])
                dve.scalar_tensor_tensor(out=aff_scale[:], in0=aff_scale[:], scalar=1.0, in1=gn,
                                         op0=ALU.add, op1=ALU.mult).then_inc(v_ada, 1)
                dve.scalar_tensor_tensor(out=gqk[:], in0=gqk[:], scalar=float(DH) ** -0.5, in1=gk_b[:],
                                         op0=ALU.mult, op1=ALU.mult).then_inc(v_ada, 1)
                for e, hid in enumerate(HID):
                    step(dve.tensor_scalar(router_bias[:, e:e + 1], router_bias[:, e:e + 1],
                                           -COST_LAMBDA * 2 * L * hid, None, ALU.add))
                dve.wait_ge(p_const, P_CONSTS)
                step(dve.tensor_scalar(region0[:], iota_e[:, 0:E], float(REGION), None, ALU.mult))
                step(dve.tensor_copy(sel[:], ident[:, 0:HG].unsqueeze(2).to_broadcast([P, HG, P])))
                split_x(0)
                for n in range(W_QKV_PARTS):
                    split_lo(n)
                dve.wait_ge(a_ssx, NT)
                rsqrt(rx[:, TB:NT], rs_b[:, 0:NT - TB], ssx[:, TB:NT], D)
                for n in range(W_QKV_PARTS, NPART):
                    split_lo(n)
                for n in range(4):
                    sum_squares(0, n)
                scale_x(1)
                normalise_qk(0)
                split_x(1)

                for b in range(NB):
                    for g in range(NG + 1):
                        for j in range(HG):
                            h = HG * g + j
                            if g < NG:
                                if h % 2 == 1:
                                    dve.wait_ge(e_T, HEADS * b + h + 1)
                                    dve.tensor_copy(stacks[:, h % 8, :], b_t[1][:]).then_inc(v_evT, 1)
                                if j >= 1:
                                    row_max(b, h - 1)
                        if g < NG:
                            row_max(b, HG * g + HG - 1)
                            dve.wait_ge(e_mT, NG * b + g + 1)
                            dve.tensor_scalar(negmax_row[0:HG, g % 2, :], b_t[0][0:HG, 0:SEQ], -1.0, None,
                                              ALU.mult).then_inc(v_mrow, 1)
                        if g == 0 and b >= 1:
                            place(b - 1)
                        if g >= 1:
                            norm(b, g - 1)
                        if g < NG and b + 1 < NB:
                            sum_squares(b + 1, g)
                    for i in range(2):
                        dve.wait_ge(a_of, 2 * b + i + 1)
                        dve.tensor_copy(oT[0][:, i, :], o_f[:, i, :]).then_inc(v_oT, 1)
                        dve.wait_ge(v_oT, 4 * b + 2 * i + 1)
                        dve.tensor_tensor(oT[1][:, i, :], o_f[:, i, :], oT[0][:, i, :].bitcast(F32), ALU.subtract).then_inc(v_oT, 1)
                    if b + 2 < NB:
                        scale_x(b + 2)
                    if b + 1 < NB:
                        normalise_qk(b + 1)
                    for i in range(2):
                        dve.wait_ge(e_yT, 2 * b + i + 1)
                        dve.tensor_tensor(y_f[:, i, :], b_s[i][:], o_f[:, i, :], ALU.add).then_inc(v_y, 1)
                    for i in range(2):
                        dve.wait_ge(a_yhi, 2 * b + i + 1)
                        dve.tensor_tensor(yT[1][:, i, :], y_f[:, i, :], yT[0][:, i, :].bitcast(F32), ALU.subtract).then_inc(v_ylo, 1)
                    for i in range(2):
                        dve.wait_ge(a_gyhi, 2 * b + i + 1)
                        dve.tensor_tensor(gyT[1][:, i, :], gy_f[:, i, :], gyT[0][:, i, :].bitcast(F32), ALU.subtract).then_inc(v_gylo, 1)
                    for t in range(TB):
                        dve.wait_ge(e_down, TB * (b + 1))
                        if b >= 1:
                            dve.wait_ge(d_slots, 64 * b)
                        else:
                            dve.wait_ge(d_yzero, 16)
                        dve.tensor_tensor(gh_tok[:, t, :], b_a[0][:, t * L:(t + 1) * L], down_bias[:], ALU.add).then_inc(v_h, 1)
                    dve.wait_ge(e_router, b + 1)
                    dve.tensor_tensor(logits[:, b * TB:(b + 1) * TB, :], b_pv[:, 0:TB * E].rearrange("p (t e) -> p t e", e=E),
                                      router_bias[:].unsqueeze(1).to_broadcast([P, TB, E]), ALU.add).then_inc(v_logits, 1)
                    if b + 2 < NB:
                        split_x(b + 2)
                    for t in range(TB):
                        dve.wait_ge(e_core, TB * b + t + 1)
                        dve.tensor_tensor(resid[:, b * TB + t, :], resid[:, b * TB + t, :], b_s[t][:], ALU.add).then_inc(v_core, 1)
                    choose(b)
                place(NB - 1)
                dve.wait_ge(e_count, 1)
                step(dve.tensor_copy(counts[:], b_s[0][:, 0:E]))

            @block.tensor
            def _(pe):
                def three(out_ap, lhs, rhs, first, last):
                    pe.matmul(out_ap, lhs[0], rhs[0], start=first, stop=False)
                    pe.matmul(out_ap, lhs[0], rhs[1], start=False, stop=False)
                    return pe.matmul(out_ap, lhs[1], rhs[0], start=False, stop=last)

                def x_T(b):
                    pe.wait_ge(v_xs, TB * (b + 1))
                    if b >= 2:
                        pe.wait_ge(a_of, 2 * (b - 2) + 2)
                    for half in range(2):
                        if half == 1 and b >= 2:
                            pe.wait_ge(a_exp, HEADS * (b - 1))
                        for c in (2 * half, 2 * half + 1):
                            for t in range(TB):
                                mm = pe.transpose((b_t[1], b_a[1])[half][:, (c % 2) * SEQ + t * P:(c % 2) * SEQ + (t + 1) * P],
                                                  xs[:, t * D + c * P:t * D + (c + 1) * P], ident[:])
                        mm.then_inc(e_xT, 1)

                CHUNKS = [(0, 0), (0, 1), (1, 0), (1, 1), (0, 2), (1, 2)]

                def qkv(b, n, c):
                    t, part = CHUNKS[n]
                    if c == 0:
                        if n == 0:
                            pe.wait_ge(v_xT, 2 * (b + 1))
                        if 6 * b + n >= 1:
                            pe.wait_ge(a_mm, 6 * b + n)
                    if b == 0 and n == 0:
                        pe.wait_ge(v_wsplit.sem, c + 1)
                    mm = three(b_mm[:], [w[:, c, t * P:(t + 1) * P] for w in xt],
                               [w[:, c, part * D:(part + 1) * D] for w in w_qkv], c == 0, c == KC - 1)
                    if c == KC - 1:
                        mm.then_inc(e_qkv, 1)

                def stack_T(b, h):
                    if h == 0:
                        pe.wait_ge(v_qlo, 4 * (b + 1))
                        if b >= 1:
                            pe.wait_ge(a_ghT, b)
                    if h == 1:
                        pe.wait_ge(a_xaff, KC * min(b + 2, NB))
                    if h >= 2:
                        if h % 2 == 0:
                            pe.wait_ge(a_evT, 8 * b + h // 2)
                        else:
                            pe.wait_ge(v_evT, 8 * b + h // 2)
                    if h % HG == 0 and h > 0:
                        pe.wait_ge(v_mrow, NG * b + h // HG)
                    for half, src in ((0, q_tok), (1, k_tok)):
                        for t in range(TB):
                            w = src[:, t, h, :].bitcast(F32)
                            o = (half * TB + t) * P
                            mm = pe.transpose(b_t[h % 2][:, o:o + P], w, ident[:])
                    mm.then_inc(e_T, 1)

                def scores(b, h):
                    if h % 2 == 0:
                        pe.wait_ge(a_evT, 8 * b + h // 2 + 1)
                    else:
                        pe.wait_ge(v_evT, 8 * b + h // 2 + 1)
                    if h >= 2:
                        pe.wait_ge(v_max, HEADS * b + h - 1)
                    elif b >= 1:
                        pe.wait_ge(v_core, TB * b)
                    st = stacks[:, h % 8, :]
                    for t in range(TB):
                        mm = pe.matmul(b_s[h % 2][:, t * SEQ:(t + 1) * SEQ], st[:, t * P:(t + 1) * P], st[:, SEQ:2 * SEQ],
                                       start=True, stop=True)
                    mm.then_inc(e_S, 1)

                def max_T(b, g):
                    pe.wait_ge(v_max, HEADS * b + HG * (g + 1))
                    pe.wait_ge(a_evT, 8 * b + 2 * (g + 1))
                    for t in range(TB):
                        mm = pe.transpose(b_t[0][0:HG, t * P:(t + 1) * P], rowmax[:, g % 2, t, :], ident[:])
                    mm.then_inc(e_mT, 1)

                def scores_T(b, h):
                    g, j = h // HG, h % HG
                    if j == 0:
                        pe.wait_ge(v_mrow, NG * b + g + 1)
                    if h >= 2:
                        pe.wait_ge(a_exp, HEADS * b + h - 1)
                    else:
                        if b >= 1:
                            pe.wait_ge(v_h, TB * b)
                        pe.wait_ge(a_xaff, KC * min(b + 2, NB))
                    st = stacks[:, h % 8, :]
                    for k in range(TB):
                        o = b_a[h % 2][:, k * SEQ:(k + 1) * SEQ]
                        pe.matmul(o, st[:, SEQ + k * P:SEQ + (k + 1) * P], st[:, 0:SEQ], start=True, stop=False)
                        mm = pe.matmul(o, sel[:, j, :], negmax_row[:, g % 2, :], start=False, stop=True)
                    mm.then_inc(e_ST, 1)

                def ranks(b):
                    pe.wait_ge(v_chosen, b + 1)
                    for t in range(TB):
                        o = b_pv[:, t * E:(t + 1) * E]
                        pe.matmul(o, before[:], chosen[:, t, :], start=True, stop=False)
                        mm = pe.matmul(o, ones[:], chosen_sum[:, t, :], start=False, stop=True)
                    mm.then_inc(e_rank, 1)

                def values(b, h):
                    g, j = h // HG, h % HG
                    pe.wait_ge(a_exp, HEADS * b + h + 1)
                    if j == 0:
                        if g >= 1:
                            pe.wait_ge(v_norm, 2 * (NG * b + g))
                        else:
                            pe.wait_ge(a_mm, 6 * b + 6)
                            if b >= 1:
                                pe.wait_ge(v_slot, b)
                    for t in range(TB):
                        for k in range(TB):
                            o = (t * HG + j) * VW
                            mm = pe.matmul(b_pv[:, o:o + VW], att[:, h % 4, k * SEQ + t * P:k * SEQ + (t + 1) * P],
                                           v_tok[:, k, h, :], start=k == 0, stop=k == TB - 1)
                    if j == HG - 1:
                        mm.then_inc(e_PV, 1)

                def o_T(b):
                    pe.wait_ge(v_norm, 2 * NG * (b + 1))
                    pe.wait_ge(v_mrow, NG * (b + 1))
                    pe.wait_ge(v_evT, 8 * (b + 1))
                    for half in range(2):
                        for c in (2 * half, 2 * half + 1):
                            for t in range(TB):
                                mm = pe.transpose(b_t[half][:, (c % 2) * SEQ + t * P:(c % 2) * SEQ + (t + 1) * P],
                                                  o_tok[:, t, c * P:(c + 1) * P], ident[:])
                        mm.then_inc(e_oT, 1)

                def feat(w, c):
                    return w[:, c // 2, (c % 2) * SEQ:(c % 2 + 1) * SEQ]

                def y_T(b):
                    pe.wait_ge(v_oT, 4 * (b + 1))
                    if b == 0:
                        pe.wait_ge(v_wsplit.sem, W_OUT_PARTS)
                    for f in range(KC):
                        for c in range(KC):
                            mm = three(b_s[f // 2][:, (f % 2) * SEQ:(f % 2 + 1) * SEQ],
                                       [w[:, c, f * P:(f + 1) * P] for w in w_out], [feat(w, c) for w in oT],
                                       c == 0, c == KC - 1)
                        if f % 2 == 1:
                            mm.then_inc(e_yT, 1)

                def down_and_router(b):
                    pe.wait_ge(a_yhi, 2 * (b + 1))
                    pe.wait_ge(v_ylo, 2 * (b + 1))
                    if b == 0:
                        pe.wait_ge(v_wsplit.sem, W_DOWN_PARTS)
                    pe.wait_ge(a_exp, HEADS * (b + 1))
                    for t in range(TB):
                        for c in range(KC):
                            mm = three(b_a[0][:, t * L:(t + 1) * L], [feat(w, c)[:, t * P:(t + 1) * P] for w in yT],
                                       [w[:, c, :] for w in w_down], c == 0, c == KC - 1)
                        mm.then_inc(e_down, 1)
                    for t in range(TB):
                        for c in range(KC):
                            mm = pe.matmul(b_pv[:, t * E:(t + 1) * E], feat(y_f, c)[:, t * P:(t + 1) * P], w_router[:, c, :],
                                           start=c == 0, stop=c == KC - 1)
                    mm.then_inc(e_router, 1)

                def core(b):
                    pe.wait_ge(a_gyhi, 2 * (b + 1))
                    pe.wait_ge(v_gylo, 2 * (b + 1))
                    for t in range(TB):
                        for c in range(KC):
                            mm = three(b_s[t][:], [feat(w, c)[:, t * P:(t + 1) * P] for w in gyT],
                                       [w[:, c, :] for w in w_core], c == 0, c == KC - 1)
                        mm.then_inc(e_core, 1)

                def gh_T(b):
                    pe.wait_ge(a_gh, TB * (b + 1))
                    for c in range(LC):
                        for t in range(TB):
                            mm = pe.transpose(b_t[0][:, c * SEQ + t * P:c * SEQ + (t + 1) * P], gh_tok[:, t, c * P:(c + 1) * P], ident[:])
                    mm.then_inc(e_ghT, 1)

                pe.wait_ge(d_small, 16 * SMALL)
                pe.wait_ge(p_const, 2)
                for c in range(KC):
                    mm = pe.transpose(b_s[0][:, c * NB:(c + 1) * NB], cond_row[:, c * P:(c + 1) * P], ident[0:NB, 0:NB])
                mm.then_inc(e_condT, 1)
                pe.wait_ge(v_condT, 1)
                for c in range(KC):
                    pe.wait_ge(d_wemb[c % 2], 16 * (c // 2 + 1))
                    for f in range(2 * KC):
                        mm = pe.matmul(b_s[1][:, c * 64 + f * NB:c * 64 + (f + 1) * NB], stage[c % 2][:, f * P:(f + 1) * P],
                                       condT[:, c, :], start=True, stop=True)
                    mm.then_inc(e_ada, 1)
                x_T(0)
                for n in range(6):
                    for c in range(KC):
                        qkv(0, n, c)
                x_T(1)
                for b in range(NB):
                    for g in range(NG + 1):
                        for j in range(HG):
                            h = HG * g + j
                            if g < NG:
                                stack_T(b, h)
                            if g >= 1:
                                scores_T(b, h - HG)
                            if g < NG and b + 1 < NB:
                                qkv(b + 1, g, j)
                            if g < NG and j >= 1:
                                scores(b, h - 1)
                            if g >= 1 and j >= 1:
                                values(b, h - HG - 1)
                            if b >= 1 and (g, j) == (0, 1):
                                ranks(b - 1)
                        if g < NG:
                            scores(b, HG * g + HG - 1)
                        if g >= 1:
                            values(b, HG * g - 1)
                        if g < NG:
                            max_T(b, g)
                    o_T(b)
                    if b + 1 < NB:
                        for c in range(KC):
                            qkv(b + 1, 4, c)
                    y_T(b)
                    if b + 1 < NB:
                        for c in range(KC):
                            qkv(b + 1, 5, c)
                    if b + 2 < NB:
                        x_T(b + 2)
                    down_and_router(b)
                    core(b)
                    gh_T(b)
                ranks(NB - 1)
                pe.wait_ge(v_core, NT)
                pe.matmul(b_s[0][:, 0:E], ones[:], chosen_sum[:, TB, :], start=True, stop=True).then_inc(e_count, 1)

        with ExitStack() as ph:
            def sb(name, shape, dt=F32):
                return sbt(name, shape, dt, ph)

            def pair(name, shape):
                return sb(name + "_hi", shape, F32R), sb(name + "_lo", shape, F32R)

            KX = 2 * E + 1
            QB = 2
            NQ = NB // QB
            acc = sb("acc", [P, NT, L])
            wst = [sb(f"wst{r}", [P, max(NBK[r::2]), 2, LC * BLK]) for r in range(2)]
            ring = pair("ring", [P, RING, 2, LC * BLK])
            SHARED_SLOT = RING - 1
            ghT_f = sb("ghT_f", [P, 2, QB * LC * SEQ])
            ghT = pair("ghT", [P, 2, QB * LC * SEQ])
            hid_f = sb("hid_f", [P, 2, HB, ST])
            hid = pair("hid", [P, 2, HB, ST])
            x_slots = sb("x_slots", [P, 2, L])
            xT = pair("x_T", [P, LC * ST])
            y_slots = sb("y_slots", [P, 2, L])
            b1_col = sb("b1_col", [P, NEB * HB])
            sb1_col = sb("sb1_col", [P, HB])
            bias_out = sb("bias_out", [P, 2, D])
            w_up = pair("w_up", [P, LC * D])
            count_i = sb("count_i", [P, E], I32)
            tiles_f = sb("tiles_f", [P, E])
            first_f = sb("first_f", [P, E + 1])
            row_f = sb("row_f", [P, 3, E])
            route_i = sb("route_i", [P, 3, E + 1], I32)
            y_rows = sb("y_rows", [P, 2, NT])
            y_idx = sb("y_idx", [P, 2, NT], U32)
            picked = sb("picked2", [P, 2, NT, E])
            ex = sb("ex", [P, NT, E])
            gate = sb("gate", [P, 2, NT])
            zz = sb("zz", [P, 4, NT])
            gx = sb("gx", [P, NT, KX])
            corr_rhs = sb("corr_rhs", [KX, L])
            accT = pair("accT", [P, 2, LC * P])
            YR = 4
            y_got = ghT_f[:].rearrange("p q (r k l) -> p (q r) k l", r=YR // 2, k=2)
            gxT = wst[0][0:KX].rearrange("p k w n -> p (k w n)")[:, 0:NT * P]
            upst = wst[0][:, NBK[0]].rearrange("p w n -> p (w n)")
            assert LC * D == 2 * LC * BLK and NT * P <= NBK[2] * 2 * LC * BLK

            d_gh, d_misc, d_out = [sem("d_gh0"), sem("d_gh1")], sem("d_misc"), sem("d_out")
            d_ws, d_we = sem("d_ws"), [sem("d_we0"), sem("d_we1")]
            d_pad, d_xs, d_y, d_y_last, d_m = sem("d_pad"), sem("d_xs"), sem("d_y"), sem("d_y_last"), sem("d_m")
            d_got = [sem(f"d_got{r}") for r in range(YR)]
            pk, vk = Sem(sem("pk")), Sem(sem("vk"))
            v_tiles, v_rows, v_idx = sem("v_tiles"), sem("v_rows"), sem("v_idx")
            v_gate, a_gate, v_gates = sem("v_gate"), sem("a_gate"), sem("v_gates")
            a_whi, v_whi, p_wlo = sem("a_whi"), sem("v_whi"), sem("p_wlo")
            v_ghi, v_glo = sem("v_ghi"), sem("v_glo")
            e_h, a_gelu, v_hhi, v_hlo = sem("e_h"), sem("a_gelu"), sem("v_hhi"), sem("v_hlo")
            e_y, a_y = sem("e_y"), sem("a_y")
            e_x, a_xhi, v_xlo = sem("e_x"), sem("a_xhi"), sem("v_xlo")
            a_uhi, v_ulo = sem("a_uhi"), sem("v_ulo")
            e_gxT, v_gxT, e_corr, v_sum = sem("e_gxT"), sem("v_gxT"), sem("e_corr"), sem("v_sum")
            e_aT, a_ahi, v_alo, e_up, v_up = sem("e_aT"), sem("a_ahi"), sem("v_alo"), sem("e_up"), sem("v_up")

            h_bank = ((bank["mm"], bank["pv"]), (bank["t0"], bank["t1"]))
            y_bank = ((bank["s0"], bank["s1"]), (bank["a0"], bank["a1"]))
            x_bank = bank["a1"]

            H0, Y0, PER_TILE = NB * HB, NB * 2, MAXB * HB

            def event(T, k, hb):
                return T * PER_TILE + (H0 + k * HB + hb + 1)

            def step_of(nb, k, hb):
                return 1 + (MAXB - nb) * HB if (k, hb) == (nb - 1, HB - 1) else 1

            w1_dram = a["e_w1"].rearrange("(c p) (j n) -> p j c n", p=P, n=BLK)
            w2_dram = a["e_w2"].rearrange("(j c p) n -> p j c n", p=P, c=HB)
            we_count = [32 * sum(NBK[e % 2:e + 1:2]) for e in range(E)]
            MISC = 7

            def first_tiles(eng):
                eng.wait_ge(v_tiles, 1)
                return [0] + [eng.value_load(route_i[0:1, 0, e:e + 1], min_val=e, max_val=MAXT) for e in range(1, E + 1)]

            def rows(dram, first):
                return dram[bass.ds(first, ST), :].rearrange("(t p) d -> p t d", p=P)

            P_ZERO, P_CONST, P_RESID = 1, 3, 4
            block = ph.enter_context(nc.Block())

            @block.sync
            def _(sp):
                def load_gh(q):
                    if q >= 2:
                        sp.wait_ge(v_glo, q - 1)
                    sp.dma_start(ghT_f[:, q % 2, :].rearrange("p (b n) -> p b n", b=QB),
                                 ght_dram[:, q * QB:(q + 1) * QB, :]).then_inc(d_gh[q % 2], 16)

                def load_expert(e):
                    for k in range(NBK[e]):
                        for w, dram in ((0, w1_dram), (1, w2_dram)):
                            sp.dma_start(wst[e % 2][:, k, w, :].rearrange("p (c n) -> p c n", c=2),
                                         dram[:, B0[e] + k, :, :]).then_inc(d_we[e % 2], 16)

                load_gh(0)
                for w, name in ((0, "s_w1"), (1, "s_w2")):
                    sp.dma_start(wst[1][:, MAXB - 1, w, :].rearrange("p (c n) -> p c n", c=2),
                                 a[name].rearrange("(c p) n -> p c n", p=P)).then_inc(d_ws, 16)
                with nc.allow_non_contiguous_dma(reason="columns of biases"):
                    sp.dma_start(sb1_col[:], a["s_b1"].rearrange("(c p) -> p c", p=P)).then_inc(d_misc, 16)
                    sp.dma_start(b1_col[:], a["e_b1"].rearrange("(c p) -> p c", p=P)).then_inc(d_misc, 16)
                load_gh(1)
                load_expert(0)
                load_expert(1)
                sp.dma_start(bias_out[:, 0, :], a["up_b"].partition_broadcast(P)).then_inc(d_misc, 16)
                sp.dma_start(bias_out[:, 1, :], a["core_b"].partition_broadcast(P)).then_inc(d_misc, 16)
                sp.dma_start(corr_rhs[E:2 * E, :], a["e_b2"]).then_inc(d_misc, 16)
                sp.dma_start(corr_rhs[2 * E:KX, :], a["s_b2"].unsqueeze(0)).then_inc(d_misc, 16)
                sp.dma_start(upst.rearrange("p (c n) -> p c n", c=LC),
                             a["up_w"].rearrange("(c p) n -> p c n", p=P)).then_inc(d_misc, 16)
                load_gh(2)
                load_gh(3)
                first = first_tiles(sp)
                sp.wait_ge(v_rows, 1)
                sp.wait_ge(pk.sem, P_ZERO)
                for e in range(E):
                    r = sp.value_load(route_i[0:1, 1, e:e + 1], min_val=e * REGION, max_val=(e + 1) * REGION - ST)
                    sp.dma_start(rows(slots_dram, r), y_slots[:]).then_inc(d_pad, 16)
                sp.wait_ge(d_pad, 16 * E)
                for e in range(E):
                    if e + 2 < E:
                        if e == 0:
                            sp.wait_ge(v_ulo, 1)
                        sp.wait_ge(p_wlo, 2 * (1 + B0[e + 1]))
                        load_expert(e + 2)
                    with sp.Fori(first[e], first[e + 1]) as T:
                        sp.wait_ge(e_x, T + 1)
                        sp.dma_start(x_slots[:], rows(slots_dram, nc.s_assert_within(
                            (T - first[e]) * ST + e * REGION, e * REGION, (e + 1) * REGION - ST,
                            skip_runtime_bounds_check_because="T is a tile of expert e, which has at most REGION // ST"))).then_inc(d_xs, 16)
                        sp.wait_ge(a_y, T * 2 + Y0)
                        sp.dma_start(rows(y_dram, T * ST), y_slots[:]).then_inc(d_y, 16)
                sp.wait_ge(e_x, first[E] + 1)
                sp.dma_start(x_slots[:], rows(slots_dram, 0)).then_inc(d_xs, 16)
                sp.wait_ge(a_y, first[E] * 2 + Y0)
                sp.dma_start(rows(y_dram, first[E] * ST), y_slots[:]).then_inc(d_y_last, 16)
                sp.wait_ge(d_y_last, 16)
                for e in range(E):
                    r = sp.value_load(route_i[0:1, 2, e:e + 1], min_val=ST, max_val=(MAXT + 1) * ST - 1)
                    sp.dma_start(corr_rhs[e:e + 1, :], y_dram[bass.ds(r, 1), :]).then_inc(d_m, 16)
                for i in range(NT):
                    sp.wait_ge(v_up, i + 1)
                    sp.dma_start(out_dram[:, i, :], resid[:, i, :]).then_inc(d_out, 16)
                sp.wait_ge(d_out, 16 * NT)

            @block.gpsimd
            def _(pool):
                pk.inc(pool.memset(y_slots[:], 0.0))
                pk.inc(pool.memset(gx[:, :, E:2 * E], 1.0))
                pk.inc(pool.memset(gx[:, :, 2 * E:KX], SHARED_SCALE))

                def split_lo(n, src, slot):
                    for w, hi_ready in ((0, a_whi), (1, v_whi)):
                        pool.wait_ge(hi_ready, n + 1)
                        pool.tensor_tensor(ring[1][:, slot, w, :], src[:, w, :], ring[0][:, slot, w, :].bitcast(F32),
                                           ALU.subtract).then_inc(p_wlo, 1)

                def expert_lo(e):
                    for k in range(NBK[e]):
                        split_lo(1 + B0[e] + k, wst[e % 2][:, k], (B0[e] + k) % RING)

                split_lo(0, wst[1][:, MAXB - 1], SHARED_SLOT)
                expert_lo(0)
                expert_lo(1)
                pool.wait_ge(d_misc, 16 * MISC)
                pk.inc(pool.tensor_tensor(bias_out[:, 0, :], bias_out[:, 0, :], bias_out[:, 1, :], ALU.add))
                pool.wait_ge(pk.sem, pk.count)
                for i in range(NT):
                    pk.inc(pool.tensor_tensor(resid[:, i, :], resid[:, i, :], bias_out[:, 0, :], ALU.add))
                for e in range(2, E):
                    expert_lo(e)
                pool.wait_ge(v_idx, 1)
                pool.wait_ge(d_y_last, 16)
                for i in range(NT):
                    if i >= YR:
                        pool.wait_ge(v_sum, i - YR + 1)
                    for k in range(2):
                        pool.indirect_dma_start(
                            out=y_got[:, i % YR, k, :], out_offset=None, in_=y_dram,
                            in_offset=bass.IndirectOffsetOnAxis(ap=y_idx[:, k, i:i + 1], axis=0),
                            bounds_check=(MAXT + 1) * ST - 1, oob_is_err=True).then_inc(d_got[i % YR], 16)

            @block.scalar
            def _(act):
                def split_w1(n, src, slot):
                    act.activation(ring[0][:, slot, 0, :], src[:, 0, :], ACT.Copy).then_inc(a_whi, 1)

                def expert_w1(e):
                    act.wait_ge(d_we[e % 2], we_count[e])
                    for k in range(NBK[e]):
                        split_w1(1 + B0[e] + k, wst[e % 2][:, k], (B0[e] + k) % RING)

                def gelu(bank_, k, hb, bias):
                    return act.activation(hid_f[:, k % 2, hb, :], bank_[:, 0:ST], ACT.Gelu, bias=bias)

                act.wait_ge(d_ws, 32)
                split_w1(0, wst[1][:, MAXB - 1], SHARED_SLOT)
                act.wait_ge(v_gate, 1)
                act.activation(ex[:], ex[:], ACT.Exp).then_inc(a_gate, 1)
                act.wait_ge(d_misc, 16 * MISC)
                for u in range(NB + 1):
                    if u < NB:
                        for hb in range(HB):
                            act.wait_ge(e_h, u * HB + hb + 1)
                            gelu(h_bank[u % 2][hb], u, hb, sb1_col[:, hb:hb + 1]).then_inc(a_gelu, 1)
                    if u == 1:
                        expert_w1(0)
                    if u == 2:
                        act.activation(w_up[0][:], upst, ACT.Copy).then_inc(a_uhi, 1)
                    if u >= 1:
                        for tt in range(2):
                            act.wait_ge(e_y, (u - 1) * 2 + tt + 1)
                            act.activation(acc[:, (u - 1) * 2 + tt, :], y_bank[(u - 1) % 2][tt][:, 0:L], ACT.Copy,
                                           scale=SHARED_SCALE).then_inc(a_y, 1)
                act.wait_ge(v_gate, 2)
                act.activation(zz[:, 2, :], zz[:, 2, :], ACT.Exp).then_inc(a_gate, 1)

                first = first_tiles(act)
                act.wait_ge(e_x, 2)
                act.activation(xT[0][:], x_bank[:], ACT.Copy).then_inc(a_xhi, 1)
                for e in range(E):
                    if e + 1 < E:
                        if e >= 1:
                            act.wait_ge(e_y, first[e - 1] * 2 + Y0)
                        expert_w1(e + 1)
                    nb = NBK[e]
                    with act.Fori(first[e], first[e + 1]) as T:
                        for k in range(nb):
                            for hb in range(HB):
                                act.wait_ge(e_h, event(T, k, hb))
                                g = (B0[e] + k) * HB + hb
                                gelu(h_bank[k % 2][hb], k, hb, b1_col[:, g:g + 1]).then_inc(a_gelu, step_of(nb, k, hb))
                        act.wait_ge(e_x, T + 3)
                        act.activation(xT[0][:], x_bank[:], ACT.Copy).then_inc(a_xhi, 1)
                        act.wait_ge(d_y, T * 16 + 16)
                        for tt in range(2):
                            act.wait_ge(e_y, T * 2 + (Y0 + tt + 1))
                            act.activation(y_slots[:, tt, :], y_bank[0][tt][:, 0:L], ACT.Copy).then_inc(a_y, 1)
                for i in range(NT):
                    act.wait_ge(e_aT, i + 1)
                    if i >= 2:
                        act.wait_ge(e_up, i - 1)
                    act.activation(accT[0][:, i % 2, :], bank[("t0", "t1")[i % 2]][:, 0:LC * P], ACT.Copy).then_inc(a_ahi, 1)

            @block.vector
            def _(dve):
                def step(ins):
                    dve.wait_ge(vk.sem, vk.inc(ins))

                def split_gh(q):
                    dve.wait_ge(d_gh[q % 2], 16 * (q // 2 + 1))
                    if q >= 2:
                        dve.wait_ge(e_h, (q - 1) * QB * HB)
                    dve.tensor_copy(ghT[0][:, q % 2, :], ghT_f[:, q % 2, :]).then_inc(v_ghi, 1)
                    dve.wait_ge(v_ghi, q + 1)
                    dve.tensor_tensor(ghT[1][:, q % 2, :], ghT_f[:, q % 2, :], ghT[0][:, q % 2, :].bitcast(F32),
                                      ALU.subtract).then_inc(v_glo, 1)

                def expert_w2(e):
                    dve.wait_ge(d_we[e % 2], we_count[e])
                    for k in range(NBK[e]):
                        dve.tensor_copy(ring[0][:, (B0[e] + k) % RING, 1, :], wst[e % 2][:, k, 1, :]).then_inc(v_whi, 1)

                def split_hid(k, hb, done, by):
                    dve.wait_ge(a_gelu, done)
                    dve.tensor_copy(hid[0][:, k % 2, hb, :], hid_f[:, k % 2, hb, :]).then_inc(v_hhi, by)
                    dve.wait_ge(v_hhi, done)
                    dve.tensor_tensor(hid[1][:, k % 2, hb, :], hid_f[:, k % 2, hb, :], hid[0][:, k % 2, hb, :].bitcast(F32),
                                      ALU.subtract).then_inc(v_hlo, by)

                step(dve.tensor_copy(count_i[:], counts[:]))
                step(dve.tensor_single_scalar(count_i[:], count_i[:], ST.bit_length() - 1, ALU.logical_shift_right))
                step(dve.tensor_copy(tiles_f[:], count_i[:]))
                step(dve.tensor_scalar(first_f[:, 0:1], counts[:, 0:1], 0.0, None, ALU.mult))
                for e in range(E):
                    step(dve.scalar_tensor_tensor(out=first_f[:, e + 1:e + 2], in0=tiles_f[:, e:e + 1], scalar=1.0,
                                                  in1=first_f[:, e:e + 1], op0=ALU.add, op1=ALU.add))
                dve.tensor_copy(route_i[:, 0, :], first_f[:]).then_inc(v_tiles, 1)
                step(dve.tensor_reduce(zz[:, 0, :], logits[:], AX.X, ALU.max))
                dve.tensor_tensor(ex[:], logits[:], zz[:, 0, :].unsqueeze(2).to_broadcast([P, NT, E]), ALU.subtract).then_inc(v_gate, 1)
                dve.wait_ge(d_ws, 32)
                dve.tensor_copy(ring[0][:, SHARED_SLOT, 1, :], wst[1][:, MAXB - 1, 1, :]).then_inc(v_whi, 1)
                split_gh(0)
                step(dve.tensor_tensor(row_f[:, 0, :], region0[:], counts[:], ALU.add))
                step(dve.tensor_scalar(row_f[:, 2, :], first_f[:, 0:E], 1.0, float(ST), ALU.add, ALU.mult))
                step(dve.tensor_tensor(row_f[:, 1, :], row_f[:, 2, :], counts[:], ALU.add))
                dve.tensor_copy(route_i[:, 1:3, 0:E], row_f[:, 0:2, :]).then_inc(v_rows, 1)
                split_gh(1)

                def route():
                    step(dve.tensor_tensor(row_f[:, 2, :], row_f[:, 2, :], region0[:], ALU.subtract))
                    for k in range(2):
                        step(dve.tensor_tensor(picked[:, k], onehot[:, k], row_f[:, 2, :].unsqueeze(1).to_broadcast([P, NT, E]), ALU.mult))
                    step(dve.tensor_reduce(y_rows[:], picked[:], AX.X, ALU.add))
                    step(dve.tensor_tensor(y_rows[:], y_rows[:], slotf[:], ALU.add))
                    dve.tensor_copy(y_idx[:], y_rows[:]).then_inc(v_idx, 1)

                def probabilities():
                    dve.wait_ge(a_gate, 1)
                    step(dve.tensor_reduce(zz[:, 0, :], ex[:], AX.X, ALU.add))
                    step(dve.reciprocal(zz[:, 1, :], zz[:, 0, :]))
                    dve.wait_ge(v_idx, 1)
                    step(dve.tensor_tensor(picked[:, 1], onehot[:, 1], ex[:], ALU.mult))
                    step(dve.tensor_reduce(zz[:, 2, :], picked[:, 1], AX.X, ALU.add))
                    step(dve.tensor_tensor(zz[:, 2, :], zz[:, 2, :], zz[:, 1, :], ALU.mult))
                    dve.tensor_tensor(zz[:, 2, :], zz[:, 2, :], zz[:, 1, :], ALU.subtract).then_inc(v_gate, 1)

                def gates():
                    dve.wait_ge(a_gate, 2)
                    step(dve.tensor_scalar(zz[:, 3, :], zz[:, 2, :], 1.0, None, ALU.add))
                    step(dve.reciprocal(gate[:, 0, :], zz[:, 3, :]))
                    step(dve.tensor_tensor(gate[:, 1, :], gate[:, 0, :], zz[:, 2, :], ALU.mult))
                    for k in range(2):
                        step(dve.tensor_tensor(picked[:, k], onehot[:, k], gate[:, k, :].unsqueeze(2).to_broadcast([P, NT, E]), ALU.mult))
                    step(dve.tensor_tensor(picked[:, 0], picked[:, 0], picked[:, 1], ALU.add))
                    dve.wait_ge(pk.sem, P_CONST)
                    dve.tensor_scalar(gx[:, :, 0:E], picked[:, 0], -1.0, 1.0, ALU.mult, ALU.add).then_inc(v_gates, 1)

                for u in range(NB):
                    for hb in range(HB):
                        split_hid(u, hb, u * HB + hb + 1, 1)
                    if u == 0:
                        expert_w2(0)
                    if u in (1, 3):
                        split_gh(u // 2 + 2)
                    if u == 4:
                        route()
                    if u == 5:
                        dve.wait_ge(a_uhi, 1)
                        dve.tensor_tensor(w_up[1][:], upst, w_up[0][:].bitcast(F32), ALU.subtract).then_inc(v_ulo, 1)
                    if u == 6:
                        probabilities()

                first = first_tiles(dve)
                dve.wait_ge(a_xhi, 1)
                dve.tensor_tensor(xT[1][:], x_bank[:], xT[0][:].bitcast(F32), ALU.subtract).then_inc(v_xlo, 1)
                for e in range(E):
                    if e + 1 < E:
                        if e >= 1:
                            dve.wait_ge(e_y, first[e - 1] * 2 + Y0)
                        expert_w2(e + 1)
                    nb = NBK[e]
                    with dve.Fori(first[e], first[e + 1]) as T:
                        for k in range(nb):
                            for hb in range(HB):
                                split_hid(k, hb, event(T, k, hb), step_of(nb, k, hb))
                        dve.wait_ge(a_xhi, T + 2)
                        dve.tensor_tensor(xT[1][:], x_bank[:], xT[0][:].bitcast(F32), ALU.subtract).then_inc(v_xlo, 1)
                gates()
                dve.wait_ge(p_wlo, 2 * (1 + NEB))
                for q in range(NT // 4):
                    dve.wait_ge(e_gxT, q + 1)
                    dve.tensor_copy(gxT[:, q * 4 * P:(q + 1) * 4 * P], h_bank[q // 2][q % 2][0:KX, :]).then_inc(v_gxT, 1)
                for i in range(NT + 2):
                    if i < NT:
                        dve.wait_ge(d_got[i % YR], 32 * (i // YR + 1))
                        for k in range(2):
                            step(dve.scalar_tensor_tensor(out=acc[:, i, :], in0=y_got[:, i % YR, k, :], scalar=gate[:, k, i:i + 1],
                                                          in1=acc[:, i, :], op0=ALU.mult, op1=ALU.add))
                        dve.wait_ge(e_corr, i + 1)
                        dve.tensor_tensor(acc[:, i, :], acc[:, i, :], h_bank[0][i % 2][:, 0:L], ALU.add).then_inc(v_sum, 1)
                    if 1 <= i <= NT:
                        w = i - 1
                        dve.wait_ge(a_ahi, w + 1)
                        dve.tensor_tensor(accT[1][:, w % 2, :], bank[("t0", "t1")[w % 2]][:, 0:LC * P], accT[0][:, w % 2, :].bitcast(F32),
                                          ALU.subtract).then_inc(v_alo, 1)
                    if i >= 2:
                        w = i - 2
                        dve.wait_ge(e_up, w + 1)
                        if w == 0:
                            dve.wait_ge(pk.sem, P_RESID + NT)
                        dve.tensor_tensor(resid[:, w, :], resid[:, w, :], y_bank[0][w % 2][:], ALU.add).then_inc(v_up, 1)

            @block.tensor
            def _(pe):
                def terms(lhs, rhs):
                    return ((lhs[0], rhs[0]), (lhs[0], rhs[1]), (lhs[1], rhs[0]))

                def hidden(out_bank, slot, hb, x_by_feature):
                    k_terms = []
                    for c in range(LC):
                        o = c * BLK + hb * P
                        k_terms += terms([w[:, slot, 0, o:o + P] for w in ring], x_by_feature(c))
                    for i, (l, r) in enumerate(k_terms):
                        mm = pe.matmul(out_bank[:, 0:ST], l, r, start=i == 0, stop=i == len(k_terms) - 1)
                    return mm

                def output(banks, slot, parity, hb, first_of_tile, last_of_tile):
                    for tt in range(2):
                        lhs = [w[:, parity, hb, tt * P:(tt + 1) * P] for w in hid]
                        for i, (l, r) in enumerate(terms(lhs, [w[:, slot, 1, hb * L:(hb + 1) * L] for w in ring])):
                            mm = pe.matmul(banks[tt][:, 0:L], l, r, start=first_of_tile and i == 0, stop=last_of_tile and i == 2)
                        if last_of_tile:
                            mm.then_inc(e_y, 1)

                def shared_hidden(u):
                    q = u // QB
                    if u % QB == 0:
                        pe.wait_ge(v_glo, q + 1)
                    if u == 0:
                        pe.wait_ge(p_wlo, 2)
                        pe.sem_inc(e_x, 1)
                    for hb in range(HB):
                        hidden(h_bank[u % 2][hb], SHARED_SLOT, hb,
                               lambda c: [w[:, q % 2, (u % QB) * LC * SEQ + c * SEQ:(u % QB) * LC * SEQ + (c + 1) * SEQ]
                                          for w in ghT]).then_inc(e_h, 1)

                def x_T(ready):
                    pe.wait_ge(d_xs, ready)
                    for c in range(LC):
                        for t in range(2):
                            mm = pe.transpose(x_bank[:, c * ST + t * P:c * ST + (t + 1) * P], x_slots[:, t, c * P:(c + 1) * P], ident[:])
                    mm.then_inc(e_x, 1)

                shared_hidden(0)
                for u in range(NB):
                    if u + 1 < NB:
                        shared_hidden(u + 1)
                    if u >= 2:
                        pe.wait_ge(a_y, 2 * (u - 1))
                    for hb in range(HB):
                        pe.wait_ge(v_hlo, u * HB + hb + 1)
                        output(y_bank[u % 2], SHARED_SLOT, u % 2, hb, hb == 0, hb == HB - 1)

                first = first_tiles(pe)
                pe.wait_ge(a_y, Y0)
                x_T(16)
                for e in range(E):
                    nb = NBK[e]
                    pe.wait_ge(p_wlo, 2 * (1 + B0[e + 1]))
                    slots = [(B0[e] + k) % RING for k in range(nb)]

                    def expert_hidden(T, k):
                        for hb in range(HB):
                            hidden(h_bank[k % 2][hb], slots[k], hb,
                                   lambda c: [w[:, c * ST:(c + 1) * ST] for w in xT]).then_inc(e_h, step_of(nb, k, hb))

                    with pe.Fori(first[e], first[e + 1]) as T:
                        pe.wait_ge(v_xlo, T + 1)
                        expert_hidden(T, 0)
                        for k in range(nb):
                            if k + 1 < nb:
                                expert_hidden(T, k + 1)
                            else:
                                x_T(T * 16 + 32)
                            if k == 0:
                                pe.wait_ge(a_y, T * 2 + Y0)
                            for hb in range(HB):
                                pe.wait_ge(v_hlo, event(T, k, hb))
                                output(y_bank[0], slots[k], k % 2, hb, (k, hb) == (0, 0), (k, hb) == (nb - 1, HB - 1))

                pe.wait_ge(v_gates, 1)
                for q in range(NT // 4):
                    for t in range(4):
                        mm = pe.transpose(h_bank[q // 2][q % 2][0:KX, t * P:(t + 1) * P], gx[:, 4 * q + t, :], ident[:])
                    mm.then_inc(e_gxT, 1)

                def corr(i):
                    if i >= 2:
                        pe.wait_ge(v_sum, i - 1)
                    pe.matmul(h_bank[0][i % 2][:, 0:L], gxT[:, i * P:(i + 1) * P], corr_rhs[:], start=True, stop=True).then_inc(e_corr, 1)

                pe.wait_ge(v_gxT, NT // 4)
                pe.wait_ge(d_m, 16 * E)
                corr(0)
                corr(1)
                for i in range(NT + 1):
                    if i < NT:
                        pe.wait_ge(v_sum, i + 1)
                        if i >= 2:
                            pe.wait_ge(v_alo, i - 1)
                        for c in range(LC):
                            mm = pe.transpose(bank[("t0", "t1")[i % 2]][:, c * P:(c + 1) * P], acc[:, i, c * P:(c + 1) * P], ident[:])
                        mm.then_inc(e_aT, 1)
                        if i + 2 < NT:
                            corr(i + 2)
                    if i >= 1:
                        w = i - 1
                        pe.wait_ge(v_alo, w + 1)
                        if w == 0:
                            pe.wait_ge(v_ulo, 1)
                            pe.wait_ge(a_y, first[E] * 2 + Y0)
                        if w >= 2:
                            pe.wait_ge(v_up, w - 1)
                        k_terms = []
                        for c in range(LC):
                            k_terms += terms([t[:, w % 2, c * P:(c + 1) * P] for t in accT], [t[:, c * D:(c + 1) * D] for t in w_up])
                        for k, (l, r) in enumerate(k_terms):
                            mm = pe.matmul(y_bank[0][w % 2][:], l, r, start=k == 0, stop=k == len(k_terms) - 1)
                        mm.then_inc(e_up, 1)



def kernel(**inputs):
    import numpy as np
    import concourse.bacc as bacc
    from concourse.bass_utils import run_bass_kernel_spmd

    c = {k.removeprefix("L0_"): np.ascontiguousarray(v) for k, v in inputs.items()}
    E = len(HID)
    arrays = {
        "x": c["x"], "cond": c["cond_2048"], "w_emb": c["cond_W_emb"], "b_emb": c["cond_b_emb"],
        "g_norm": c["cond_g_norm"], "w_qkv": c["cond_W_qkv"], "g_q": c["cond_g_q"], "g_k": c["cond_g_k"],
        "w_out": c["cond_W_out"], "down_w": c["ffn_down_w"], "down_b": c["ffn_down_b"], "up_w": c["ffn_up_w"],
        "up_b": c["ffn_up_b"], "router_w": c["ffn_router_w"], "router_b": c["ffn_router_b"],
        "core_w": c["ffn_core_w"], "core_b": c["ffn_core_b"],
        "e_w1": np.concatenate([c[f"ffn_e{e}_w1"] for e in range(E)], axis=1),
        "e_b1": np.concatenate([c[f"ffn_e{e}_b1"] for e in range(E)]),
        "e_w2": np.concatenate([c[f"ffn_e{e}_w2"] for e in range(E)], axis=0),
        "e_b2": np.stack([c[f"ffn_e{e}_b2"] for e in range(E)]),
        "s_w1": c["ffn_shared_w1"], "s_b1": c["ffn_shared_b1"], "s_w2": c["ffn_shared_w2"], "s_b2": c["ffn_shared_b2"],
    }
    nc = bacc.Bacc("TRN2", target_bir_lowering=False, num_devices=1, dynamic_dma_scratch_size=4096)
    aps = {n: nc.dram_tensor(f"in_{n}", v.shape, mybir.dt.from_np(v.dtype), kind="ExternalInput").ap()
           for n, v in arrays.items()}
    out = nc.dram_tensor("out_0", c["x"].shape, F32, kind="ExternalOutput").ap()
    adaln_moe_program(nc, aps, out)
    r = run_bass_kernel_spmd(nc, [{f"in_{n}": v for n, v in arrays.items()}], core_ids=[0])
    return r.results[0]["out_0"]
```

```python
from contextlib import ExitStack

import concourse.bass as bass
from concourse import mybir

ALU = mybir.AluOpType
ACT = mybir.ActivationFunctionType
AX = mybir.AxisListType
F32 = mybir.dt.float32
F32R = mybir.dt.float32r
BF16 = mybir.dt.bfloat16
I32 = mybir.dt.int32
U32 = mybir.dt.uint32

P = 128
HID = [256, 512, 768, 1024, 256, 512, 768, 1024]
HEADS = 16
EPS = 1e-6
COST_LAMBDA = 1e-7
SHARED_SCALE = 0.1


class Sem:

    def __init__(self, sem):
        self.sem, self.count = sem, 0

    def inc(self, ins, by=1):
        ins.then_inc(self.sem, by)
        self.count += by
        return self.count


def adaln_moe_program(nc, a, out):
    x, cond = a["x"], a["cond"]
    NB, SEQ, D = x.shape
    L = a["down_w"].shape[1]
    E = len(HID)
    NT = NB * SEQ // P
    TB = SEQ // P
    KC = D // P
    LC = L // P
    DH = D // HEADS
    HG = 4
    LAG = 6
    NG = HEADS // HG
    BLK = 256
    HB = BLK // P
    NBK = [h // BLK for h in HID]
    B0 = [sum(NBK[:e]) for e in range(E + 1)]
    NEB = B0[E]
    MAXB = max(NBK)
    ST = 2 * P
    REGION = NB * SEQ + ST
    MAXT = 2 * NB * SEQ // ST + E
    RING = 9
    VW = DH + 1
    PVW = 96
    QW = 3 * DH
    assert SEQ == 256 and D == 512 and L == 256 and DH == 32 and TB == 2

    xt_dram = x.rearrange("b (t p) d -> p (b t) d", p=P)
    out_dram = out.rearrange("b (t p) d -> p (b t) d", p=P)
    slots_dram = nc.dram_tensor("slots_scratch", [E * REGION, L], F32).ap()
    y_dram = nc.dram_tensor("y_scratch", [(MAXT + 1) * ST, L], F32).ap()
    ght_dram = nc.dram_tensor("ght_scratch", [P, NB, LC * SEQ], F32).ap()

    with ExitStack() as top:
        def sbt(name, shape, dt=F32, ctx=top):
            return ctx.enter_context(nc.sbuf_tensor(name, shape, dt))

        def sem(name):
            return top.enter_context(nc.semaphore(name))

        bank = {n: top.enter_context(nc.psum_tensor("ps_" + n, [P, 512], F32))
                for n in ("mm", "t0", "t1", "s0", "s1", "a0", "a1", "pv")}
        b_t, b_s, b_a = (bank["t0"], bank["t1"]), (bank["s0"], bank["s1"]), (bank["a0"], bank["a1"])
        b_mm, b_pv = bank["mm"], bank["pv"]

        resid = sbt("resid", [P, NT, D])
        ident = sbt("ident", [P, P])
        logits = sbt("logits", [P, NT, E])
        onehot = sbt("onehot", [P, 2, NT, E])
        slotf = sbt("slotf", [P, 2, NT])
        counts = sbt("counts", [P, E])
        region0 = sbt("region0", [P, E])
        iota_e = sbt("iota_e", [P, E + 1])
        slot_idx = sbt("slot_idx", [P, 2, NT], U32)

        gh_tok = sbt("gh_tok", [P, TB, L])
        before = sbt("before", [P, P], BF16)
        ones = sbt("ones", [P, P], BF16)
        chosen = sbt("chosen", [P, TB, E], BF16)
        chosen_sum = sbt("chosen_sum", [P, TB + 1, E], BF16)
        rank = sbt("rank", [P, TB, E])
        picked_slot = sbt("picked_slot", [P, 2, TB, E])

        v_step = Sem(sem("v_step"))
        v_chosen, e_rank, v_slot, d_slots = sem("v_chosen"), sem("e_rank"), sem("v_slot"), sem("d_slots")

        def ranks(pe, b, to):
            pe.wait_ge(v_chosen, b + 1)
            for t in range(TB):
                o = to[:, t * E:(t + 1) * E]
                pe.matmul(o, before[:], chosen[:, t, :], start=True, stop=False)
                mm = pe.matmul(o, ones[:], chosen_sum[:, t, :], start=False, stop=True)
            mm.then_inc(e_rank, 1)

        def place(dve, b, ranks_at):
            def step(ins):
                dve.wait_ge(v_step.sem, v_step.inc(ins))

            dve.wait_ge(e_rank, b + 1)
            step(dve.tensor_tensor(rank[:], ranks_at[:, 0:TB * E].rearrange("p (t e) -> p t e", e=E),
                                   region0[:].unsqueeze(1).to_broadcast([P, TB, E]), ALU.add))
            tiles = slice(b * TB, (b + 1) * TB)
            for k in range(2):
                v_step.inc(dve.tensor_tensor(picked_slot[:, k, :, :], onehot[:, k, tiles, :], rank[:], ALU.mult))
            dve.wait_ge(v_step.sem, v_step.count)
            step(dve.tensor_reduce(slotf[:, :, tiles], picked_slot[:], AX.X, ALU.add))
            dve.tensor_copy(slot_idx[:, :, tiles], slotf[:, :, tiles]).then_inc(v_slot, 1)

        def scatter(pool, b):
            pool.wait_ge(v_slot, b + 1)
            for t in range(TB):
                for k in range(2):
                    i = b * TB + t
                    pool.indirect_dma_start(
                        out=slots_dram, out_offset=bass.IndirectOffsetOnAxis(ap=slot_idx[:, k, i:i + 1], axis=0),
                        in_=gh_tok[:, t, :], in_offset=None, bounds_check=E * REGION - 1,
                        oob_is_err=True).then_inc(d_slots, 16)

        with ExitStack() as ph:
            def sb(name, shape, dt=F32):
                return sbt(name, shape, dt, ph)

            def pair(name, shape):
                return sb(name + "_hi", shape, F32R), sb(name + "_lo", shape, F32R)

            w_qkv = pair("w_qkv", [P, KC, 3 * D])
            w_out = pair("w_out", [P, KC, D])
            w_core = pair("w_core", [P, KC, D])
            w_down = pair("w_down", [P, KC, L])
            w_router = sb("w_router", [P, KC, E])
            xs = sb("xs", [P, KC * SEQ])
            xt = pair("xt", [P, KC, SEQ])
            qkraw = sb("qkraw", [P, 4, D])
            sq = sb("sq", [P, 2, D])
            q_tok = sb("q_tok", [P, TB, HEADS, QW], F32R)
            k_tok = sb("k_tok", [P, TB, HEADS, QW], F32R)
            stacks = sb("stacks", [P, 8, 512], F32R)
            att = sb("att", [P, 4, 512])
            v_rows = sb("v_rows", [P, TB, HEADS * VW + PVW - VW])
            v_tok = v_rows[:, :, 0:HEADS * VW].rearrange("p t (h w) -> p t h w", w=VW)
            o_tok = xs[:].rearrange("p (t d) -> p t d", d=D)
            top8 = sb("top8", [P, TB, 8])
            idx8 = sb("idx8", [P, TB, 8], U32)
            idxf = sb("idxf", [P, TB, 8])
            ght = sq[:, 1, :]
            rowmax = sb("rowmax", [P, 2, TB, HG])
            table_in = sb("table_in", [1, 1])
            ident_r = sb("ident_r", [P, P], F32R)
            rden = sb("rden", [P, TB, HG])
            ss = sb("ss", [P, 4, HEADS])
            rs = sb("rs", [P, 4, HEADS])
            rs_b = sb("rs_b", [P, 4 * HEADS])
            ssx = sb("ssx", [P, NT])
            rx = sb("rx", [P, NT])
            cond_row = sb("cond_row", [NB, D])
            condT = sb("condT", [P, KC, NB])
            bemb_col = sb("bemb_col", [P, 2 * KC])
            gnorm_col = sb("gnorm_col", [P, KC])
            aff_scale = sb("aff_scale", [P, KC, NB])
            aff_shift = sb("aff_shift", [P, KC, NB])
            gqk = sb("gqk", [P, DH])
            gk_b = sb("gk_b", [P, DH])
            down_bias = sb("down_bias", [P, L])
            router_bias = sb("router_bias", [P, E])

            oT = stacks[:, 0:2, :], stacks[:, 2:4, :]
            yT = stacks[:, 4:6, :], stacks[:, 6:8, :]
            gyT = oT
            o_f, y_f = att[:, 0:2, :], att[:, 2:4, :]
            gy_f = o_f
            stage = att[:].rearrange("p a b -> p (a b)"), qkraw[:].rearrange("p a b -> p (a b)")
            emb_stage = sq[:].rearrange("p a b -> p (a b)"), v_rows[:].rearrange("p t w -> p (t w)")[:, 0:2 * D]

            def quarter(n, part):
                w = (q_tok, k_tok)[n % 2][:, n // 2, :, :].rearrange("p h (r d) -> p h r d", d=DH)
                if n % 2 == 0:
                    return w[:, :, 1:2, :] if part else w[:, :, 0:3:2, :]
                return w[:, :, 2:3, :] if part else w[:, :, 0:2, :]

            def times(n, r):
                return qkraw[:, n, :].rearrange("p (h d) -> p h d", d=DH).unsqueeze(2).to_broadcast([P, HEADS, r, DH])

            d_x = [sem(f"d_x{b}") for b in range(NB)]
            d_cond, d_small, d_wemb = sem("d_cond"), sem("d_small"), [sem("d_wemb0"), sem("d_wemb1")]
            d_w = [sem("d_w0"), sem("d_w1")]
            d_ght = sem("d_ght")
            p_const = sem("p_const")
            pc = Sem(p_const)
            v_wsplit, a_wsplit = Sem(sem("v_wsplit")), Sem(sem("a_wsplit"))
            a_ssx, a_table = sem("a_ssx"), Sem(sem("a_table"))
            e_condT, e_ada = sem("e_condT"), sem("e_ada")
            v_condT, v_ada = sem("v_condT"), sem("v_ada")
            v_xs, e_xT, a_xaff, v_xT = sem("v_xs"), sem("e_xT"), sem("a_xaff"), sem("v_xT")
            e_qkv, a_mm = sem("e_qkv"), sem("a_mm")
            p_sq, p_gq, v_ss = sem("p_sq"), sem("p_gq"), sem("v_ss")
            v_qn, a_qhi, v_qlo = sem("v_qn"), sem("a_qhi"), sem("v_qlo")
            e_T, a_evT, v_evT = sem("e_T"), sem("a_evT"), sem("v_evT")
            e_S, v_max, e_mT, v_mrow, a_sel = sem("e_S"), sem("v_max"), sem("e_mT"), sem("v_mrow"), sem("a_sel")
            e_ST, a_exp, e_PV, v_rden, v_norm = sem("e_ST"), sem("a_exp"), sem("e_PV"), sem("v_rden"), sem("v_norm")
            e_oT, a_of, v_oT = sem("e_oT"), sem("a_of"), sem("v_oT")
            e_yT, v_y, a_yhi, v_ylo, a_gy, a_gyhi, v_gylo = (
                sem("e_yT"), sem("v_y"), sem("a_yhi"), sem("v_ylo"), sem("a_gy"), sem("a_gyhi"), sem("v_gylo"))
            e_down, v_h, a_gh, e_router, v_logits = sem("e_down"), sem("v_h"), sem("a_gh"), sem("e_router"), sem("v_logits")
            d_yzero = sem("d_yzero")
            e_core, v_core, e_ghT, a_ghT = sem("e_core"), sem("v_core"), sem("e_ghT"), sem("a_ghT")

            parts = []
            wq_dram = a["w_qkv"].rearrange("(c p) n -> p c n", p=P)
            for c in range(KC):
                parts.append((wq_dram[:, c, :], [w[:, c, :] for w in w_qkv], 3 * D))
            for w, name in ((w_out, "w_out"), (w_core, "core_w"), (w_down, "down_w")):
                n = a[name].shape[1]
                dram = a[name].rearrange("(c p) n -> p c n", p=P)
                parts.append((dram, [t[:].rearrange("p c n -> p (c n)") for t in w], KC * n))
            NPART = len(parts)

            def chunk_bank(b, n):
                return b_pv if b == 0 and n % 2 == 1 else b_mm

            def stage_of(n):
                return stage[n % 2 if n < KC else 0]
            W_QKV_PARTS, W_OUT_PARTS, W_CORE_PARTS, W_DOWN_PARTS = KC, KC + 1, KC + 2, KC + 3
            block = ph.enter_context(nc.Block())

            SMALL = 7
            P_IDENT, P_ZEROS, P_CONSTS, P_VONES = 2, 3, 7, 9

            @block.sync
            def _(sp):
                def load_emb(c):
                    if c >= 2:
                        sp.wait_ge(e_ada, c - 1)
                    sp.dma_start(emb_stage[c % 2],
                                 a["w_emb"].rearrange("(c p) n -> p c n", p=P)[:, c, :]).then_inc(d_wemb[c % 2], 16)

                sp.dma_start(cond_row[:], cond).then_inc(d_cond, 16)
                load_emb(0)
                load_emb(1)
                sp.dma_start(resid[:, 0:TB, :], xt_dram[:, 0:TB, :]).then_inc(d_x[0], 16)
                with nc.allow_non_contiguous_dma(reason="columns of biases and gains"):
                    sp.dma_start(bemb_col[:], a["b_emb"].rearrange("(c p) -> p c", p=P)).then_inc(d_small, 16)
                    sp.dma_start(gnorm_col[:], a["g_norm"].rearrange("(c p) -> p c", p=P)).then_inc(d_small, 16)
                    sp.dma_start(w_router[:], a["router_w"].rearrange("(c p) n -> p c n", p=P)).then_inc(d_small, 16)
                    sp.dma_start(gqk[:], a["g_q"].partition_broadcast(P)).then_inc(d_small, 16)
                    sp.dma_start(gk_b[:], a["g_k"].partition_broadcast(P)).then_inc(d_small, 16)
                    sp.dma_start(down_bias[:], a["down_b"].partition_broadcast(P)).then_inc(d_small, 16)
                    sp.dma_start(router_bias[:], a["router_b"].partition_broadcast(P)).then_inc(d_small, 16)
                def load_part(n):
                    src, _, size = parts[n]
                    if n >= 2:
                        sp.wait_ge(v_wsplit.sem, n - 1 if n <= KC else n)
                    dst = stage_of(n)[:, 0:size]
                    if len(src.shape) == 3:
                        dst = dst.rearrange("p (c n) -> p c n", c=KC)
                    sp.dma_start(dst, src).then_inc(d_w[n % 2], 16)

                def load_x(b):
                    sp.dma_start(resid[:, b * TB:(b + 1) * TB, :], xt_dram[:, b * TB:(b + 1) * TB, :]).then_inc(d_x[b], 16)

                load_part(0)
                load_part(1)
                load_emb(2)
                load_emb(3)
                load_part(2)
                load_part(3)
                load_x(1)
                load_part(4)
                for b in range(2, 5):
                    load_x(b)
                load_part(5)
                for b in range(5, NB):
                    load_x(b)
                load_part(6)
                sp.wait_ge(p_const, P_ZEROS)
                sp.dma_start(y_dram.rearrange("(n p) d -> p n d", p=P),
                             gh_tok[:, 0, :].unsqueeze(1).to_broadcast([P, (MAXT + 1) * ST // P, L])).then_inc(d_yzero, 16)
                for b in range(NB):
                    sp.wait_ge(a_ghT, b + 1)
                    sp.dma_start(ght_dram[:, b, :], ght).then_inc(d_ght, 16)
                sp.wait_ge(d_ght, 16 * NB)
                sp.wait_ge(d_yzero, 16)


            @block.gpsimd
            def _(pool):
                pc.inc(pool.memset(ident[:], 0.0))
                pool.wait_ge(p_const, 1)
                pc.inc(pool.affine_select(out=ident[:], in_=ident[:], compare_op=ALU.not_equal, fill=1.0,
                                          base=0, pattern=[[-1, P]], channel_multiplier=1))
                pc.inc(pool.memset(gh_tok[:], 0.0))
                pc.inc(pool.memset(ones[:], 1.0))
                pool.wait_ge(p_const, 4)
                pc.inc(pool.affine_select(out=before[:], in_=ones[:], compare_op=ALU.is_gt, fill=0.0,
                                          base=0, pattern=[[1, P]], channel_multiplier=-1))
                pc.inc(pool.iota(iota_e[:], pattern=[[1, E + 1]], base=0, channel_multiplier=0,
                                 allow_small_or_imprecise_dtypes=True))
                pc.inc(pool.memset(chosen_sum[:, 0, :], 0.0))
                assert pc.count == P_CONSTS
                pool.wait_ge(e_ada, KC)
                pc.inc(pool.memset(v_rows[:, :, HEADS * VW:], 0.0))
                pc.inc(pool.memset(v_tok[:, :, :, DH:VW], 1.0))

                g_b = gqk[:].unsqueeze(1).to_broadcast([P, HEADS, DH])
                for b in range(NB):
                    for n in range(4):
                        pool.wait_ge(a_mm, 6 * b + n + 1)
                        if 4 * b + n >= 2:
                            pool.wait_ge(v_ss, 4 * b + n - 1)
                        if n == 1 and b >= 2:
                            pool.wait_ge(d_ght, 16 * (b - 1))
                        pool.tensor_tensor(sq[:, n % 2, :], qkraw[:, n, :], qkraw[:, n, :], ALU.mult).then_inc(p_sq, 1)
                        if n % 2 == 0:
                            if n == 0 and b == 0:
                                pool.wait_ge(v_ada, 2)
                            pool.wait_ge(p_sq, 4 * b + n + 1)
                            q = qkraw[:, n, :].rearrange("p (h d) -> p h d", d=DH)
                            pool.tensor_tensor(q, q, g_b, ALU.mult).then_inc(p_gq, 1)
                    if b >= 2:
                        scatter(pool, b - 2)
                scatter(pool, NB - 2)

            @block.scalar
            def _(act):
                def row_squares(b):
                    act.wait_ge(d_x[b], 16)
                    for t in range(TB):
                        i = b * TB + t
                        if i >= 8:
                            act.wait_ge(a_ssx, i - 7)
                        act.activation(stacks[:, i % 8, :], resid[:, i, :], ACT.Square,
                                       accum_out=ssx[:, i:i + 1]).then_inc(a_ssx, 1)

                def split_hi(n):
                    act.wait_ge(d_w[n % 2], 16 * (n // 2 + 1))
                    _, (hi, _), size = parts[n]
                    a_wsplit.inc(act.activation(hi, stage_of(n)[:, 0:size], ACT.Copy))

                def x_affine(b):
                    for c in range(KC):
                        src = (b_t[1], b_a[1])[c // 2][:, (c % 2) * SEQ:(c % 2 + 1) * SEQ]
                        if c % 2 == 0:
                            act.wait_ge(e_xT, 2 * b + c // 2 + 1)
                        if c == 0:
                            act.wait_ge(e_xT, 2 * b + 2)
                        act.activation(xs[:, c * SEQ:(c + 1) * SEQ], src, ACT.Identity,
                                       bias=aff_shift[:, c, b:b + 1], scale=aff_scale[:, c, b:b + 1]).then_inc(a_xaff, 1)

                def select_heads(b):
                    if b == 0:
                        act.wait_ge(a_ssx, NT)
                    else:
                        act.wait_ge(e_core, TB * b)
                    act.activation(stacks[QW:QW + HG, :, SEQ:2 * SEQ].rearrange("p (r j) n -> p r j n", j=HG),
                                   ident[QW:QW + HG, QW:QW + HG].unsqueeze(1).unsqueeze(3).to_broadcast([HG, 2, HG, SEQ]),
                                   ACT.Copy).then_inc(a_sel, 1)

                def copy_chunk(b, n):
                    act.wait_ge(e_qkv, 6 * b + n + 1)
                    src = chunk_bank(b, n)
                    if n < 4:
                        act.activation(qkraw[:, n, :], src[:], ACT.Copy).then_inc(a_mm, 1)
                    else:
                        act.activation(v_tok[:, n - 4, :, 0:DH], src[:].rearrange("p (h d) -> p h d", d=DH),
                                       ACT.Copy).then_inc(a_mm, 1)

                def q_hi(b, ns):
                    for n in ns:
                        act.wait_ge(v_qn, 4 * b + n + 1)
                        act.activation(quarter(n, 0), times(n, 2), ACT.Copy).then_inc(a_qhi, 1)

                def ev_T(b, h):
                    act.wait_ge(e_T, HEADS * b + h + 1)
                    act.activation(stacks[0:QW, h % 8, :], b_t[h % 2][0:QW, :], ACT.Copy).then_inc(a_evT, 1)

                def load_table(func):
                    if a_table.count:
                        act.wait_ge(a_table.sem, a_table.count)
                    a_table.inc(act.activation(table_in[:], ident[0:1, 0:1], func))

                def exp(b, h):
                    act.wait_ge(e_ST, HEADS * b + h + 1)
                    act.activation(att[:, h % 4, :], b_a[h % 2][:], ACT.Exp).then_inc(a_exp, 1)

                row_squares(0)
                for n in range(W_QKV_PARTS):
                    split_hi(n)
                row_squares(1)
                act.wait_ge(v_ada, 1)
                x_affine(0)
                act.wait_ge(v_wsplit.sem, W_QKV_PARTS)
                copy_chunk(0, 0)
                split_hi(W_QKV_PARTS)
                copy_chunk(0, 1)
                row_squares(2)
                row_squares(3)
                copy_chunk(0, 2)
                row_squares(4)
                copy_chunk(0, 3)
                act.wait_ge(p_const, P_VONES)
                copy_chunk(0, 4)
                split_hi(W_OUT_PARTS)
                copy_chunk(0, 5)
                q_hi(0, range(4))
                x_affine(1)
                load_table(ACT.Exp)
                for b in range(5, NB):
                    row_squares(b)
                select_heads(0)

                for b in range(NB):
                    for s in range(HEADS + LAG):
                        if s < HEADS and s % 2 == 0:
                            ev_T(b, s)
                        if s < HEADS and s % HG == HG - 1 and b + 1 < NB:
                            copy_chunk(b + 1, s // HG)
                        if b >= 1 and s == 1:
                            select_heads(b)
                        if b == 0 and s == 2:
                            split_hi(W_CORE_PARTS)
                        if b == 0 and s == LAG:
                            act.wait_ge(v_wsplit.sem, NPART)
                        if s >= LAG:
                            exp(b, s - LAG)
                        if s == HEADS + LAG - 1 and b + 1 < NB:
                            q_hi(b + 1, (0,))
                    for i in range(2):
                        act.wait_ge(e_oT, 2 * b + i + 1)
                        act.activation(o_f[:, i, :], b_t[i][:], ACT.Copy).then_inc(a_of, 1)
                    if b + 1 < NB:
                        q_hi(b + 1, (1, 2, 3))
                        copy_chunk(b + 1, 4)
                    load_table(ACT.Gelu)
                    for i in range(2):
                        act.wait_ge(v_y, 2 * b + i + 1)
                        act.activation(yT[0][:, i, :], y_f[:, i, :], ACT.Copy).then_inc(a_yhi, 1)
                    for i in range(2):
                        act.activation(gy_f[:, i, :], y_f[:, i, :], ACT.Gelu).then_inc(a_gy, 1)
                    for i in range(2):
                        act.wait_ge(a_gy, 2 * b + i + 1)
                        act.activation(gyT[0][:, i, :], gy_f[:, i, :], ACT.Copy).then_inc(a_gyhi, 1)
                    if b + 1 < NB:
                        copy_chunk(b + 1, 5)
                    for t in range(TB):
                        act.wait_ge(v_h, 2 * b + t + 1)
                        act.activation(gh_tok[:, t, :], gh_tok[:, t, :], ACT.Gelu).then_inc(a_gh, 1)
                    if b + 2 < NB:
                        x_affine(b + 2)
                    if b + 1 < NB:
                        load_table(ACT.Exp)
                    act.wait_ge(e_ghT, b + 1)
                    if b >= 1:
                        act.wait_ge(d_ght, 16 * b)
                    act.activation(ght, b_a[0][:], ACT.Copy).then_inc(a_ghT, 1)

            @block.vector
            def _(dve):
                def step(ins):
                    dve.wait_ge(v_step.sem, v_step.inc(ins))

                def rsqrt(dst, tmp, src, mean_over):
                    step(dve.tensor_scalar(src, src, 1.0 / mean_over, EPS, ALU.mult, ALU.add))
                    step(dve.tensor_single_scalar(tmp.bitcast(I32), src.bitcast(I32), 1, ALU.logical_shift_right))
                    step(dve.tensor_scalar(dst.bitcast(I32), tmp.bitcast(I32), -1, 0x5F3759DF, ALU.mult, ALU.add))
                    for _ in range(3):
                        step(dve.tensor_tensor(tmp, dst, dst, ALU.mult))
                        step(dve.scalar_tensor_tensor(out=tmp, in0=tmp, scalar=-0.5, in1=src, op0=ALU.mult, op1=ALU.mult))
                        step(dve.scalar_tensor_tensor(out=dst, in0=tmp, scalar=1.5, in1=dst, op0=ALU.add, op1=ALU.mult))

                def split_lo(n):
                    dve.wait_ge(a_wsplit.sem, n + 1)
                    _, (hi, lo), size = parts[n]
                    v_wsplit.inc(dve.tensor_tensor(lo, stage_of(n)[:, 0:size], hi.bitcast(F32), ALU.subtract))

                def scale_x(b):
                    for t in range(TB):
                        i = b * TB + t
                        dve.tensor_scalar(xs[:, t * D:(t + 1) * D], resid[:, i, :], rx[:, i:i + 1], None,
                                          ALU.mult).then_inc(v_xs, 1)

                def split_x(b):
                    dve.wait_ge(a_xaff, KC * (b + 1))
                    hi, lo = (w[:].rearrange("p c s -> p (c s)") for w in xt)
                    dve.tensor_copy(hi, xs[:]).then_inc(v_xT, 1)
                    dve.wait_ge(v_xT, 2 * b + 1)
                    dve.tensor_tensor(lo, xs[:], hi.bitcast(F32), ALU.subtract).then_inc(v_xT, 1)

                def sum_squares(b, n):
                    dve.wait_ge(p_sq, 4 * b + n + 1)
                    dve.tensor_reduce(ss[:, n, :], sq[:, n % 2, :].rearrange("p (h d) -> p h d", d=DH),
                                      AX.X, ALU.add).then_inc(v_ss, 1)

                def head_norms(b):
                    dve.wait_ge(v_ss, 4 * (b + 1))
                    flat = lambda t: t[:].rearrange("p n h -> p (n h)")
                    rsqrt(flat(rs), rs_b[:], flat(ss), DH)
                    dve.wait_ge(p_gq, 2 * (b + 1))

                def normalise(b, ns):
                    for n in ns:
                        q = qkraw[:, n, :].rearrange("p (h d) -> p h d", d=DH)
                        dve.tensor_tensor(q, q, rs[:, n, :].unsqueeze(2).to_broadcast([P, HEADS, DH]),
                                          ALU.mult).then_inc(v_qn, 1)

                def q_lo(b, ns):
                    for n in ns:
                        dve.wait_ge(a_qhi, 4 * b + n + 1)
                        dve.tensor_tensor(quarter(n, 1), times(n, 1), quarter(n, 0)[:, :, 0:1, :].bitcast(F32), ALU.subtract).then_inc(v_qlo, 1)

                def choose(b):
                    tiles = slice(b * TB, (b + 1) * TB)
                    dve.wait_ge(v_logits, b + 1)
                    for t in range(TB):
                        ins = dve.max(top8[:, t, :], logits[:, b * TB + t, :])
                        v_step.inc(ins)
                    dve.wait_ge(v_step.sem, v_step.count)
                    for t in range(TB):
                        v_step.inc(dve.max_index(idx8[:, t, :], top8[:, t, :], logits[:, b * TB + t, :]))
                    dve.wait_ge(v_step.sem, v_step.count)
                    step(dve.tensor_copy(idxf[:], idx8[:]))
                    if b >= 1:
                        step(dve.tensor_copy(chosen_sum[:, 0, :], chosen_sum[:, TB, :]))
                    for k in range(2):
                        v_step.inc(dve.tensor_tensor(onehot[:, k, tiles, :], iota_e[:, 0:E].unsqueeze(1).to_broadcast([P, TB, E]),
                                                     idxf[:, :, k:k + 1].to_broadcast([P, TB, E]), ALU.is_equal))
                    dve.wait_ge(v_step.sem, v_step.count)
                    step(dve.tensor_tensor(chosen[:], onehot[:, 0, tiles, :], onehot[:, 1, tiles, :], ALU.add))
                    for t in range(TB):
                        ins = dve.tensor_tensor(chosen_sum[:, t + 1, :], chosen_sum[:, t, :], chosen[:, t, :], ALU.add)
                        if t < TB - 1:
                            step(ins)
                    ins.then_inc(v_chosen, 1)

                def norm(b, g):
                    dve.wait_ge(e_PV, NG * b + g + 1)
                    pv = b_pv[:].rearrange("p (t n) -> p t n", t=TB)[:, :, 0:HG * VW].rearrange("p t (j w) -> p t j w", w=VW)
                    dve.reciprocal(rden[:], pv[:, :, :, DH]).then_inc(v_rden, 1)
                    dve.wait_ge(v_rden, NG * b + g + 1)
                    for t in range(TB):
                        o = o_tok[:, t, g * HG * DH:(g + 1) * HG * DH].rearrange("p (j d) -> p j d", d=DH)
                        dve.tensor_tensor(o, pv[:, t, :, 0:DH], rden[:, t, :].unsqueeze(2).to_broadcast([P, HG, DH]),
                                          ALU.mult).then_inc(v_norm, 1)

                def row_max(b, h):
                    dve.wait_ge(e_S, HEADS * b + h + 1)
                    dve.tensor_reduce(rowmax[:, (h // HG) % 2, :, h % HG], b_s[h % 2][:].rearrange("p (t k) -> p t k", t=TB),
                                      AX.X, ALU.max).then_inc(v_max, 1)

                dve.wait_ge(e_condT, 1)
                dve.tensor_copy(condT[:], b_s[0][:, 0:KC * NB].rearrange("p (c b) -> p c b", b=NB)).then_inc(v_condT, 1)
                dve.wait_ge(a_ssx, TB)
                rsqrt(rx[:, 0:TB], rs_b[:, 0:TB], ssx[:, 0:TB], D)
                scale_x(0)
                split_lo(0)
                split_lo(1)
                dve.wait_ge(d_small, 16 * SMALL)
                dve.wait_ge(e_ada, KC)
                step(dve.tensor_copy(rs_b[:], b_s[1][:, 0:64]))
                for c in range(1, KC):
                    step(dve.tensor_tensor(rs_b[:], rs_b[:], b_s[1][:, c * 64:(c + 1) * 64], ALU.add))
                ada = rs_b[:].rearrange("p (f b) -> p f b", b=NB)
                step(dve.tensor_tensor(aff_shift[:], ada[:, KC:, :], bemb_col[:, KC:].unsqueeze(2).to_broadcast([P, KC, NB]), ALU.add))
                step(dve.tensor_tensor(aff_scale[:], ada[:, 0:KC, :], bemb_col[:, 0:KC].unsqueeze(2).to_broadcast([P, KC, NB]), ALU.add))
                gn = gnorm_col[:].unsqueeze(2).to_broadcast([P, KC, NB])
                dve.scalar_tensor_tensor(out=aff_scale[:], in0=aff_scale[:], scalar=1.0, in1=gn,
                                         op0=ALU.add, op1=ALU.mult).then_inc(v_ada, 1)
                dve.scalar_tensor_tensor(out=gqk[:], in0=gqk[:], scalar=float(DH) ** -0.5, in1=gk_b[:],
                                         op0=ALU.mult, op1=ALU.mult).then_inc(v_ada, 1)
                for e, hid in enumerate(HID):
                    step(dve.tensor_scalar(router_bias[:, e:e + 1], router_bias[:, e:e + 1],
                                           -COST_LAMBDA * 2 * L * hid, None, ALU.add))
                dve.wait_ge(p_const, P_CONSTS)
                step(dve.tensor_copy(ident_r[:], ident[:]))
                step(dve.tensor_scalar(region0[:], iota_e[:, 0:E], float(REGION), None, ALU.mult))
                split_lo(2)
                split_x(0)
                split_lo(3)
                dve.wait_ge(a_ssx, 2 * TB)
                rsqrt(rx[:, TB:2 * TB], rs_b[:, 0:TB], ssx[:, TB:2 * TB], D)
                scale_x(1)
                sum_squares(0, 0)
                split_lo(W_QKV_PARTS)
                sum_squares(0, 1)
                sum_squares(0, 2)
                sum_squares(0, 3)
                head_norms(0)
                normalise(0, range(4))
                q_lo(0, range(4))
                split_x(1)
                split_lo(W_OUT_PARTS)
                dve.wait_ge(a_ssx, NT)
                rsqrt(rx[:, 2 * TB:NT], rs_b[:, 0:NT - 2 * TB], ssx[:, 2 * TB:NT], D)

                for b in range(NB):
                    for s in range(HEADS + LAG + 1):
                        if s < HEADS and s % 2 == 1:
                            dve.wait_ge(e_T, HEADS * b + s + 1)
                            dve.tensor_copy(stacks[0:QW, s % 8, :], b_t[1][0:QW, :]).then_inc(v_evT, 1)
                        if 1 <= s <= HEADS:
                            row_max(b, s - 1)
                        if s > HG and s % HG == 1 and s // HG <= NG:
                            g = s // HG - 1
                            dve.wait_ge(e_mT, NG * b + g + 1)
                            for i in range(g % 2 * HG, (g % 2 + 1) * HG, 2):
                                dve.tensor_scalar(stacks[QW:QW + HG, i:i + 2, 0:SEQ],
                                                  b_t[1][0:HG, 0:SEQ].unsqueeze(1).to_broadcast([HG, 2, SEQ]),
                                                  -1.0, None, ALU.mult).then_inc(v_mrow, 1)
                        if s >= LAG + HG and (s - LAG) % HG == 0:
                            norm(b, (s - LAG) // HG - 1)
                        if b + 1 < NB and s == HEADS + 2:
                            head_norms(b + 1)
                        if b + 1 < NB and s == HEADS + 3:
                            normalise(b + 1, (0, 1))
                        if b >= 1 and s == LAG + HG + 1:
                            choose(b - 1)
                        if b == 0 and s == 3:
                            split_lo(W_CORE_PARTS)
                        if s >= HG and s % HG == 0 and s <= HEADS and b + 1 < NB:
                            sum_squares(b + 1, s // HG - 1)
                    for i in range(2):
                        dve.wait_ge(a_of, 2 * b + i + 1)
                        dve.tensor_copy(oT[0][:, i, :], o_f[:, i, :]).then_inc(v_oT, 1)
                        dve.wait_ge(v_oT, 4 * b + 2 * i + 1)
                        dve.tensor_tensor(oT[1][:, i, :], o_f[:, i, :], oT[0][:, i, :].bitcast(F32), ALU.subtract).then_inc(v_oT, 1)
                    if b >= 1:
                        place(dve, b - 1, b_pv)
                    if b + 2 < NB:
                        scale_x(b + 2)
                    if b + 1 < NB:
                        normalise(b + 1, (2, 3))
                        q_lo(b + 1, range(4))
                    for i in range(2):
                        dve.wait_ge(e_yT, 2 * b + i + 1)
                        dve.tensor_tensor(y_f[:, i, :], b_s[i][:], o_f[:, i, :], ALU.add).then_inc(v_y, 1)
                    for i in range(2):
                        dve.wait_ge(a_yhi, 2 * b + i + 1)
                        dve.tensor_tensor(yT[1][:, i, :], y_f[:, i, :], yT[0][:, i, :].bitcast(F32), ALU.subtract).then_inc(v_ylo, 1)
                    for i in range(2):
                        dve.wait_ge(a_gyhi, 2 * b + i + 1)
                        dve.tensor_tensor(gyT[1][:, i, :], gy_f[:, i, :], gyT[0][:, i, :].bitcast(F32), ALU.subtract).then_inc(v_gylo, 1)
                    for t in range(TB):
                        dve.wait_ge(e_down, TB * (b + 1))
                        if b >= 1:
                            dve.wait_ge(d_slots, 64 * b)
                        else:
                            dve.wait_ge(d_yzero, 16)
                        dve.tensor_tensor(gh_tok[:, t, :], b_a[0][:, t * L:(t + 1) * L], down_bias[:], ALU.add).then_inc(v_h, 1)
                    dve.wait_ge(e_router, b + 1)
                    dve.tensor_tensor(logits[:, b * TB:(b + 1) * TB, :], b_pv[:, 0:TB * E].rearrange("p (t e) -> p t e", e=E),
                                      router_bias[:].unsqueeze(1).to_broadcast([P, TB, E]), ALU.add).then_inc(v_logits, 1)
                    if b == NB - 1:
                        choose(b)
                    if b + 2 < NB:
                        split_x(b + 2)
                    for t in range(TB):
                        dve.wait_ge(e_core, TB * b + t + 1)
                        dve.tensor_tensor(resid[:, b * TB + t, :], resid[:, b * TB + t, :], b_s[t][:], ALU.add).then_inc(v_core, 1)

            @block.tensor
            def _(pe):
                def three(out_ap, lhs, rhs, first, last):
                    pe.matmul(out_ap, lhs[0], rhs[0], start=first, stop=False)
                    pe.matmul(out_ap, lhs[0], rhs[1], start=False, stop=False)
                    return pe.matmul(out_ap, lhs[1], rhs[0], start=False, stop=last)

                def x_T(b):
                    pe.wait_ge(v_xs, TB * (b + 1))
                    if b >= 2:
                        pe.wait_ge(a_of, 2 * (b - 2) + 2)
                    for half in range(2):
                        if half == 1 and b >= 2:
                            pe.wait_ge(a_exp, HEADS * (b - 1))
                        for c in (2 * half, 2 * half + 1):
                            for t in range(TB):
                                mm = pe.transpose((b_t[1], b_a[1])[half][:, (c % 2) * SEQ + t * P:(c % 2) * SEQ + (t + 1) * P],
                                                  xs[:, t * D + c * P:t * D + (c + 1) * P], ident[:])
                        mm.then_inc(e_xT, 1)

                CHUNKS = [(0, 0), (0, 1), (1, 0), (1, 1), (0, 2), (1, 2)]

                def qkv(b, n, c):
                    t, part = CHUNKS[n]
                    if c == 0:
                        if n == 0:
                            pe.wait_ge(v_xT, 2 * (b + 1))
                        if b >= 1:
                            pe.wait_ge(a_mm, 6 * b + n)
                        elif n >= 2:
                            pe.wait_ge(a_mm, n - 1)
                    if b == 0 and n == 0:
                        pe.wait_ge(v_wsplit.sem, c + 1)
                    mm = three(chunk_bank(b, n)[:], [w[:, c, t * P:(t + 1) * P] for w in xt],
                               [w[:, c, part * D:(part + 1) * D] for w in w_qkv], c == 0, c == KC - 1)
                    if c == KC - 1:
                        mm.then_inc(e_qkv, 1)

                def stack_T(b, h):
                    if h == 0:
                        pe.wait_ge(v_qlo, 4 * (b + 1))
                        if b >= 1:
                            pe.wait_ge(a_of, 2 * b - 1)
                    if h == 1:
                        pe.wait_ge(a_xaff, KC * min(b + 2, NB))
                    if h >= 2:
                        if h % 2 == 0:
                            pe.wait_ge(a_evT, 8 * b + h // 2)
                        else:
                            pe.wait_ge(v_evT, 8 * b + h // 2)
                    if h >= 7 and h % HG == HG - 1:
                        pe.wait_ge(v_mrow, 2 * (NG * b + h // HG))
                    for half, src in ((0, q_tok), (1, k_tok)):
                        for t in range(TB):
                            o = (half * TB + t) * P
                            mm = pe.transpose(b_t[h % 2][0:QW, o:o + P].bitcast(F32R), src[:, t, h, :], ident_r[:])
                    mm.then_inc(e_T, 1)

                def scores(b, h):
                    if h % 2 == 0:
                        pe.wait_ge(a_evT, 8 * b + h // 2 + 1)
                    else:
                        pe.wait_ge(v_evT, 8 * b + h // 2 + 1)
                    if h >= 2:
                        pe.wait_ge(v_max, HEADS * b + h - 1)
                    elif b >= 1:
                        pe.wait_ge(v_core, TB * b)
                    st = stacks[0:QW, h % 8, :]
                    for t in range(TB):
                        mm = pe.matmul(b_s[h % 2][:, t * SEQ:(t + 1) * SEQ], st[:, t * P:(t + 1) * P], st[:, SEQ:2 * SEQ],
                                       start=True, stop=True)
                    mm.then_inc(e_S, 1)

                def max_T(b, g):
                    pe.wait_ge(v_max, HEADS * b + HG * (g + 1))
                    pe.wait_ge(v_evT, 8 * b + min(2 * g + 3, HEADS // 2))
                    for t in range(TB):
                        mm = pe.transpose(b_t[1][0:HG, t * P:(t + 1) * P], rowmax[:, g % 2, t, :], ident[:])
                    mm.then_inc(e_mT, 1)

                def scores_T(b, h):
                    g, j = h // HG, h % HG
                    if h == 0:
                        pe.wait_ge(a_sel, b + 1)
                    if j % 2 == 0:
                        pe.wait_ge(v_mrow, 2 * (NG * b + g) + j // 2 + 1)
                    if h >= 2:
                        pe.wait_ge(a_exp, HEADS * b + h - 1)
                    else:
                        if b >= 1:
                            pe.wait_ge(a_ghT, b)
                        pe.wait_ge(a_xaff, KC * min(b + 2, NB))
                    st = stacks[0:QW + HG, h % 8, :]
                    for k in range(TB):
                        mm = pe.matmul(b_a[h % 2][:, k * SEQ:(k + 1) * SEQ], st[:, SEQ + k * P:SEQ + (k + 1) * P], st[:, 0:SEQ],
                                       start=True, stop=True)
                    mm.then_inc(e_ST, 1)

                def values(b, h):
                    g, j = h // HG, h % HG
                    pe.wait_ge(a_exp, HEADS * b + h + 1)
                    if j == 0:
                        if g >= 1:
                            pe.wait_ge(v_norm, 2 * (NG * b + g))
                        else:
                            pe.wait_ge(a_mm, 6 * b + 6)
                            if b >= 1:
                                pe.wait_ge(v_logits, b)
                    for t in range(TB):
                        for k in range(TB):
                            o = t * L + j * VW
                            mm = pe.matmul(b_pv[:, o:o + PVW], att[:, h % 4, k * SEQ + t * P:k * SEQ + (t + 1) * P],
                                           v_rows[:, k, h * VW:h * VW + PVW], start=k == 0, stop=k == TB - 1)
                    if j == HG - 1:
                        mm.then_inc(e_PV, 1)

                def o_T(b):
                    pe.wait_ge(a_evT, 8 * (b + 1))
                    pe.wait_ge(v_mrow, 2 * NG * (b + 1))
                    for half in range(2):
                        pe.wait_ge(v_norm, NG * (2 * b + half + 1))
                        if half == 1 and b + 1 < NB:
                            qkv(b + 1, 4, 0)
                        for c in (2 * half, 2 * half + 1):
                            for t in range(TB):
                                mm = pe.transpose(b_t[half][:, (c % 2) * SEQ + t * P:(c % 2) * SEQ + (t + 1) * P],
                                                  o_tok[:, t, c * P:(c + 1) * P], ident[:])
                        mm.then_inc(e_oT, 1)

                def feat(w, c):
                    return w[:, c // 2, (c % 2) * SEQ:(c % 2 + 1) * SEQ]

                def y_T(b):
                    pe.wait_ge(v_oT, 4 * (b + 1))
                    if b == 0:
                        pe.wait_ge(v_wsplit.sem, W_OUT_PARTS)
                    for f in range(KC):
                        for c in range(KC):
                            mm = three(b_s[f // 2][:, (f % 2) * SEQ:(f % 2 + 1) * SEQ],
                                       [w[:, c, f * P:(f + 1) * P] for w in w_out], [feat(w, c) for w in oT],
                                       c == 0, c == KC - 1)
                        if f % 2 == 1:
                            mm.then_inc(e_yT, 1)

                def down_and_router(b):
                    pe.wait_ge(a_yhi, 2 * (b + 1))
                    pe.wait_ge(v_ylo, 2 * (b + 1))
                    if b == 0:
                        pe.wait_ge(v_wsplit.sem, W_DOWN_PARTS)
                    pe.wait_ge(a_exp, HEADS * (b + 1))
                    for t in range(TB):
                        for c in range(KC):
                            mm = three(b_a[0][:, t * L:(t + 1) * L], [feat(w, c)[:, t * P:(t + 1) * P] for w in yT],
                                       [w[:, c, :] for w in w_down], c == 0, c == KC - 1)
                        mm.then_inc(e_down, 1)
                    if b >= 1:
                        pe.wait_ge(v_slot, b)
                    for t in range(TB):
                        for c in range(KC):
                            mm = pe.matmul(b_pv[:, t * E:(t + 1) * E], feat(y_f, c)[:, t * P:(t + 1) * P], w_router[:, c, :],
                                           start=c == 0, stop=c == KC - 1)
                    mm.then_inc(e_router, 1)

                def core(b, t):
                    if t == 0:
                        pe.wait_ge(a_gyhi, 2 * (b + 1))
                        pe.wait_ge(v_gylo, 2 * (b + 1))
                    for c in range(KC):
                        mm = three(b_s[t][:], [feat(w, c)[:, t * P:(t + 1) * P] for w in gyT],
                                   [w[:, c, :] for w in w_core], c == 0, c == KC - 1)
                    mm.then_inc(e_core, 1)

                def gh_T(b):
                    pe.wait_ge(a_gh, TB * (b + 1))
                    for c in range(LC):
                        for t in range(TB):
                            mm = pe.transpose(b_a[0][:, c * SEQ + t * P:c * SEQ + (t + 1) * P], gh_tok[:, t, c * P:(c + 1) * P], ident[:])
                    mm.then_inc(e_ghT, 1)

                pe.wait_ge(d_cond, 16)
                pe.wait_ge(p_const, P_IDENT)
                for c in range(KC):
                    mm = pe.transpose(b_s[0][:, c * NB:(c + 1) * NB], cond_row[:, c * P:(c + 1) * P], ident[0:NB, 0:NB])
                mm.then_inc(e_condT, 1)
                pe.wait_ge(v_condT, 1)
                for c in range(KC):
                    pe.wait_ge(d_wemb[c % 2], 16 * (c // 2 + 1))
                    for f in range(2 * KC):
                        mm = pe.matmul(b_s[1][:, c * 64 + f * NB:c * 64 + (f + 1) * NB], emb_stage[c % 2][:, f * P:(f + 1) * P],
                                       condT[:, c, :], start=True, stop=True)
                    mm.then_inc(e_ada, 1)
                x_T(0)
                for n in range(6):
                    for c in range(KC):
                        qkv(0, n, c)
                x_T(1)
                for b in range(NB):
                    for s in range(HEADS + LAG + 1):
                        if s < HEADS:
                            stack_T(b, s)
                            if b + 1 < NB:
                                qkv(b + 1, s // HG, s % HG)
                        if s == HEADS + 1:
                            max_T(b, NG - 1)
                        if LAG <= s < HEADS + LAG:
                            scores_T(b, s - LAG)
                        if 1 <= s <= HEADS:
                            scores(b, s - 1)
                        if s > LAG:
                            values(b, s - LAG - 1)
                        if HG < s < HEADS and s % HG == 1:
                            max_T(b, s // HG - 1)
                    o_T(b)
                    if b >= 1:
                        ranks(pe, b - 1, b_pv)
                    if b + 1 < NB:
                        for c in range(1, KC):
                            qkv(b + 1, 4, c)
                    y_T(b)
                    if b + 1 < NB:
                        for c in range(KC):
                            qkv(b + 1, 5, c)
                    if b + 2 < NB:
                        x_T(b + 2)
                    down_and_router(b)
                    core(b, 0)
                    gh_T(b)
                    core(b, 1)

        with ExitStack() as ph:
            def sb(name, shape, dt=F32):
                return sbt(name, shape, dt, ph)

            def pair(name, shape):
                return sb(name + "_hi", shape, F32R), sb(name + "_lo", shape, F32R)

            KX = 2 * E + 1
            QB = 2
            acc = sb("acc", [P, NT, L])
            wst = [sb(f"wst{r}", [P, max(NBK[r::2]), 2, LC * BLK]) for r in range(2)]
            ring = pair("ring", [P, RING, 2, LC * BLK])
            SHARED_SLOT = RING - 1
            ghT_f = sb("ghT_f", [P, 2, QB * LC * SEQ])
            ghT = pair("ghT", [P, 2, QB * LC * SEQ])
            hid_f = sb("hid_f", [P, 2, HB, ST])
            hid = pair("hid", [P, 2, HB, ST])
            x_slots = gh_tok
            assert ST == TB * P
            xT = pair("x_T", [P, LC * ST])
            y_slots = sb("y_slots", [P, 2, L])
            b1_col = sb("b1_col", [P, NEB * HB])
            sb1_col = sb("sb1_col", [P, HB])
            bias_out = sb("bias_out", [P, 2, D])
            w_up = pair("w_up", [P, LC * D])
            count_i = sb("count_i", [P, E], I32)
            tiles_f = sb("tiles_f", [P, E])
            first_f = sb("first_f", [P, E + 1])
            row_f = sb("row_f", [P, 3, E])
            route_i = sb("route_i", [P, 3, E + 1], I32)
            y_rows = sb("y_rows", [P, 2, NT])
            y_idx = sb("y_idx", [P, 2, NT], U32)
            picked = sb("picked2", [P, 2, NT, E])
            ex = sb("ex", [P, NT, E])
            gate = sb("gate", [P, 2, NT])
            zz = sb("zz", [P, 4, NT])
            gx = sb("gx", [P, NT, KX])
            corr_rhs = sb("corr_rhs", [KX, L])
            table_of, told = sb("table_of", [1, 1]), sb("told", [1, 1])
            accT = pair("accT", [P, 2, LC * P])
            YR = 4
            y_got = ghT_f[:].rearrange("p q (r k l) -> p (q r) k l", r=YR // 2, k=2)
            gxT = wst[0][0:KX].rearrange("p k w n -> p (k w n)")[:, 0:NT * P]
            upst = wst[0][:, NBK[0]].rearrange("p w n -> p (w n)")
            assert LC * D == 2 * LC * BLK and NT * P <= NBK[2] * 2 * LC * BLK

            d_gh, d_misc, d_out = [sem("d_gh0"), sem("d_gh1")], sem("d_misc"), sem("d_out")
            d_b1, d_ws, d_we = sem("d_b1"), sem("d_ws"), [sem(f"d_we{n}") for n in range(4)]
            d_pad, d_xs, d_y, d_m = sem("d_pad"), sem("d_xs"), sem("d_y"), [sem("d_m0"), sem("d_m1")]
            d_got = [sem(f"d_got{r}") for r in range(YR)]
            pk, vk = Sem(sem("pk")), Sem(sem("vk"))
            v_tiles, v_rows, v_idx = sem("v_tiles"), sem("v_rows"), sem("v_idx")
            v_gate, a_gate, v_gates = sem("v_gate"), sem("a_gate"), sem("v_gates")
            a_whi, v_whi, p_wlo, v_slo = sem("a_whi"), sem("v_whi"), sem("p_wlo"), sem("v_slo")
            v_ghi, v_glo = sem("v_ghi"), sem("v_glo")
            e_h, a_gelu, v_hhi, v_hlo = sem("e_h"), sem("a_gelu"), sem("v_hhi"), sem("v_hlo")
            e_y, a_y, a_stored, a_table = sem("e_y"), sem("a_y"), sem("a_stored"), sem("a_table2")
            e_x, a_xhi, v_xlo = sem("e_x"), sem("a_xhi"), sem("v_xlo")
            a_uhi, v_ulo = sem("a_uhi"), sem("v_ulo")
            e_count, v_count = sem("e_count"), sem("v_count")
            e_gxT, v_gxT, e_corr, v_sum = sem("e_gxT"), sem("v_gxT"), sem("e_corr"), sem("v_sum")
            e_aT, a_ahi, v_alo, e_up, v_up = sem("e_aT"), sem("a_ahi"), sem("v_alo"), sem("e_up"), sem("v_up")

            h_bank = ((bank["mm"], bank["pv"]), (bank["t0"], bank["t1"]))
            y_bank = ((bank["s0"], bank["s1"]), (bank["a0"], bank["a1"]))
            x_bank = bank["a1"]
            rank_bank, count_bank = y_bank[1]

            H0, Y0, PER_TILE = NB * HB, NB * 2, MAXB * HB

            def event(T, k, hb):
                return T * PER_TILE + (H0 + k * HB + hb + 1)

            def step_of(nb, k, hb):
                return 1 + (MAXB - nb) * HB if (k, hb) == (nb - 1, HB - 1) else 1

            we_count = [16 * sum((n + 1) // 2 for n in NBK[e % 2 + (2 if e >= 2 else 0):e + 1:2]) for e in range(E)]

            def we_sem(e):
                return d_we[e] if e < 2 else d_we[2 + e % 2]

            MISC = 6

            def first_tiles(eng, first, upto):
                if not first:
                    eng.wait_ge(v_tiles, 1)
                    first.append(0)
                while len(first) <= upto:
                    e = len(first)
                    first.append(eng.value_load(route_i[0:1, 0, e:e + 1], min_val=e, max_val=MAXT))

            def rows(dram, first):
                return dram[bass.ds(first, ST), :].rearrange("(t p) d -> p t d", p=P)

            P_ZERO, P_CONST, P_RESID = 1, 3, 4
            def load_expert(eng, e):
                for k in range(0, NBK[e], 2):
                    m = min(2, NBK[e] - k)
                    eng.dma_start(wst[e % 2][:, k:k + m, :, :],
                                  a["e_w"][:, B0[e] + k:B0[e] + k + m, :, :]).then_inc(we_sem(e), 16)

            def image_rows(eng, start, row, n_tiles):
                for e, r in zip(range(start, E, 2), row):
                    if e == start:
                        eng.wait_ge(d_y, n_tiles * 16 + 16)
                    eng.dma_start(corr_rhs[e:e + 1, :], y_dram[bass.ds(r, 1), :]).then_inc(d_m[start], 16)

            block = ph.enter_context(nc.Block())

            @block.sync
            def _(sp):
                def load_gh(q):
                    if q >= 2:
                        sp.wait_ge(v_glo, q - 1)
                    sp.dma_start(ghT_f[:, q % 2, :].rearrange("p (b n) -> p b n", b=QB),
                                 ght_dram[:, q * QB:(q + 1) * QB, :]).then_inc(d_gh[q % 2], 16)

                load_gh(0)
                for w, name in ((0, "s_w1"), (1, "s_w2")):
                    sp.dma_start(wst[1][:, MAXB - 1, w, :].rearrange("p (c n) -> p c n", c=2),
                                 a[name].rearrange("(c p) n -> p c n", p=P)).then_inc(d_ws, 16)
                with nc.allow_non_contiguous_dma(reason="columns of biases"):
                    sp.dma_start(sb1_col[:], a["s_b1"].rearrange("(c p) -> p c", p=P)).then_inc(d_b1, 16)
                load_gh(1)
                load_expert(sp, 0)
                load_expert(sp, 1)
                with nc.allow_non_contiguous_dma(reason="columns of biases"):
                    sp.dma_start(b1_col[:], a["e_b1"].rearrange("(c p) -> p c", p=P)).then_inc(d_misc, 16)
                sp.dma_start(bias_out[:, 0, :], a["up_b"].partition_broadcast(P)).then_inc(d_misc, 16)
                sp.dma_start(bias_out[:, 1, :], a["core_b"].partition_broadcast(P)).then_inc(d_misc, 16)
                sp.dma_start(corr_rhs[E:2 * E, :], a["e_b2"]).then_inc(d_misc, 16)
                sp.dma_start(corr_rhs[2 * E:KX, :], a["s_b2"].unsqueeze(0)).then_inc(d_misc, 16)
                sp.dma_start(upst.rearrange("p (c n) -> p c n", c=LC),
                             a["up_w"].rearrange("(c p) n -> p c n", p=P)).then_inc(d_misc, 16)
                load_gh(2)
                load_gh(3)
                sp.wait_ge(d_slots, 16 * 2 * NT)
                sp.wait_ge(v_rows, 1)
                sp.wait_ge(pk.sem, P_ZERO)
                for e in range(E):
                    r = sp.value_load(route_i[0:1, 1, e:e + 1], min_val=e * REGION, max_val=(e + 1) * REGION - ST)
                    sp.dma_start(rows(slots_dram, r), y_slots[:]).then_inc(d_pad, 16)
                first = []
                first_tiles(sp, first, E)
                image_row = [sp.value_load(route_i[0:1, 2, e:e + 1], min_val=ST, max_val=(MAXT + 1) * ST - 1) for e in range(0, E, 2)]
                sp.wait_ge(d_pad, 16 * E)
                for e in range(E):
                    with sp.Fori(first[e], first[e + 1]) as T:
                        sp.wait_ge(e_x, T + 1)
                        sp.dma_start(x_slots[:], rows(slots_dram, nc.s_assert_within(
                            (T - first[e]) * ST + e * REGION, e * REGION, (e + 1) * REGION - ST,
                            skip_runtime_bounds_check_because="T is a tile of expert e, which has at most REGION // ST"))).then_inc(d_xs, 16)
                sp.wait_ge(e_x, first[E] + 1)
                sp.dma_start(x_slots[:], rows(slots_dram, 0)).then_inc(d_xs, 16)
                image_rows(sp, 0, image_row, first[E])
                for i in range(NT):
                    sp.wait_ge(v_up, i + 1)
                    sp.dma_start(out_dram[:, i, :], resid[:, i, :]).then_inc(d_out, 16)
                sp.wait_ge(d_out, 16 * NT)

            @block.gpsimd
            def _(pool):
                pk.inc(pool.memset(y_slots[:], 0.0))
                pk.inc(pool.memset(gx[:, :, E:2 * E], 1.0))
                pk.inc(pool.memset(gx[:, :, 2 * E:KX], SHARED_SCALE))

                def split_lo(n, src, slot):
                    for w, hi_ready in ((0, a_whi), (1, v_whi)):
                        pool.wait_ge(hi_ready, n + 1)
                        pool.tensor_tensor(ring[1][:, slot, w, :], src[:, w, :], ring[0][:, slot, w, :].bitcast(F32),
                                           ALU.subtract).then_inc(p_wlo, 1)

                def expert_lo(e):
                    for k in range(NBK[e]):
                        split_lo(1 + B0[e] + k, wst[e % 2][:, k], (B0[e] + k) % RING)

                scatter(pool, NB - 1)
                expert_lo(0)
                pool.wait_ge(v_ulo, 1)
                pool.wait_ge(p_wlo, 2 * B0[1])
                load_expert(pool, 2)
                expert_lo(1)
                pool.wait_ge(p_wlo, 2 * B0[2])
                load_expert(pool, 3)
                for e in range(2, E):
                    expert_lo(e)
                    if e + 2 < E:
                        pool.wait_ge(p_wlo, 2 * B0[e + 1])
                        load_expert(pool, e + 2)
                    if e == 4:
                        pool.wait_ge(d_misc, 16 * MISC)
                        pk.inc(pool.tensor_tensor(bias_out[:, 0, :], bias_out[:, 0, :], bias_out[:, 1, :], ALU.add))
                    if e >= 4:
                        pool.wait_ge(pk.sem, P_CONST + 1)
                        for i in range((e - 4) * NT // 4, (e - 3) * NT // 4):
                            pk.inc(pool.tensor_tensor(resid[:, i, :], resid[:, i, :], bias_out[:, 0, :], ALU.add))
                pool.wait_ge(v_idx, 1)
                pool.wait_ge(a_stored, 1)
                for i in range(NT):
                    if i >= YR:
                        pool.wait_ge(v_sum, i - YR + 1)
                    for k in range(2):
                        pool.indirect_dma_start(
                            out=y_got[:, i % YR, k, :], out_offset=None, in_=y_dram,
                            in_offset=bass.IndirectOffsetOnAxis(ap=y_idx[:, k, i:i + 1], axis=0),
                            bounds_check=(MAXT + 1) * ST - 1, oob_is_err=True).then_inc(d_got[i % YR], 16)

            @block.scalar
            def _(act):
                def split_w1(n, src, slot):
                    act.activation(ring[0][:, slot, 0, :], src[:, 0, :], ACT.Copy).then_inc(a_whi, 1)

                def expert_w1(e):
                    act.wait_ge(we_sem(e), we_count[e])
                    for k in range(NBK[e]):
                        split_w1(1 + B0[e] + k, wst[e % 2][:, k], (B0[e] + k) % RING)

                def gelu(bank_, k, hb, bias):
                    return act.activation(hid_f[:, k % 2, hb, :], bank_[:, 0:ST], ACT.Gelu, bias=bias)

                act.wait_ge(v_gate, 1)
                act.activation(ex[:], ex[:], ACT.Exp).then_inc(a_gate, 1)
                act.wait_ge(v_gate, 2)
                act.activation(zz[:, 2, :], zz[:, 2, :], ACT.Exp).then_inc(a_gate, 1)
                act.activation(table_of[:], ident[0:1, 0:1], ACT.Gelu).then_inc(a_table, 1)
                act.wait_ge(d_ws, 32)
                split_w1(0, wst[1][:, MAXB - 1], SHARED_SLOT)
                act.wait_ge(d_b1, 16)
                first = []
                for u in range(NB + 1):
                    if 2 <= u < NB:
                        first_tiles(act, first, (u - 1) * E // (NB - 2))
                    if u < NB:
                        for hb in range(HB):
                            act.wait_ge(e_h, u * HB + hb + 1)
                            gelu(h_bank[u % 2][hb], u, hb, sb1_col[:, hb:hb + 1]).then_inc(a_gelu, 1)
                    if u == 1:
                        expert_w1(0)
                    if u == 3:
                        expert_w1(1)
                    if u == 2:
                        act.wait_ge(d_misc, 16 * MISC)
                        act.activation(w_up[0][:], upst, ACT.Copy).then_inc(a_uhi, 1)
                    if u >= 1:
                        for tt in range(2):
                            act.wait_ge(e_y, (u - 1) * 2 + tt + 1)
                            act.activation(acc[:, (u - 1) * 2 + tt, :], y_bank[(u - 1) % 2][tt][:, 0:L], ACT.Copy,
                                           scale=SHARED_SCALE).then_inc(a_y, 1)
                act.wait_ge(pk.sem, P_ZERO)
                act.dma_start(rows(y_dram, 0), y_slots[:]).then_inc(d_y, 16)
                act.wait_ge(e_x, 2)
                act.activation(xT[0][:], x_bank[:], ACT.Copy).then_inc(a_xhi, 1)
                for e in range(E):
                    if 1 <= e < E - 1:
                        act.wait_ge(e_y, first[e - 1] * 2 + Y0)
                        expert_w1(e + 1)
                    nb = NBK[e]
                    with act.Fori(first[e], first[e + 1]) as T:
                        for k in range(nb):
                            for hb in range(HB):
                                act.wait_ge(e_h, event(T, k, hb))
                                g = (B0[e] + k) * HB + hb
                                gelu(h_bank[k % 2][hb], k, hb, b1_col[:, g:g + 1]).then_inc(a_gelu, step_of(nb, k, hb))
                        act.wait_ge(e_x, T + 3)
                        act.activation(xT[0][:], x_bank[:], ACT.Copy).then_inc(a_xhi, 1)
                        act.wait_ge(d_y, T * 16 + 16)
                        for tt in range(2):
                            act.wait_ge(e_y, T * 2 + (Y0 + tt + 1))
                            act.activation(y_slots[:, tt, :], y_bank[0][tt][:, 0:L], ACT.Copy).then_inc(a_y, 1)
                        act.wait_ge(a_y, T * 2 + (Y0 + 2))
                        act.dma_start(rows(y_dram, T * ST + ST), y_slots[:]).then_inc(d_y, 16)
                image_row = [act.value_load(route_i[0:1, 2, e:e + 1], min_val=ST, max_val=(MAXT + 1) * ST - 1) for e in range(1, E, 2)]
                act.wait_ge(d_y, first[E] * 16 + 16)
                act.activation(told[:], ident[0:1, 0:1], ACT.Copy).then_inc(a_stored, 1)
                image_rows(act, 1, image_row, first[E])
                for i in range(NT):
                    act.wait_ge(e_aT, i + 1)
                    if i >= 2:
                        act.wait_ge(e_up, i - 1)
                    act.activation(accT[0][:, i % 2, :], bank[("t0", "t1")[i % 2]][:, 0:LC * P], ACT.Copy).then_inc(a_ahi, 1)

            @block.vector
            def _(dve):
                def step(ins):
                    dve.wait_ge(vk.sem, vk.inc(ins))

                def split_gh(q):
                    dve.wait_ge(d_gh[q % 2], 16 * (q // 2 + 1))
                    if q >= 2:
                        dve.wait_ge(e_h, (q - 1) * QB * HB)
                    dve.tensor_copy(ghT[0][:, q % 2, :], ghT_f[:, q % 2, :]).then_inc(v_ghi, 1)
                    dve.wait_ge(v_ghi, q + 1)
                    dve.tensor_tensor(ghT[1][:, q % 2, :], ghT_f[:, q % 2, :], ghT[0][:, q % 2, :].bitcast(F32),
                                      ALU.subtract).then_inc(v_glo, 1)

                def expert_w2(e):
                    dve.wait_ge(we_sem(e), we_count[e])
                    for k in range(NBK[e]):
                        dve.tensor_copy(ring[0][:, (B0[e] + k) % RING, 1, :], wst[e % 2][:, k, 1, :]).then_inc(v_whi, 1)

                def split_hid(k, hb, done, by):
                    dve.wait_ge(a_gelu, done)
                    dve.tensor_copy(hid[0][:, k % 2, hb, :], hid_f[:, k % 2, hb, :]).then_inc(v_hhi, by)
                    dve.wait_ge(v_hhi, done)
                    dve.tensor_tensor(hid[1][:, k % 2, hb, :], hid_f[:, k % 2, hb, :], hid[0][:, k % 2, hb, :].bitcast(F32),
                                      ALU.subtract).then_inc(v_hlo, by)

                def logits_down():
                    step(dve.tensor_reduce(zz[:, 0, :], logits[:], AX.X, ALU.max))
                    dve.tensor_tensor(ex[:], logits[:], zz[:, 0, :].unsqueeze(2).to_broadcast([P, NT, E]),
                                      ALU.subtract).then_inc(v_gate, 1)

                def probabilities():
                    dve.wait_ge(a_gate, 1)
                    step(dve.tensor_reduce(zz[:, 0, :], ex[:], AX.X, ALU.add))
                    step(dve.reciprocal(zz[:, 1, :], zz[:, 0, :]))
                    step(dve.tensor_tensor(picked[:, 1], onehot[:, 1], ex[:], ALU.mult))
                    step(dve.tensor_reduce(zz[:, 2, :], picked[:, 1], AX.X, ALU.add))
                    step(dve.tensor_tensor(zz[:, 2, :], zz[:, 2, :], zz[:, 1, :], ALU.mult))
                    dve.tensor_tensor(zz[:, 2, :], zz[:, 2, :], zz[:, 1, :], ALU.subtract).then_inc(v_gate, 1)

                def gates():
                    dve.wait_ge(a_gate, 2)
                    step(dve.tensor_scalar(zz[:, 3, :], zz[:, 2, :], 1.0, None, ALU.add))
                    step(dve.reciprocal(gate[:, 0, :], zz[:, 3, :]))
                    step(dve.tensor_tensor(gate[:, 1, :], gate[:, 0, :], zz[:, 2, :], ALU.mult))
                    for k in range(2):
                        step(dve.tensor_tensor(picked[:, k], onehot[:, k], gate[:, k, :].unsqueeze(2).to_broadcast([P, NT, E]), ALU.mult))
                    step(dve.tensor_tensor(picked[:, 0], picked[:, 0], picked[:, 1], ALU.add))
                    dve.wait_ge(pk.sem, P_CONST)
                    dve.tensor_scalar(gx[:, :, 0:E], picked[:, 0], -1.0, 1.0, ALU.mult, ALU.add).then_inc(v_gates, 1)

                logits_down()
                place(dve, NB - 1, rank_bank)
                probabilities()
                dve.wait_ge(e_count, 1)
                dve.tensor_copy(counts[:], count_bank[:, 0:E]).then_inc(v_count, 1)
                dve.wait_ge(v_count, 1)
                gates()
                dve.wait_ge(d_ws, 32)
                dve.tensor_copy(ring[0][:, SHARED_SLOT, 1, :], wst[1][:, MAXB - 1, 1, :]).then_inc(v_whi, 1)
                for w, hi_ready in ((0, a_whi), (1, v_whi)):
                    dve.wait_ge(hi_ready, 1)
                    dve.tensor_tensor(ring[1][:, SHARED_SLOT, w, :], wst[1][:, MAXB - 1, w, :],
                                      ring[0][:, SHARED_SLOT, w, :].bitcast(F32), ALU.subtract).then_inc(v_slo, 1)
                split_gh(0)
                split_gh(1)

                def tiles():
                    step(dve.tensor_copy(count_i[:], counts[:]))
                    step(dve.tensor_single_scalar(count_i[:], count_i[:], ST.bit_length() - 1, ALU.logical_shift_right))
                    step(dve.tensor_copy(tiles_f[:], count_i[:]))
                    step(dve.tensor_scalar(first_f[:, 0:1], counts[:, 0:1], 0.0, None, ALU.mult))
                    for e in range(E):
                        step(dve.scalar_tensor_tensor(out=first_f[:, e + 1:e + 2], in0=tiles_f[:, e:e + 1], scalar=1.0,
                                                      in1=first_f[:, e:e + 1], op0=ALU.add, op1=ALU.add))
                    dve.tensor_copy(route_i[:, 0, :], first_f[:]).then_inc(v_tiles, 1)
                    step(dve.tensor_tensor(row_f[:, 0, :], region0[:], counts[:], ALU.add))
                    step(dve.tensor_scalar(row_f[:, 2, :], first_f[:, 0:E], 1.0, float(ST), ALU.add, ALU.mult))
                    step(dve.tensor_tensor(row_f[:, 1, :], row_f[:, 2, :], counts[:], ALU.add))
                    dve.tensor_copy(route_i[:, 1:3, 0:E], row_f[:, 0:2, :]).then_inc(v_rows, 1)

                def route():
                    step(dve.tensor_tensor(row_f[:, 2, :], row_f[:, 2, :], region0[:], ALU.subtract))
                    for k in range(2):
                        step(dve.tensor_tensor(picked[:, k], onehot[:, k], row_f[:, 2, :].unsqueeze(1).to_broadcast([P, NT, E]), ALU.mult))
                    step(dve.tensor_reduce(y_rows[:], picked[:], AX.X, ALU.add))
                    step(dve.tensor_tensor(y_rows[:], y_rows[:], slotf[:], ALU.add))
                    dve.tensor_copy(y_idx[:], y_rows[:]).then_inc(v_idx, 1)

                first = []
                for u in range(NB):
                    if 2 <= u:
                        first_tiles(dve, first, (u - 1) * E // (NB - 2))
                    for hb in range(HB):
                        split_hid(u, hb, u * HB + hb + 1, 1)
                    if u == 0:
                        tiles()
                        expert_w2(0)
                    if u == 3:
                        expert_w2(1)
                    if u in (1, 3):
                        split_gh(u // 2 + 2)
                    if u == 4:
                        route()
                    if u == 2:
                        dve.wait_ge(a_uhi, 1)
                        dve.tensor_tensor(w_up[1][:], upst, w_up[0][:].bitcast(F32), ALU.subtract).then_inc(v_ulo, 1)

                dve.wait_ge(a_xhi, 1)
                dve.tensor_tensor(xT[1][:], x_bank[:], xT[0][:].bitcast(F32), ALU.subtract).then_inc(v_xlo, 1)
                for e in range(E):
                    if 1 <= e < E - 1:
                        dve.wait_ge(e_y, first[e - 1] * 2 + Y0)
                        expert_w2(e + 1)
                    nb = NBK[e]
                    with dve.Fori(first[e], first[e + 1]) as T:
                        for k in range(nb):
                            for hb in range(HB):
                                split_hid(k, hb, event(T, k, hb), step_of(nb, k, hb))
                        dve.wait_ge(a_xhi, T + 2)
                        dve.tensor_tensor(xT[1][:], x_bank[:], xT[0][:].bitcast(F32), ALU.subtract).then_inc(v_xlo, 1)
                dve.wait_ge(p_wlo, 2 * NEB)
                for q in range(NT // 4):
                    dve.wait_ge(e_gxT, q + 1)
                    dve.tensor_copy(gxT[:, q * 4 * P:(q + 1) * 4 * P], h_bank[q // 2][q % 2][0:KX, :]).then_inc(v_gxT, 1)
                for i in range(NT + 2):
                    if i < NT:
                        dve.wait_ge(d_got[i % YR], 32 * (i // YR + 1))
                        for k in range(2):
                            step(dve.scalar_tensor_tensor(out=acc[:, i, :], in0=y_got[:, i % YR, k, :], scalar=gate[:, k, i:i + 1],
                                                          in1=acc[:, i, :], op0=ALU.mult, op1=ALU.add))
                        dve.wait_ge(e_corr, i + 1)
                        dve.tensor_tensor(acc[:, i, :], acc[:, i, :], h_bank[0][i % 2][:, 0:L], ALU.add).then_inc(v_sum, 1)
                    if 1 <= i <= NT:
                        w = i - 1
                        dve.wait_ge(a_ahi, w + 1)
                        dve.tensor_tensor(accT[1][:, w % 2, :], bank[("t0", "t1")[w % 2]][:, 0:LC * P], accT[0][:, w % 2, :].bitcast(F32),
                                          ALU.subtract).then_inc(v_alo, 1)
                    if i >= 2:
                        w = i - 2
                        dve.wait_ge(e_up, w + 1)
                        if w == 0:
                            dve.wait_ge(pk.sem, P_RESID + NT)
                        dve.tensor_tensor(resid[:, w, :], resid[:, w, :], y_bank[0][w % 2][:], ALU.add).then_inc(v_up, 1)

            @block.tensor
            def _(pe):
                def terms(lhs, rhs):
                    return ((lhs[0], rhs[0]), (lhs[0], rhs[1]), (lhs[1], rhs[0]))

                def hidden(out_bank, slot, hb, x_by_feature):
                    k_terms = []
                    for c in range(LC):
                        o = c * BLK + hb * P
                        k_terms += terms([w[:, slot, 0, o:o + P] for w in ring], x_by_feature(c))
                    for i, (l, r) in enumerate(k_terms):
                        mm = pe.matmul(out_bank[:, 0:ST], l, r, start=i == 0, stop=i == len(k_terms) - 1)
                    return mm

                def output(banks, slot, parity, hb, first_of_tile, last_of_tile):
                    for tt in range(2):
                        lhs = [w[:, parity, hb, tt * P:(tt + 1) * P] for w in hid]
                        for i, (l, r) in enumerate(terms(lhs, [w[:, slot, 1, hb * L:(hb + 1) * L] for w in ring])):
                            mm = pe.matmul(banks[tt][:, 0:L], l, r, start=first_of_tile and i == 0, stop=last_of_tile and i == 2)
                        if last_of_tile:
                            mm.then_inc(e_y, 1)

                def shared_hidden(u):
                    q = u // QB
                    if u % QB == 0:
                        pe.wait_ge(v_glo, q + 1)
                    if u == 0:
                        pe.wait_ge(v_slo, 2)
                        pe.sem_inc(e_x, 1)
                    for hb in range(HB):
                        hidden(h_bank[u % 2][hb], SHARED_SLOT, hb,
                               lambda c: [w[:, q % 2, (u % QB) * LC * SEQ + c * SEQ:(u % QB) * LC * SEQ + (c + 1) * SEQ]
                                          for w in ghT]).then_inc(e_h, 1)

                def x_T(ready):
                    pe.wait_ge(d_xs, ready)
                    for c in range(LC):
                        for t in range(2):
                            mm = pe.transpose(x_bank[:, c * ST + t * P:c * ST + (t + 1) * P], x_slots[:, t, c * P:(c + 1) * P], ident[:])
                    mm.then_inc(e_x, 1)

                ranks(pe, NB - 1, rank_bank)
                pe.matmul(count_bank[:, 0:E], ones[:], chosen_sum[:, TB, :], start=True, stop=True).then_inc(e_count, 1)
                shared_hidden(0)
                first = []
                for u in range(NB):
                    if 2 <= u:
                        first_tiles(pe, first, (u - 1) * E // (NB - 2))
                    if u + 1 < NB:
                        shared_hidden(u + 1)
                    if u >= 2:
                        pe.wait_ge(a_y, 2 * (u - 1))
                    elif u == 1:
                        pe.wait_ge(v_count, 1)
                    for hb in range(HB):
                        pe.wait_ge(v_hlo, u * HB + hb + 1)
                        output(y_bank[u % 2], SHARED_SLOT, u % 2, hb, hb == 0, hb == HB - 1)

                pe.wait_ge(a_y, Y0)
                x_T(16)
                for e in range(E):
                    nb = NBK[e]
                    pe.wait_ge(p_wlo, 2 * B0[e + 1])
                    slots = [(B0[e] + k) % RING for k in range(nb)]

                    def expert_hidden(T, k):
                        for hb in range(HB):
                            hidden(h_bank[k % 2][hb], slots[k], hb,
                                   lambda c: [w[:, c * ST:(c + 1) * ST] for w in xT]).then_inc(e_h, step_of(nb, k, hb))

                    with pe.Fori(first[e], first[e + 1]) as T:
                        pe.wait_ge(v_xlo, T + 1)
                        expert_hidden(T, 0)
                        for k in range(nb):
                            if k + 1 < nb:
                                expert_hidden(T, k + 1)
                            else:
                                x_T(T * 16 + 32)
                            if k == 0:
                                pe.wait_ge(a_y, T * 2 + Y0)
                            for hb in range(HB):
                                pe.wait_ge(v_hlo, event(T, k, hb))
                                output(y_bank[0], slots[k], k % 2, hb, (k, hb) == (0, 0), (k, hb) == (nb - 1, HB - 1))

                pe.wait_ge(v_gates, 1)
                for q in range(NT // 4):
                    for t in range(4):
                        mm = pe.transpose(h_bank[q // 2][q % 2][0:KX, t * P:(t + 1) * P], gx[:, 4 * q + t, :], ident[:])
                    mm.then_inc(e_gxT, 1)

                def corr(i):
                    if i >= 2:
                        pe.wait_ge(v_sum, i - 1)
                    pe.matmul(h_bank[0][i % 2][:, 0:L], gxT[:, i * P:(i + 1) * P], corr_rhs[:], start=True, stop=True).then_inc(e_corr, 1)

                pe.wait_ge(v_gxT, NT // 4)
                for part in d_m:
                    pe.wait_ge(part, 8 * E)
                corr(0)
                corr(1)
                for i in range(NT + 1):
                    if i < NT:
                        pe.wait_ge(v_sum, i + 1)
                        if i >= 2:
                            pe.wait_ge(v_alo, i - 1)
                        for c in range(LC):
                            mm = pe.transpose(bank[("t0", "t1")[i % 2]][:, c * P:(c + 1) * P], acc[:, i, c * P:(c + 1) * P], ident[:])
                        mm.then_inc(e_aT, 1)
                        if i + 2 < NT:
                            corr(i + 2)
                    if i >= 1:
                        w = i - 1
                        pe.wait_ge(v_alo, w + 1)
                        if w == 0:
                            pe.wait_ge(v_ulo, 1)
                            pe.wait_ge(a_y, first[E] * 2 + Y0)
                        if w >= 2:
                            pe.wait_ge(v_up, w - 1)
                        k_terms = []
                        for c in range(LC):
                            k_terms += terms([t[:, w % 2, c * P:(c + 1) * P] for t in accT], [t[:, c * D:(c + 1) * D] for t in w_up])
                        for k, (l, r) in enumerate(k_terms):
                            mm = pe.matmul(y_bank[0][w % 2][:], l, r, start=k == 0, stop=k == len(k_terms) - 1)
                        mm.then_inc(e_up, 1)



def kernel(**inputs):
    import numpy as np
    import concourse.bacc as bacc
    from concourse.bass_utils import run_bass_kernel_spmd

    c = {k.removeprefix("L0_"): np.ascontiguousarray(v) for k, v in inputs.items()}
    E = len(HID)
    arrays = {
        "x": c["x"], "cond": c["cond_2048"], "w_emb": c["cond_W_emb"], "b_emb": c["cond_b_emb"],
        "g_norm": c["cond_g_norm"], "w_qkv": c["cond_W_qkv"], "g_q": c["cond_g_q"], "g_k": c["cond_g_k"],
        "w_out": c["cond_W_out"], "down_w": c["ffn_down_w"], "down_b": c["ffn_down_b"], "up_w": c["ffn_up_w"],
        "up_b": c["ffn_up_b"], "router_w": c["ffn_router_w"], "router_b": c["ffn_router_b"],
        "core_w": c["ffn_core_w"], "core_b": c["ffn_core_b"],
        "e_w": np.ascontiguousarray(np.stack([
            np.concatenate([c[f"ffn_e{e}_w1"] for e in range(E)], axis=1).reshape(2, P, -1, 256).transpose(1, 2, 0, 3),
            np.concatenate([c[f"ffn_e{e}_w2"] for e in range(E)], axis=0).reshape(-1, 2, P, 256).transpose(2, 0, 1, 3),
        ], axis=2).reshape(P, -1, 2, 512)),
        "e_b1": np.concatenate([c[f"ffn_e{e}_b1"] for e in range(E)]),
        "e_b2": np.stack([c[f"ffn_e{e}_b2"] for e in range(E)]),
        "s_w1": c["ffn_shared_w1"], "s_b1": c["ffn_shared_b1"], "s_w2": c["ffn_shared_w2"], "s_b2": c["ffn_shared_b2"],
    }
    nc = bacc.Bacc("TRN2", target_bir_lowering=False, num_devices=1, dynamic_dma_scratch_size=4096)
    aps = {n: nc.dram_tensor(f"in_{n}", v.shape, mybir.dt.from_np(v.dtype), kind="ExternalInput").ap()
           for n, v in arrays.items()}
    out = nc.dram_tensor("out_0", c["x"].shape, F32, kind="ExternalOutput").ap()
    adaln_moe_program(nc, aps, out)
    r = run_bass_kernel_spmd(nc, [{f"in_{n}": v for n, v in arrays.items()}], core_ids=[0])
    return r.results[0]["out_0"]
```
